# Optimizing a Trainium2 kernel written in Bass

```python
import numpy as np
import jax
import jax.numpy as jnp

def _softmax(x, axis=-1):
    return jax.nn.softmax(x, axis=axis)

def _gelu(x):
    return jax.nn.gelu(x, approximate=True)

def _silu(x):
    return jax.nn.silu(x)

def _sigmoid(x):
    return jax.nn.sigmoid(x)

def _layernorm(x, axis=-1, eps=1e-05):
    m = jnp.mean(x, axis=axis, keepdims=True)
    v = jnp.var(x, axis=axis, keepdims=True)
    return (x - m) / jnp.sqrt(v + eps)

def _scatter_add(tgt, idx, src, axis=0):
    return tgt.at[idx].add(src)

def _segment_sum(src, seg, n):
    return jax.ops.segment_sum(src, seg, n)
kernel_name = 'mk_prb_d1_jaxref_r4_431418'

def setup_inputs(seed: int=0):
    np.random.seed(seed)
    _w = jnp.asarray

    def _L0_attn_setup():
        import jax, jax.numpy as jnp
        import numpy as np
        D_MODEL = 512
        N_HEADS = 16
        HEAD_DIM = D_MODEL // N_HEADS
        SCALE_BASE = 128

        def rotate_half(x):
            x1, x2 = jnp.split(x, 2, axis=-1)
            return jnp.concatenate((-x2, x1), axis=-1)

        def rotary_xpos(seq_len, dim, dtype=jnp.float32):
            inv_freq = 1.0 / 10000.0 ** (jnp.arange(0, dim, 2, dtype=jnp.float32) / dim)
            t = jnp.arange(seq_len, dtype=jnp.float32)
            freqs = jnp.einsum('i,j->ij', t, inv_freq)
            freqs = jnp.concatenate((freqs, freqs), axis=-1)
            scale_base = (jnp.arange(0, dim, 2, dtype=jnp.float32) + 0.4 * dim) / (1.4 * dim)
            power = (t - seq_len // 2) / SCALE_BASE
            scale = scale_base[None, :] ** power[:, None]
            scale = jnp.concatenate((scale, scale), axis=-1)
            return (freqs.astype(dtype), scale.astype(dtype))

        def apply_rotary(t, pos, scale):
            return t * jnp.cos(pos) * scale + rotate_half(t) * jnp.sin(pos) * scale
        key = jax.random.key(seed)
        ks = jax.random.split(key, 5)
        B, S = (2, 512)
        hidden_states = jax.random.normal(ks[0], (B, S, D_MODEL), dtype=jnp.float32)
        w_q = jax.random.normal(ks[1], (N_HEADS * HEAD_DIM, D_MODEL), dtype=jnp.float32) * 0.02
        w_kv = jax.random.normal(ks[2], (2 * HEAD_DIM, D_MODEL), dtype=jnp.float32) * 0.02
        w_proj = jax.random.normal(ks[3], (D_MODEL, N_HEADS * HEAD_DIM), dtype=jnp.float32) * 0.02
        b_proj = jax.random.normal(ks[4], (D_MODEL,), dtype=jnp.float32) * 0.02
        return {'hidden_states': hidden_states, 'w_q': w_q, 'w_kv': w_kv, 'w_proj': w_proj, 'b_proj': b_proj}
    _L0_attn_in = _L0_attn_setup()

    def _L0_ffn_setup():
        import jax, jax.numpy as jnp
        import numpy as np
        H, LAT, INTER, E, G, TOPK_G, TOP_K = (512, 256, 256, 32, 4, 2, 8)
        SHARED_INTER = 1024
        ROUTED_SCALE = 2.5
        B, S = (2, 256)

        def relu2(x):
            return jnp.square(jax.nn.relu(x))
        key = jax.random.key(seed)
        ks = jax.random.split(key, 9)
        w = 0.02
        return {'hidden_states': jax.random.normal(ks[0], (B, S, H), jnp.float32), 'gate_w': jax.random.normal(ks[1], (E, H), jnp.float32) * w, 'gate_bias': jax.random.normal(ks[2], (E,), jnp.float32) * w, 'fc1_w': jax.random.normal(ks[3], (LAT, H), jnp.float32) * w, 'fc2_w': jax.random.normal(ks[4], (H, LAT), jnp.float32) * w, 'w1': jax.random.normal(ks[5], (E, INTER, LAT), jnp.float32) * w, 'w2': jax.random.normal(ks[6], (E, LAT, INTER), jnp.float32) * w, 'shared_up_w': jax.random.normal(ks[7], (SHARED_INTER, H), jnp.float32) * w, 'shared_down_w': jax.random.normal(ks[8], (H, SHARED_INTER), jnp.float32) * w}
    _L0_ffn_in = _L0_ffn_setup()
    _d = {'L0_attn_hidden_states': _L0_attn_in['hidden_states'], 'L0_attn_w_q': _L0_attn_in['w_q'], 'L0_attn_w_kv': _L0_attn_in['w_kv'], 'L0_attn_w_proj': _L0_attn_in['w_proj'], 'L0_attn_b_proj': _L0_attn_in['b_proj'], 'L0_ffn_gate_w': _L0_ffn_in['gate_w'], 'L0_ffn_gate_bias': _L0_ffn_in['gate_bias'], 'L0_ffn_fc1_w': _L0_ffn_in['fc1_w'], 'L0_ffn_fc2_w': _L0_ffn_in['fc2_w'], 'L0_ffn_w1': _L0_ffn_in['w1'], 'L0_ffn_w2': _L0_ffn_in['w2'], 'L0_ffn_shared_up_w': _L0_ffn_in['shared_up_w'], 'L0_ffn_shared_down_w': _L0_ffn_in['shared_down_w']}
    _x0 = _d['L0_attn_hidden_states']
    _d['L0_attn_hidden_states'] = jax.random.normal(jax.random.fold_in(jax.random.key(seed), 1), (8, 512, 512), dtype=_x0.dtype)
    del _x0
    return _d

def reference(L0_attn_hidden_states, L0_attn_w_q, L0_attn_w_kv, L0_attn_w_proj, L0_attn_b_proj, L0_ffn_gate_w, L0_ffn_gate_bias, L0_ffn_fc1_w, L0_ffn_fc2_w, L0_ffn_w1, L0_ffn_w2, L0_ffn_shared_up_w, L0_ffn_shared_down_w):

    def _L0_attn_ref(hidden_states, w_q, w_kv, w_proj, b_proj):
        import jax, jax.numpy as jnp
        import numpy as np
        D_MODEL = 512
        N_HEADS = 16
        HEAD_DIM = D_MODEL // N_HEADS
        SCALE_BASE = 128

        def rotate_half(x):
            x1, x2 = jnp.split(x, 2, axis=-1)
            return jnp.concatenate((-x2, x1), axis=-1)

        def rotary_xpos(seq_len, dim, dtype=jnp.float32):
            inv_freq = 1.0 / 10000.0 ** (jnp.arange(0, dim, 2, dtype=jnp.float32) / dim)
            t = jnp.arange(seq_len, dtype=jnp.float32)
            freqs = jnp.einsum('i,j->ij', t, inv_freq)
            freqs = jnp.concatenate((freqs, freqs), axis=-1)
            scale_base = (jnp.arange(0, dim, 2, dtype=jnp.float32) + 0.4 * dim) / (1.4 * dim)
            power = (t - seq_len // 2) / SCALE_BASE
            scale = scale_base[None, :] ** power[:, None]
            scale = jnp.concatenate((scale, scale), axis=-1)
            return (freqs.astype(dtype), scale.astype(dtype))

        def apply_rotary(t, pos, scale):
            return t * jnp.cos(pos) * scale + rotate_half(t) * jnp.sin(pos) * scale
        B, S, _ = hidden_states.shape
        q = hidden_states @ w_q.T
        kv = hidden_states @ w_kv.T
        k, v = jnp.split(kv, 2, axis=-1)
        q = q.reshape(B, S, N_HEADS, HEAD_DIM).transpose(0, 2, 1, 3)
        scale_w = HEAD_DIM ** (-0.5)
        q = q * scale_w
        k = k * scale_w
        pos, xscale = rotary_xpos(S, HEAD_DIM, q.dtype)
        q = apply_rotary(q, pos, xscale)
        k = apply_rotary(k, pos, 1.0 / xscale)
        attn = jnp.einsum('bnih,bjh->bnij', q, k)
        causal = jnp.triu(jnp.ones((S, S), dtype=bool), 1)
        attn = jnp.where(causal, -jnp.finfo(attn.dtype).max, attn)
        attn = jax.nn.softmax(attn, axis=-1)
        out = jnp.einsum('bnij,bjd->bind', attn, v)
        out = out.reshape(B, S, N_HEADS * HEAD_DIM)
        out = out @ w_proj.T + b_proj
        return out

    def _L0_ffn_ref(hidden_states, gate_w, gate_bias, fc1_w, fc2_w, w1, w2, shared_up_w, shared_down_w):
        import jax, jax.numpy as jnp
        import numpy as np
        H, LAT, INTER, E, G, TOPK_G, TOP_K = (512, 256, 256, 32, 4, 2, 8)
        SHARED_INTER = 1024
        ROUTED_SCALE = 2.5
        B, S = (2, 256)

        def relu2(x):
            return jnp.square(jax.nn.relu(x))
        orig_shape = hidden_states.shape
        x = hidden_states.reshape(-1, H)
        T = x.shape[0]
        logits = jnp.einsum('th,eh->te', x.astype(jnp.float32), gate_w)
        scores = jax.nn.sigmoid(logits)
        sb = scores + gate_bias
        grp = sb.reshape(T, G, E // G)
        group_scores = jax.lax.top_k(grp, 2)[0].sum(-1)
        _, gidx = jax.lax.top_k(group_scores, TOPK_G)
        gmask = jax.nn.one_hot(gidx, G, dtype=sb.dtype).sum(1)
        masked = jnp.where(gmask[:, :, None] > 0, grp, -jnp.inf).reshape(T, E)
        _, topi = jax.lax.top_k(masked, TOP_K)
        wsel = jnp.take_along_axis(scores, topi, axis=1)
        wsel = wsel / wsel.sum(-1, keepdims=True) * ROUTED_SCALE
        cw = jnp.zeros((T, E), jnp.float32).at[jnp.arange(T)[:, None], topi].add(wsel)
        x_lat = x @ fc1_w.T
        h = relu2(jnp.einsum('tl,eil->eti', x_lat, w1))
        h = h * cw.T[:, :, None]
        y_lat = jnp.einsum('eti,eli->tl', h, w2)
        routed = y_lat @ fc2_w.T
        shared = relu2(x @ shared_up_w.T) @ shared_down_w.T
        return (shared + routed).reshape(orig_shape)
    x = L0_attn_hidden_states
    xn = _layernorm(x, axis=-1)
    x = x + _L0_attn_ref(xn, L0_attn_w_q, L0_attn_w_kv, L0_attn_w_proj, L0_attn_b_proj) + _L0_ffn_ref(xn, L0_ffn_gate_w, L0_ffn_gate_bias, L0_ffn_fc1_w, L0_ffn_fc2_w, L0_ffn_w1, L0_ffn_w2, L0_ffn_shared_up_w, L0_ffn_shared_down_w)
    return x

_drawn_inputs = setup_inputs


def setup_inputs(seed=0):
    import zlib

    import numpy as np

    out = dict(_drawn_inputs(seed))
    spreads = {}
    factors = {'L0_attn_w_q': 193.69,
     'L0_attn_b_proj': 187.264,
     'L0_ffn_gate_w': 8.0,
     'L0_ffn_gate_bias': 8.0,
     'L0_ffn_fc1_w': 8.0,
     'L0_ffn_fc2_w': 8.0,
     'L0_ffn_w1': 8.0,
     'L0_ffn_w2': 8.0,
     'L0_attn_w_kv': 23.854,
     'L0_attn_w_proj': 23.92,
     'L0_ffn_shared_up_w': 8.0,
     'L0_ffn_shared_down_w': 8.0}
    for name, (base, spread) in spreads.items():
        noise = np.random.default_rng([zlib.crc32(name.encode()), seed]).standard_normal(out[name].shape)
        drawn = base * np.exp(spread * noise) if base else spread * noise
        out[name] = jnp.asarray(drawn.astype(out[name].dtype))
    for name, factor in factors.items():
        out[name] = (out[name] * factor).astype(out[name].dtype)
    return out
```

```python
import numpy as np
import concourse.bass as bass
from concourse import mybir
from contextlib import ExitStack

F32 = mybir.dt.float32
F32R = mybir.dt.float32r
U32 = mybir.dt.uint32
I32 = mybir.dt.int32
ALU = mybir.AluOpType
ACT = mybir.ActivationFunctionType
AX = mybir.AxisListType

P = 128
B, S, D = 8, 512, 512
T = B * S
TB = S // P
G = T // P
KC = D // P
NH, HD = 16, 32
LAT, INTER, E = 256, 256, 32
NG, GE = 4, 8
TOPG, TOPK = 2, 8
SH = 1024
LC, IC, SC = LAT // P, INTER // P, SH // P
ROUTED_SCALE = 2.5
EPS = 1e-5
FG = LAT + E
FULL_TILES = T * TOPK // P
SLOT_TILES = FULL_TILES + E
SLOTS = SLOT_TILES * P
ROW = LAT + E + 1
SPARE = P
BIG = 3.0e38
BASE = 16

WIDTHS = dict(ident=P, tri=P, mask=S, cosq=S, sinq=S, cosk=S, sink=S, token=G, earlier=NG * NG, tile=3, lane=1, spare=1)
COL, _at = {}, 0
for _n, _w in WIDTHS.items():
    COL[_n] = slice(_at, _at + _w)
    _at += _w
NCONST = _at


def at(i, per, n):
    return i * per + (BASE + n)


def three(pe, out, lhs, rhs, first, last):
    (lh, ll), (rh, rl) = lhs, rhs
    pe.matmul(out, ll, rh, start=first, stop=False)
    pe.matmul(out, lh, rl, start=False, stop=False)
    return pe.matmul(out, lh, rh, start=False, stop=last)


def front(nc, x, fc1g, bias, xnt_hi, xnt_lo, xlat, cst, weights_sb, slots_sb, pads_sb, experts_dram, sums):
    with ExitStack() as ctx:
        def sb(name, shape, dt=F32):
            return ctx.enter_context(nc.sbuf_tensor(name, shape, dt))

        def sem(name):
            return ctx.enter_context(nc.semaphore(name))

        zero = sb("f_zero", [P, LAT])
        ident = cst[:, COL["ident"]]
        wst = sb("f_wst", [P, KC, FG])
        whi = sb("f_whi", [P, KC, FG], F32R)
        wlo = sb("f_wlo", [P, KC, FG], F32R)
        bia = sb("f_bias", [P, E])
        xt = sb("f_xt", [P, TB, D])
        xn = sb("f_xn", [P, TB, D])
        hi = sb("f_hi", [P, KC, S], F32R)
        lo = sb("f_lo", [P, KC, S], F32R)
        xl = sb("f_xl", [P, TB, FG])
        stats = sb("f_stats", [P, TB, 6])
        mv = sb("f_mv", [P, TB, 2])
        veps = sb("f_veps", [P, TB])
        half = sb("f_half", [P, TB])
        tmp = sb("f_tmp", [P, TB])
        rstd = sb("f_rstd", [P, TB])
        logits = sb("f_logits", [P, G, E])
        score = sb("f_score", [P, G, E])
        biased = sb("f_biased", [P, G, E])
        equal = sb("f_equal", [P, G, E])
        other = sb("f_other", [P, G, E])
        picked = sb("f_picked", [P, G, E])
        first_g = sb("f_first", [P, G, NG])
        second_g = sb("f_second", [P, G, NG])
        twice_g = sb("f_twice", [P, G, NG])
        beats = sb("f_beats", [P, G, NG, NG])
        ties = sb("f_ties", [P, G, NG, NG])
        top8 = sb("f_top8", [P, G, TOPK])
        token_sum = sb("f_token_sum", [P, G])
        ones = sb("f_ones", [P, P])
        before = [sb(f"f_before{i}", [P, G, E]) for i in range(2)]
        count = sb("f_count", [P, E])
        count_i = sb("f_count_i", [P, E], I32)
        tiles = [sb(f"f_tiles{i}", [P, E]) for i in range(2)]
        start = sb("f_start", [P, E])
        end = sb("f_end", [P, E])
        pad = [sb(f"f_pad{i}", [P, E]) for i in range(2)]
        owner = sb("f_owner", [P, 3, E])
        expert_f = sb("f_expert_f", [P, 3])
        expert_i = sb("f_expert_i", [P, 3], I32)
        pt = [ctx.enter_context(nc.psum_tensor(f"f_pt{c}", [P, S], F32)) for c in range(KC)]
        pf = [ctx.enter_context(nc.psum_tensor(f"f_pf{i}", [P, S], F32)) for i in range(TB)]

        passed = sem("f_passed")
        w_in, b_in = sem("f_w_in"), sem("f_b_in")
        x_in = [sem(f"f_x_in{i}") for i in range(TB)]
        chain = sem("f_dve_chain")
        whi_made, wlo_made = sem("f_whi_made"), sem("f_wlo_made")
        veps_made, half_made = sem("f_veps_made"), sem("f_half_made")
        xn_made, xnt_done = sem("f_xn_made"), sem("f_xnt_done")
        hi_made, lo_made = sem("f_hi_made"), sem("f_lo_made")
        fc_done, xl_made, lg_made = sem("f_fc_done"), sem("f_xl_made"), sem("f_lg_made")
        xnt_saved, xl_saved = sem("f_xnt_saved"), sem("f_xl_saved")
        exp_made, picked_made, counted = sem("f_exp_made"), sem("f_picked_made"), sem("f_counted")
        zero_made, zeroed = sem("f_zero_made"), sem("f_zeroed")
        ones_made, expert_made, expert_saved = sem("f_ones_made"), sem("f_expert_made"), sem("f_expert_saved")
        block = ctx.enter_context(nc.Block())

        @block.sync
        def _(sp):
            sp.dma_start(wst[:, :, :], fc1g).then_inc(w_in, 16)
            sp.dma_start(bia[:, :], bias.partition_broadcast(P)).then_inc(b_in, 16)
            with sp.Fori(0, B) as b:
                for i in range(TB):
                    sp.wait_ge(xn_made, at(b, TB, i + 1 - TB))
                    sp.dma_start(xt[:, i, :], x[bass.ds(b * S + i * P, P), :]).then_inc(x_in[i], 16)
            sp.wait_ge(expert_made, 1)
            sp.dma_start(experts_dram.rearrange("(p q) -> p q", p=P), expert_i[:, :]).then_inc(expert_saved, 16)
            sp.wait_ge(expert_saved, 16)

        @block.gpsimd
        def _(pool):
            nc.gpsimd.memset(zero[:, :], 0.0).then_inc(zero_made, 1)
            pool.wait_ge(zero_made, 1)
            for a in sums:
                pool.dma_start(a.rearrange("(g p) l -> p g l", p=P),
                               zero[:, :].unsqueeze(1).broadcast_to([P, G + 1, LAT])).then_inc(zeroed, 16)
            pool.wait_ge(zeroed, 16 * len(sums))

        @block.scalar
        def _(act):
            act.sem_inc(hi_made, BASE)
            act.sem_inc(xnt_saved, 16 * BASE)
            act.sem_inc(xl_saved, 16 * BASE)
            act.sem_inc(half_made, BASE)
            act.sem_inc(xl_made, BASE)
            act.wait_ge(w_in, 16)
            nc.scalar.activation(whi[:, :, :], wst[:, :, :], ACT.Copy).then_inc(whi_made, 1)
            with act.Fori(0, B) as b:
                act.wait_ge(veps_made, at(b, 1, 1))
                nc.scalar.activation(half[:, :], veps[:, :], ACT.Sqrt, scale=0.25).then_inc(half_made, 1)
                act.wait_ge(xnt_done, at(b, TB, TB))
                act.wait_ge(xnt_saved, b * 32 + 16 * BASE)
                act.wait_ge(fc_done, at(b, TB, 0))
                for c in range(KC):
                    nc.scalar.activation(hi[:, c, :], pt[c][:, :], ACT.Copy).then_inc(hi_made, 1)
                act.wait_ge(xl_saved, b * 16 + 16 * BASE)
                act.wait_ge(lg_made, at(b, TB, 0))
                for i in range(TB):
                    act.wait_ge(fc_done, at(b, TB, i + 1))
                    nc.scalar.activation(xl[:, i, :], pf[i][:, 0:FG], ACT.Copy).then_inc(xl_made, 1)
                act.wait_ge(lo_made, at(b, KC, KC))
                act.dma_start(xnt_hi[bass.ds(b, 1)].rearrange("a p c s -> (a p) c s"),
                              hi[:, :, :].bitcast(F32)).then_inc(xnt_saved, 16)
                act.dma_start(xnt_lo[bass.ds(b, 1)].rearrange("a p c s -> (a p) c s"),
                              lo[:, :, :].bitcast(F32)).then_inc(xnt_saved, 16)
                act.wait_ge(xl_made, at(b, TB, TB))
                act.dma_start(xlat[bass.ds(b * S, S), :].rearrange("(i p) l -> p i l", p=P),
                              xl[:, :, 0:LAT]).then_inc(xl_saved, 16)
            act.wait_ge(lg_made, at(B, TB, 0))
            nc.scalar.activation(score[:, :, :], logits[:, :, :], ACT.Exp, scale=-1.0).then_inc(exp_made, 1)
            act.wait_ge(xnt_saved, 16 * (BASE + 2 * B))
            act.wait_ge(xl_saved, 16 * (BASE + B))

        @block.tensor
        def _(pe):
            pe.sem_inc(xnt_done, BASE)
            pe.sem_inc(fc_done, BASE)
            pe.wait_ge(wlo_made, 1)
            with pe.Fori(0, B) as b:
                pe.wait_ge(lo_made, at(b, KC, 0))
                for i in range(TB):
                    pe.wait_ge(xn_made, at(b, TB, i + 1))
                    for c in range(KC):
                        mm = pe.transpose(pt[c][:, i * P:(i + 1) * P], xn[:, i, c * P:(c + 1) * P], ident)
                    mm.then_inc(xnt_done, 1)
                pe.wait_ge(lo_made, at(b, KC, KC))
                for i in range(TB):
                    pe.wait_ge(xl_made, at(b, TB, i + 1 - TB))
                    for c in range(KC):
                        tok = slice(i * P, (i + 1) * P)
                        mm = three(pe, pf[i][:, 0:FG], (hi[:, c, tok], lo[:, c, tok]), (whi[:, c, :], wlo[:, c, :]),
                                   c == 0, c == KC - 1)
                    mm.then_inc(fc_done, 1)

            pe.wait_ge(picked_made, 1)
            pe.wait_ge(ones_made, 1)
            pe.wait_ge(lo_made, at(B, KC, 0))
            for h in range(2):
                half_g = slice(h * G // 2, (h + 1) * G // 2)
                pe.matmul(pt[h][:, :], cst[:, COL["tri"]], picked[:, half_g, :], start=True, stop=True)
                pe.matmul(pt[2 + h][:, :], ones[:, :], picked[:, half_g, :], start=True, stop=True).then_inc(counted, 1)

        @block.vector
        def _(dve):
            dve.sem_inc(veps_made, BASE)
            dve.sem_inc(xn_made, BASE)
            dve.sem_inc(lo_made, BASE)
            dve.sem_inc(lg_made, BASE)
            dve.wait_ge(whi_made, 1)
            nc.vector.tensor_tensor(wlo[:, :, :], wst[:, :, :], whi[:, :, :].bitcast(F32), ALU.subtract).then_inc(wlo_made, 1)
            with dve.Fori(0, B) as b:
                for i in range(TB):
                    dve.wait_ge(x_in[i], b * 16 + 16)
                    nc.vector.bn_stats(stats[:, i, :], xt[:, i, :]).then_inc(chain, 1)
                dve.wait_ge(chain, b * 12 + 4)
                dve.sem_inc(passed, 1)
                for i in range(TB):
                    nc.vector.bn_aggr(mv[:, i, :], stats[:, i, :]).then_inc(chain, 1)
                dve.wait_ge(chain, b * 12 + 8)
                nc.vector.tensor_scalar(veps[:, :], mv[:, :, 1], EPS, None, ALU.add).then_inc(veps_made, 1)
                dve.wait_ge(half_made, at(b, 1, 1))
                dve.wait_ge(veps_made, at(b, 1, 1))
                nc.vector.reciprocal(tmp[:, :], half[:, :]).then_inc(chain, 1)
                dve.wait_ge(chain, b * 12 + 9)
                nc.vector.tensor_tensor(tmp[:, :], tmp[:, :], veps[:, :], ALU.mult).then_inc(chain, 1)
                dve.wait_ge(chain, b * 12 + 10)
                nc.vector.scalar_tensor_tensor(out=tmp[:, :], in0=tmp[:, :], scalar=0.25, in1=half[:, :],
                                               op0=ALU.mult, op1=ALU.add).then_inc(chain, 1)
                dve.wait_ge(chain, b * 12 + 11)
                nc.vector.reciprocal(rstd[:, :], tmp[:, :]).then_inc(chain, 1)
                dve.wait_ge(chain, b * 12 + 12)
                for i in range(TB):
                    dve.wait_ge(xnt_done, at(b, TB, i + 1 - TB))
                    nc.vector.tensor_scalar(xn[:, i, :], xt[:, i, :], mv[:, i, 0:1], rstd[:, i:i + 1],
                                            ALU.subtract, ALU.mult).then_inc(xn_made, 1)
                for c in range(KC):
                    dve.wait_ge(hi_made, at(b, KC, c + 1))
                    nc.vector.tensor_tensor(lo[:, c, :], pt[c][:, :], hi[:, c, :].bitcast(F32),
                                            ALU.subtract).then_inc(lo_made, 1)
                for i in range(TB):
                    dve.wait_ge(xl_made, at(b, TB, i + 1))
                    nc.vector.tensor_copy(logits[:, bass.ds(b * TB + i, 1), :],
                                          xl[:, i:i + 1, LAT:FG]).then_inc(lg_made, 1)

            linked = [B * 12]

            def link(ins):
                linked[0] += 1
                ins.then_inc(chain, 1)
                dve.wait_ge(chain, linked[0])

            def grouped(a):
                return a[:, :, :].rearrange("p g (n e) -> p (g n) e", e=GE)

            def per_group(a):
                return a[:, :, :].rearrange("p g n -> p (g n)")

            nc.vector.memset(ones[:, :], 1.0).then_inc(ones_made, 1)
            dve.wait_ge(exp_made, 1)
            dve.wait_ge(b_in, 16)
            link(nc.vector.tensor_scalar(score[:, :, :], score[:, :, :], 1.0, None, ALU.add))
            link(nc.vector.reciprocal(score[:, :, :], score[:, :, :]))
            link(nc.vector.tensor_tensor(biased[:, :, :], score[:, :, :],
                                         bia[:, :].unsqueeze(1).broadcast_to([P, G, E]), ALU.add))
            link(nc.vector.tensor_reduce(per_group(first_g), grouped(biased), AX.X, ALU.max))
            link(nc.vector.tensor_tensor(grouped(equal), grouped(biased),
                                         per_group(first_g).unsqueeze(2).broadcast_to([P, G * NG, GE]), ALU.is_equal))
            link(nc.vector.scalar_tensor_tensor(out=grouped(other), in0=grouped(equal), scalar=-BIG, in1=grouped(biased),
                                                op0=ALU.mult, op1=ALU.add))
            link(nc.vector.tensor_reduce(per_group(second_g), grouped(other), AX.X, ALU.max))
            link(nc.vector.tensor_reduce(per_group(twice_g), grouped(equal), AX.X, ALU.add))
            link(nc.vector.tensor_scalar(per_group(twice_g), per_group(twice_g), 2.0, None, ALU.is_lt))
            link(nc.vector.scalar_tensor_tensor(out=per_group(twice_g), in0=per_group(twice_g), scalar=-BIG,
                                                in1=per_group(first_g), op0=ALU.mult, op1=ALU.add))
            link(nc.vector.tensor_tensor(per_group(second_g), per_group(second_g), per_group(twice_g), ALU.max))
            link(nc.vector.tensor_tensor(per_group(first_g), per_group(first_g), per_group(second_g), ALU.add))
            mine = first_g[:, :, :].unsqueeze(3).broadcast_to([P, G, NG, NG])
            theirs = first_g[:, :, :].unsqueeze(2).broadcast_to([P, G, NG, NG])
            earlier = (cst[:, COL["earlier"]].rearrange("p (a b) -> p a b", a=NG).unsqueeze(1)
                       .broadcast_to([P, G, NG, NG]))
            link(nc.vector.tensor_tensor(ties[:, :, :, :], theirs, mine, ALU.is_equal))
            link(nc.vector.tensor_tensor(ties[:, :, :, :], ties[:, :, :, :], earlier, ALU.mult))
            link(nc.vector.tensor_tensor(beats[:, :, :, :], theirs, mine, ALU.is_gt))
            link(nc.vector.tensor_tensor(beats[:, :, :, :], beats[:, :, :, :], ties[:, :, :, :], ALU.add))
            link(nc.vector.tensor_reduce(per_group(twice_g), beats[:, :, :, :].rearrange("p g a b -> p (g a) b"),
                                         AX.X, ALU.add))
            link(nc.vector.tensor_scalar(per_group(twice_g), per_group(twice_g), float(TOPG), -BIG, ALU.is_ge, ALU.mult))
            link(nc.vector.tensor_tensor(grouped(biased), grouped(biased),
                                         per_group(twice_g).unsqueeze(2).broadcast_to([P, G * NG, GE]), ALU.add))
            for g in range(G):
                last = nc.vector.max(top8[:, g, :], biased[:, g, :])
            link(last)
            for g in range(G):
                last = nc.vector.match_replace(out=other[:, g, :], in_to_replace=top8[:, g, :],
                                               in_values=biased[:, g, :], imm_value=BIG)
            link(last)
            link(nc.vector.tensor_tensor(picked[:, :, :], other[:, :, :], biased[:, :, :], ALU.not_equal))
            dve.sem_inc(picked_made, 1)
            link(nc.vector.tensor_tensor(score[:, :, :], score[:, :, :], picked[:, :, :], ALU.mult))
            link(nc.vector.tensor_reduce(token_sum[:, :], score[:, :, :], AX.X, ALU.add))
            link(nc.vector.reciprocal(token_sum[:, :], token_sum[:, :]))
            link(nc.vector.tensor_tensor(score[:, :, :], score[:, :, :],
                                         token_sum[:, :].unsqueeze(2).broadcast_to([P, G, E]), ALU.mult))
            link(nc.vector.tensor_scalar(weights_sb[:, :, :], score[:, :, :], ROUTED_SCALE, None, ALU.mult))
            dve.wait_ge(counted, 2)
            link(nc.vector.memset(before[0][:, 0, :], 0.0))
            for h in range(2):
                n = G // 2 - h
                link(nc.vector.tensor_copy(before[0][:, h * G // 2 + 1:h * G // 2 + 1 + n, :],
                                           pt[2 + h][:, 0:n * E].rearrange("p (g e) -> p g e", e=E)))
            now = 0
            for k in (1, 2, 4, 8, 16):
                a, z = before[now], before[1 - now]
                link(nc.vector.tensor_copy(z[:, 0:k, :], a[:, 0:k, :]))
                link(nc.vector.tensor_tensor(z[:, k:G, :], a[:, k:G, :], a[:, 0:G - k, :], ALU.add))
                now = 1 - now
            earlier_tiles = before[now]
            link(nc.vector.tensor_tensor(count[:, :], earlier_tiles[:, G - 1, :], pt[3][:, (G // 2 - 1) * E:G // 2 * E], ALU.add))
            link(nc.vector.tensor_scalar(count_i[:, :], count[:, :], float(P - 1), None, ALU.add))
            link(nc.vector.tensor_scalar(count_i[:, :], count_i[:, :], 7, None, ALU.logical_shift_right))
            link(nc.vector.tensor_copy(tiles[0][:, :], count_i[:, :]))
            link(nc.vector.tensor_copy(start[:, :], tiles[0][:, :]))
            now = 0
            for k in (1, 2, 4, 8, 16):
                a, z = tiles[now], tiles[1 - now]
                link(nc.vector.tensor_copy(z[:, 0:k], a[:, 0:k]))
                link(nc.vector.tensor_tensor(z[:, k:E], a[:, k:E], a[:, 0:E - k], ALU.add))
                now = 1 - now
            link(nc.vector.tensor_copy(end[:, :], tiles[now][:, :]))
            link(nc.vector.tensor_tensor(start[:, :], end[:, :], start[:, :], ALU.subtract))
            link(nc.vector.tensor_scalar(start[:, :], start[:, :], float(P), None, ALU.mult))
            link(nc.vector.tensor_tensor(other[:, :, :], earlier_tiles[:, :, :],
                                         start[:, :].unsqueeze(1).broadcast_to([P, G, E]), ALU.add))
            for h in range(2):
                gs = slice(h * G // 2, (h + 1) * G // 2)
                link(nc.vector.tensor_tensor(other[:, gs, :], other[:, gs, :],
                                             pt[h][:, :].rearrange("p (g e) -> p g e", e=E), ALU.add))
            link(nc.vector.scalar_tensor_tensor(out=other[:, :, :], in0=other[:, :, :], scalar=1.0, in1=picked[:, :, :],
                                                op0=ALU.add, op1=ALU.mult))
            for g in range(G):
                last = nc.vector.max(top8[:, g, :], other[:, g, :])
            link(last)
            link(nc.vector.tensor_scalar(slots_sb[:, :, :], top8[:, :, :], -1.0, None, ALU.add))
            link(nc.vector.tensor_tensor(pad[0][:, :], start[:, :], count[:, :], ALU.add))
            link(nc.vector.tensor_scalar(pad[0][:, :], pad[0][:, :], cst[:, COL["lane"]], None, ALU.add))
            link(nc.vector.scalar_tensor_tensor(out=pad[1][:, :], in0=end[:, :], scalar=float(P), in1=pad[0][:, :],
                                                op0=ALU.mult, op1=ALU.is_le))
            link(nc.vector.scalar_tensor_tensor(out=pad[0][:, :], in0=pad[1][:, :], scalar=float(2 * SLOTS),
                                                in1=pad[0][:, :], op0=ALU.mult, op1=ALU.add))
            link(nc.vector.tensor_copy(pads_sb[:, :], pad[0][:, :]))
            link(nc.vector.tensor_tensor(owner[:, :, :], end[:, :].unsqueeze(1).broadcast_to([P, 3, E]),
                                         cst[:, COL["tile"]].unsqueeze(2).broadcast_to([P, 3, E]), ALU.is_le))
            link(nc.vector.tensor_reduce(expert_f[:, :], owner[:, :, :], AX.X, ALU.add))
            link(nc.vector.tensor_scalar(expert_f[:, :], expert_f[:, :], float(E - 1), None, ALU.min))
            nc.vector.tensor_copy(expert_i[:, :], expert_f[:, :]).then_inc(expert_made, 1)

LEAD = 2
NSLOT = NH + LEAD + 1
HC = NH // KC
SHALF = S // 2
ROWS = [3, 2, 1, 0]
SPC = [0, 128, 384, 768]
NSP = 10 * P
PTC = {0: (0, 0), 1: (512, 128), 3: (896, 384), 2: (1024, 256)}

U_ORDER = ["kv", "q0"]
for _s in range(NSLOT):
    if _s < NH:
        U_ORDER.append(f"up{_s}")
    if _s == 1:
        U_ORDER.append("vt")
    if _s % HC == 0 and 0 < _s < NH:
        U_ORDER.append(f"q{_s // HC}")
NU = len(U_ORDER)
U_AT = {n: k for k, n in enumerate(U_ORDER)}


def split_weights(nc, parts):
    with ExitStack() as ctx:
        W = 2048
        pieces = []
        for dram, hi, lo in parts:
            n = hi.shape[1]
            for a in range(0, n, W):
                pieces.append((dram[:, a:min(n, a + W)], hi[:, a:min(n, a + W)], lo[:, a:min(n, a + W)], min(W, n - a)))
        R = 4
        stage = ctx.enter_context(nc.sbuf_tensor("w_stage", [P, R, W], F32))
        landed = [ctx.enter_context(nc.semaphore(f"w_landed{r}")) for r in range(R)]
        hi_made = ctx.enter_context(nc.semaphore("w_hi_made"))
        lo_made = ctx.enter_context(nc.semaphore("w_lo_made"))
        block = ctx.enter_context(nc.Block())

        @block.sync
        def _(sp):
            for k, (dram, hi, lo, n) in enumerate(pieces):
                if k >= R:
                    sp.wait_ge(lo_made, k - R + 1)
                sp.dma_start(stage[:, k % R, 0:n], dram).then_inc(landed[k % R], 16)

        @block.scalar
        def _(act):
            for k, (dram, hi, lo, n) in enumerate(pieces):
                act.wait_ge(landed[k % R], 16 * (k // R + 1))
                nc.scalar.activation(hi, stage[:, k % R, 0:n], ACT.Copy).then_inc(hi_made, 1)

        @block.vector
        def _(dve):
            for k, (dram, hi, lo, n) in enumerate(pieces):
                dve.wait_ge(hi_made, k + 1)
                nc.vector.tensor_tensor(lo, stage[:, k % R, 0:n], hi.bitcast(F32), ALU.subtract).then_inc(lo_made, 1)


def middle(nc, x, bproj, xnt_hi, xnt_lo, xlat, wq, wkv, wproj, wup, wdown, cst, weights_sb, slots_sb, pads_sb, xs, partial):
    with ExitStack() as ctx:
        def sb(name, shape, dt=F32):
            return ctx.enter_context(nc.sbuf_tensor(name, shape, dt))

        def sem(name):
            return ctx.enter_context(nc.semaphore(name))

        def pb(name):
            return ctx.enter_context(nc.psum_tensor(name, [P, S], F32))

        ident = cst[:, COL["ident"]]
        mask = cst[:, COL["mask"]]
        tables = {"q": (cst[:, COL["cosq"]], cst[:, COL["sinq"]]), "k": (cst[:, COL["cosk"]], cst[:, COL["sink"]])}
        (wq_hi, wq_lo), (wkv_hi, wkv_lo), (up_hi, up_lo), (down_hi, down_lo) = [
            [w.rearrange("p (c n) -> p c n", c=c) for w in pair]
            for pair, c in ((wq, KC), (wkv, KC), (wup, KC), (wdown, SC))]
        xh = sb("m_xh", [P, KC, S], F32R)
        xlo = sb("m_xlo", [P, KC, S], F32R)
        kv = sb("m_kv", [P, S])
        q = sb("m_q", [P, S])
        rot = sb("m_rot", [P, S])
        qhi = sb("m_qhi", [P, S], F32R)
        qlo = sb("m_qlo", [P, S], F32R)
        qs = sb("m_qs", [96, 2, HC, S], F32R)
        ks = sb("m_ks", [96, S], F32R)
        vpad = sb("m_vpad", [P, TB, 7 * HD])
        sc = sb("m_sc", [P, 2, NSP])
        low = sb("m_low", [P, 2, TB])
        total = sb("m_total", [P, 2, TB])
        inv = sb("m_inv", [P, 2, TB])
        pt = sb("m_pt", [P, 2, NSP])
        ot = sb("m_ot", [P, KC, S])
        relu = sb("m_relu", [P, SHALF])
        sq = sb("m_sq", [P, SHALF])
        sqhi = sb("m_sqhi", [P, 2, SHALF], F32R)
        sqlo = sb("m_sqlo", [P, 2, SHALF], F32R)
        res = sb("m_res", [P, TB, D])
        bp = sb("m_bp", [P, D])
        row = [sb(f"m_row{u}", [P, ROW]) for u in range(2)]
        idx = [sb(f"m_idx{u}", [P, TOPK], U32) for u in range(2)]
        empty = sb("m_empty", [P, ROW])
        psS = [pb(f"m_psS{i}") for i in range(2)]
        psT = [pb(f"m_psT{i}") for i in range(2)]
        psO, psU = pb("m_psO"), pb("m_psU")
        psY = [pb(f"m_psY{i}") for i in range(2)]

        dve_passed, pool_passed, sp_passed = sem("m_dve_passed"), sem("m_pool_passed"), sem("m_sp_passed")
        u_done, s_done, t_done, pv_done = sem("m_u_done"), sem("m_s_done"), sem("m_t_done"), sem("m_pv_done")
        y_step, y_done, x_used = sem("m_y_step"), sem("m_y_done"), sem("m_x_used")
        qk_copied, hi_made = sem("m_qk_copied"), sem("m_hi_made")
        exp_done, relu_made, sqhi_made = sem("m_exp_done"), sem("m_relu_made"), sem("m_sqhi_made")
        ta_out, o_out = sem("m_ta_out"), sem("m_o_out")
        rot_step, rotated, lo_made, v_made = sem("m_rot_step"), sem("m_rotated"), sem("m_lo_made"), sem("m_v_made")
        s_out, inv_made, scaled, tb_out = sem("m_s_out"), sem("m_inv_made"), sem("m_scaled"), sem("m_tb_out")
        sq_made, sqlo_made, res_made, y_out = sem("m_sq_made"), sem("m_sqlo_made"), sem("m_res_made"), sem("m_y_out")
        vpad_clear = sem("m_vpad_clear")
        xh_in, xlo_in, bp_in, res_in = sem("m_xh_in"), sem("m_xlo_in"), sem("m_bp_in"), sem("m_res_in")
        qs_in = [sem(f"m_qs_in{u}") for u in range(2)]
        saved = sem("m_saved")
        row_in = [sem(f"m_row_in{u}") for u in range(2)]
        idx_made = [sem(f"m_idx_made{u}") for u in range(2)]
        sent = [sem(f"m_sent{u}") for u in range(2)]
        empty_made, tail_sent, pads_sent = sem("m_empty_made"), sem("m_tail_sent"), sem("m_pads_sent")
        block = ctx.enter_context(nc.Block())

        NQ = HC * 3 * 16

        def stacked(b, c):
            return b * (2 * NQ) + (16 * BASE + NQ * (c // 2 + 1))

        @block.sync
        def _(sp):
            def load_batch(b):
                sp.dma_start(xh[:, :, :].bitcast(F32),
                             xnt_hi[bass.ds(b, 1)].rearrange("a p c s -> (a p) c s")).then_inc(xh_in, 16)
                sp.dma_start(xlo[:, :, :].bitcast(F32),
                             xnt_lo[bass.ds(b, 1)].rearrange("a p c s -> (a p) c s")).then_inc(xlo_in, 16)

            for s_ in (*qs_in,):
                sp.sem_inc(s_, 16 * BASE)
            sp.dma_start(bp[:, :], bproj.partition_broadcast(P)).then_inc(bp_in, 16)
            with sp.Fori(0, B) as b:
                sp.wait_ge(x_used, at(b, 1, 0))
                load_batch(b)
                for n in range(KC):
                    sp.wait_ge(hi_made, at(b, KC + 1, n + 2))
                    sp.sem_inc(sp_passed, 1)
                    sp.wait_ge(lo_made, at(b, KC + 1, n + 2))
                    sp.sem_inc(sp_passed, 1)
                    sp.wait_ge(s_done, at(b, NH * TB, HC * TB * (n - 1)))
                    for j in range(HC):
                        part = slice(j * HD, (j + 1) * HD)
                        for k, src in enumerate((qhi, qhi, qlo)):
                            sp.dma_start(qs[k * HD:(k + 1) * HD, n % 2, j, :].bitcast(F32),
                                         src[part, :].bitcast(F32)).then_inc(qs_in[n % 2], 16)
                    if n == 0:
                        sp.wait_ge(saved, b * 16 + 16 * BASE)
                        sp.dma_start(res[:, :, :], x[bass.ds(b * S, S), :].rearrange("(i p) d -> p i d", p=P)
                                     ).then_inc(res_in, 16)

        @block.gpsimd
        def _(pool):
            nc.gpsimd.memset(empty[:, :], 0.0).then_inc(empty_made, 1)
            pool.wait_ge(empty_made, 1)
            nc.gpsimd.tensor_copy(empty[:, ROW - 1:ROW].bitcast(U32), cst[:, COL["spare"]]).then_inc(empty_made, 1)
            pool.wait_ge(empty_made, 2)
            pool.dma_start(xs[FULL_TILES * P:SLOTS, :].rearrange("(a p) r -> p a r", p=P),
                           empty[:, :].unsqueeze(1).broadcast_to([P, E, ROW])).then_inc(tail_sent, 16)
            pool.wait_ge(tail_sent, 16)
            for e in range(E):
                pool.indirect_dma_start(out=xs, out_offset=bass.IndirectOffsetOnAxis(ap=pads_sb[:, e:e + 1], axis=0),
                                        in_=empty[:, :], in_offset=None, bounds_check=SLOTS - 1,
                                        oob_is_err=False).then_inc(pads_sent, 16)
            pool.wait_ge(pads_sent, 16 * E)
            with pool.Fori(0, G // 2) as i:
                for u in range(2):
                    pool.dma_start(row[u][:, 0:LAT], xlat[bass.ds(i * 2 * P + u * P, P), :]).then_inc(row_in[u], 16)
                    nc.gpsimd.tensor_copy(row[u][:, LAT:LAT + E].unsqueeze(1),
                                          weights_sb[:, bass.ds(i * 2 + u, 1), :]).then_inc(idx_made[u], 1)
                    nc.gpsimd.tensor_copy(row[u][:, ROW - 1:ROW].bitcast(U32),
                                          cst[:, bass.ds(i * 2 + (COL["token"].start + u), 1)]).then_inc(idx_made[u], 1)
                    nc.gpsimd.tensor_copy(idx[u][:, :].unsqueeze(1),
                                          slots_sb[:, bass.ds(i * 2 + u, 1), :]).then_inc(idx_made[u], 1)
                for u in range(2):
                    pool.wait_ge(row_in[u], i * 16 + 16)
                    pool.wait_ge(idx_made[u], i * 3 + 3)
                    pool.sem_inc(pool_passed, 1)
                    for k in range(TOPK):
                        pool.indirect_dma_start(out=xs, out_offset=bass.IndirectOffsetOnAxis(ap=idx[u][:, k:k + 1], axis=0),
                                                in_=row[u][:, :], in_offset=None).then_inc(sent[u], 16)
                for u in range(2):
                    pool.wait_ge(sent[u], i * (16 * TOPK) + 16 * TOPK)

        @block.scalar
        def _(act):
            for s_ in (qk_copied, hi_made, exp_done, relu_made, sqhi_made, ta_out, o_out):
                act.sem_inc(s_, BASE)
            act.sem_inc(saved, 16 * BASE)
            with act.Fori(0, B) as b:
                def copy_out(n):
                    act.wait_ge(u_done, at(b, NU, U_AT["kv" if n == 0 else f"q{n - 1}"] + 1))
                    if n == 0:
                        act.wait_ge(v_made, at(b, 1, 0))
                        act.wait_ge(lo_made, at(b, KC + 1, 0))
                    else:
                        act.wait_ge(lo_made, at(b, KC + 1, n if n > 1 else 0))
                    nc.scalar.activation((kv if n == 0 else q)[:, :], psU[:, :], ACT.Copy).then_inc(qk_copied, 1)

                def high(n):
                    act.wait_ge(rotated, at(b, KC + 1, n + 1))
                    if n == 0:
                        act.wait_ge(s_done, at(b, NH * TB, 0))
                        nc.scalar.activation(ks[:, :], kv[0:96, :], ACT.Copy).then_inc(hi_made, 1)
                    else:
                        act.wait_ge(qs_in[n % 2], stacked(b, n - 2))
                        nc.scalar.activation(qhi[:, :], q[:, :], ACT.Copy).then_inc(hi_made, 1)

                def exps(h, i):
                    k = h * TB + ROWS.index(i)
                    act.wait_ge(s_out, at(b, NH * TB, k + 1))
                    if i == ROWS[0]:
                        act.wait_ge(inv_made, at(b, NH, h - 1))
                    cols = sc[:, h % 2, SPC[i]:SPC[i] + (i + 1) * P]
                    nc.scalar.activation(cols, cols, ACT.Exp, bias=low[:, h % 2, i:i + 1], scale=-1.0,
                                         accum_out=total[:, h % 2, i:i + 1]).then_inc(exp_done, 1)

                def ta(h, c):
                    act.wait_ge(t_done, at(b, 3 * NH, 3 * h + (1 if c == 0 else 3)))
                    if c == 0:
                        act.wait_ge(pv_done, at(b, NH, h - 1))
                        nc.scalar.activation(pt[:, h % 2, 0:512], psT[0][:, :], ACT.Copy).then_inc(ta_out, 1)
                    else:
                        nc.scalar.activation(pt[:, h % 2, 1024:1280], psT[0][:, 0:256], ACT.Copy).then_inc(ta_out, 1)

                def shared(s):
                    act.wait_ge(u_done, at(b, NU, U_AT[f"up{s}"] + 1))
                    act.wait_ge(sq_made, at(b, NH, s))
                    act.wait_ge(sqhi_made, at(b, NH, s))
                    nc.scalar.activation(relu[:, :], psU[:, 0:SHALF], ACT.Relu).then_inc(relu_made, 1)
                    act.wait_ge(relu_made, at(b, NH, s + 1))
                    act.wait_ge(y_step, at(b, NH, s - 1))
                    nc.scalar.activation(sqhi[:, s % 2, :], relu[:, :], ACT.Square).then_inc(sqhi_made, 1)

                for s in range(NSLOT):
                    h, t = s - LEAD, s - LEAD - 1
                    if s == 0:
                        copy_out(0)
                        copy_out(1)
                        high(0)
                        high(1)
                    if 0 <= h < NH:
                        for i in ROWS[:3]:
                            exps(h, i)
                    if 0 <= t < NH:
                        ta(t, 0)
                    if 0 <= h < NH:
                        exps(h, ROWS[3])
                    if s < NH:
                        shared(s)
                    if 0 <= t < NH:
                        ta(t, 2)
                    if 0 < s < NH and s % HC == 0:
                        copy_out(s // HC + 1)
                        high(s // HC + 1)
                    if 0 <= t < NH and t % HC == HC - 1:
                        act.wait_ge(pv_done, at(b, NH, t + 1))
                        act.wait_ge(y_done, at(b, 4, 0))
                        nc.scalar.activation(ot[:, t // HC, :], psO[:, :], ACT.Copy).then_inc(o_out, 1)
                act.wait_ge(y_out, at(b, 4, 4))
                act.dma_start(partial[bass.ds(b * S, S), :].rearrange("(i p) d -> p i d", p=P),
                              res[:, :, :]).then_inc(saved, 16)
            act.wait_ge(saved, 16 * (BASE + B))

        @block.vector
        def _(dve):
            for s_ in (rot_step, rotated, lo_made, v_made, s_out, inv_made, scaled, tb_out, sq_made, sqlo_made,
                       res_made, y_out):
                dve.sem_inc(s_, BASE)
            nc.vector.memset(vpad[:, :, :], 0.0).then_inc(vpad_clear, 1)
            dve.wait_ge(vpad_clear, 1)
            with dve.Fori(0, B) as b:
                def rotate(n):
                    x_ = kv[0:96, :] if n == 0 else q[:, :]
                    r_ = rot[0:96, :] if n == 0 else rot[:, :]
                    cos, sin = (a[0:96, :] if n == 0 else a for a in tables["k" if n == 0 else "q"])
                    dve.wait_ge(qk_copied, at(b, KC + 1, n + 1))
                    dve.wait_ge(rotated, at(b, KC + 1, n))
                    dve.sem_inc(dve_passed, 1)
                    nc.vector.stream_shuffle(r_, x_, [(i + HD // 2) % HD for i in range(HD)]).then_inc(rot_step, 1)
                    dve.wait_ge(rot_step, at(b, 3 * (KC + 1), 3 * n + 1))
                    nc.vector.tensor_tensor(x_, x_, cos, ALU.mult).then_inc(rot_step, 1)
                    nc.vector.tensor_tensor(r_, r_, sin, ALU.mult).then_inc(rot_step, 1)
                    dve.wait_ge(rot_step, at(b, 3 * (KC + 1), 3 * n + 3))
                    nc.vector.tensor_tensor(x_, x_, r_, ALU.add).then_inc(rotated, 1)

                def low_part(n):
                    dve.wait_ge(hi_made, at(b, KC + 1, n + 1))
                    dve.wait_ge(rotated, at(b, KC + 1, n + 1))
                    if n == 0:
                        nc.vector.tensor_tensor(ks[HD:2 * HD, :], kv[HD:2 * HD, :], ks[HD:2 * HD, :].bitcast(F32),
                                                ALU.subtract).then_inc(lo_made, 1)
                    else:
                        dve.wait_ge(qs_in[n % 2], stacked(b, n - 2))
                        nc.vector.tensor_tensor(qlo[:, :], q[:, :], qhi[:, :].bitcast(F32), ALU.subtract).then_inc(lo_made, 1)

                def mask_and_min(h, i):
                    k = h * TB + ROWS.index(i)
                    dve.wait_ge(s_done, at(b, NH * TB, k + 1))
                    if i == ROWS[0]:
                        dve.wait_ge(t_done, at(b, 3 * NH, 3 * (h - 1)))
                        dve.wait_ge(exp_done, at(b, NH * TB, TB * (h - 1)))
                        dve.wait_ge(scaled, at(b, NH, h - 1))
                    n = (i + 1) * P
                    dve.sem_inc(dve_passed, 1)
                    nc.vector.tensor_tensor_reduce(out=sc[:, h % 2, SPC[i]:SPC[i] + n], in0=psS[k % 2][:, 0:n],
                                                   in1=mask[:, S - n:S], scale=1.0, scalar=3.0e38, op0=ALU.add,
                                                   op1=ALU.min, accum_out=low[:, h % 2, i:i + 1]).then_inc(s_out, 1)

                def scale(h):
                    dve.wait_ge(exp_done, at(b, NH * TB, TB * (h + 1)))
                    nc.vector.reciprocal(inv[:, h % 2, :], total[:, h % 2, :]).then_inc(inv_made, 1)
                    dve.wait_ge(inv_made, at(b, NH, h + 1))
                    for i in range(TB):
                        cols = sc[:, h % 2, SPC[i]:SPC[i] + (i + 1) * P]
                        last = nc.vector.tensor_scalar(cols, cols, inv[:, h % 2, i:i + 1], None, ALU.mult)
                    last.then_inc(scaled, 1)

                def tb(h):
                    dve.wait_ge(t_done, at(b, 3 * NH, 3 * h + 2))
                    dve.wait_ge(pv_done, at(b, NH, h - 1))
                    nc.vector.tensor_copy(pt[:, h % 2, 512:1024], psT[1][:, :]).then_inc(tb_out, 1)

                def shared(s):
                    dve.wait_ge(relu_made, at(b, NH, s + 1))
                    dve.wait_ge(sqlo_made, at(b, NH, s))
                    nc.vector.tensor_tensor(sq[:, :], relu[:, :], relu[:, :], ALU.mult).then_inc(sq_made, 1)
                    dve.wait_ge(sq_made, at(b, NH, s + 1))
                    dve.wait_ge(sqhi_made, at(b, NH, s + 1))
                    dve.wait_ge(y_step, at(b, NH, s - 1))
                    nc.vector.tensor_tensor(sqlo[:, s % 2, :], sq[:, :], sqhi[:, s % 2, :].bitcast(F32),
                                            ALU.subtract).then_inc(sqlo_made, 1)

                def add_result(k):
                    dve.wait_ge(y_done, at(b, 4, k + 1))
                    if k < 2:
                        dve.wait_ge(res_made, at(b, 1, 1))
                    else:
                        dve.wait_ge(y_out, at(b, 4, k - 1))
                    for i in range(2):
                        r_ = res[:, 2 * (k % 2) + i, :]
                        last = nc.vector.tensor_tensor(r_, psY[i][:, :], r_, ALU.add)
                    last.then_inc(y_out, 1)

                for s in range(NSLOT):
                    h, t = s - LEAD, s - LEAD - 1
                    if s == 0:
                        rotate(0)
                        rotate(1)
                        low_part(0)
                        low_part(1)
                    if s == 1:
                        dve.wait_ge(u_done, at(b, NU, U_AT["vt"] + 1))
                        dve.wait_ge(pv_done, at(b, NH, 0))
                        nc.vector.tensor_copy(vpad[:, :, 3 * HD:4 * HD],
                                              psU[:, :].rearrange("p (t n) -> p t n", n=P)[:, :, 3 * HD:4 * HD]
                                              ).then_inc(v_made, 1)
                    if 0 <= h < NH:
                        for i in ROWS:
                            mask_and_min(h, i)
                    if 0 <= t < NH:
                        tb(t)
                    if s < NH:
                        shared(s)
                    if 0 < s < NH and s % HC == 0:
                        rotate(s // HC + 1)
                    if 0 <= h < NH:
                        scale(h)
                    if 0 < s < NH and s % HC == 0:
                        low_part(s // HC + 1)
                    if s == 4:
                        dve.wait_ge(res_in, b * 16 + 16)
                        dve.wait_ge(bp_in, 16)
                        nc.vector.tensor_tensor(res[:, :, :], res[:, :, :], bp[:, :].unsqueeze(1).broadcast_to([P, TB, D]),
                                                ALU.add).then_inc(res_made, 1)
                    if s in (8, 16):
                        add_result(s // 8 - 1)
                add_result(2)
                add_result(3)

        @block.tensor
        def _(pe):
            for s_ in (u_done, s_done, t_done, pv_done, y_step, y_done, x_used):
                pe.sem_inc(s_, BASE)
            pe.wait_ge(vpad_clear, 1)
            with pe.Fori(0, B) as b:
                def bank_free(name):
                    k = U_AT[name]
                    last, back = (U_ORDER[k - 1], 0) if k else (U_ORDER[-1], 1)
                    if last.startswith("up"):
                        pe.wait_ge(relu_made, at(b, NH, int(last[2:]) + 1 - back * NH))
                    elif last == "vt":
                        pe.wait_ge(v_made, at(b, 1, 1 - back))
                    else:
                        n = 0 if last == "kv" else int(last[1:]) + 1
                        pe.wait_ge(qk_copied, at(b, KC + 1, n + 1 - back * (KC + 1)))

                def project(name, whi, wlo):
                    bank_free(name)
                    for c in range(KC):
                        mm = three(pe, psU[:, :], (whi[:, c, :], wlo[:, c, :]), (xh[:, c, :], xlo[:, c, :]),
                                   c == 0, c == KC - 1)
                    mm.then_inc(u_done, 1)

                def queries(n):
                    cols = slice(n * P, (n + 1) * P)
                    project(f"q{n}", wq_hi[:, :, cols], wq_lo[:, :, cols])

                def up(s):
                    tok = slice(s // 8 * SHALF, (s // 8 + 1) * SHALF)
                    cols = slice(s % 8 * P, (s % 8 + 1) * P)
                    bank_free(f"up{s}")
                    for c in range(KC):
                        mm = three(pe, psU[:, 0:SHALF], (up_hi[:, c, cols], up_lo[:, c, cols]),
                                   (xh[:, c, tok], xlo[:, c, tok]), c == 0, c == KC - 1)
                    mm.then_inc(u_done, 1)

                def down(s):
                    pe.wait_ge(sqhi_made, at(b, NH, s + 1))
                    pe.wait_ge(sqlo_made, at(b, NH, s + 1))
                    if s % 8 == 0:
                        pe.wait_ge(y_out, at(b, 4, s // 8))
                    for i in range(2):
                        tok = slice(i * P, (i + 1) * P)
                        mm = three(pe, psY[i][:, :], (sqhi[:, s % 2, tok], sqlo[:, s % 2, tok]),
                                   (down_hi[:, s % 8, :], down_lo[:, s % 8, :]), s % 8 == 0, s % 8 == 7)
                    mm.then_inc(y_step, 1)
                    if s % 8 == 7:
                        pe.wait_ge(y_step, at(b, NH, s + 1))
                        pe.sem_inc(y_done, 1)

                def scores(h, i):
                    k = h * TB + ROWS.index(i)
                    c = h // HC
                    if i == ROWS[0]:
                        pe.wait_ge(qs_in[c % 2], stacked(b, c))
                        if h == 0:
                            pe.wait_ge(lo_made, at(b, KC + 1, 1))
                            pe.wait_ge(hi_made, at(b, KC + 1, 1))
                    pe.wait_ge(s_out, at(b, NH * TB, k - 1))
                    n = max((i + 1) * P, 2 * P)
                    pe.matmul(psS[k % 2][:, 0:n], qs[:, c % 2, h % HC, i * P:(i + 1) * P], ks[:, 0:n],
                              start=True, stop=True).then_inc(s_done, 1)

                def transposes(h, g):
                    if g == 0:
                        pe.wait_ge(scaled, at(b, NH, h + 1))
                        pe.wait_ge(ta_out, at(b, 2 * NH, 2 * h))
                        todo = [(0, 0, i) for i in range(4)]
                    elif g == 1:
                        pe.wait_ge(tb_out, at(b, NH, h))
                        todo = [(1, 1, i) for i in range(1, 4)] + [(1, 3, 3)]
                    else:
                        pe.wait_ge(ta_out, at(b, 2 * NH, 2 * h + 1))
                        todo = [(0, 2, i) for i in range(2, 4)]
                    for bank, j, i in todo:
                        first, query = PTC[j]
                        to = (first + i * P - query) % 512
                        mm = pe.transpose(psT[bank][:, to:to + P], sc[:, h % 2, SPC[i] + j * P:SPC[i] + (j + 1) * P], ident)
                    mm.then_inc(t_done, 1)

                def values(h):
                    if h % HC == 0:
                        pe.wait_ge(o_out, at(b, KC, h // HC))
                    if h == 0:
                        pe.wait_ge(v_made, at(b, 1, 1))
                    for j in (0, 1, 3, 2):
                        if j == 0:
                            pe.wait_ge(ta_out, at(b, 2 * NH, 2 * h + 1))
                        elif j == 1:
                            pe.wait_ge(tb_out, at(b, NH, h + 1))
                        elif j == 2:
                            pe.wait_ge(ta_out, at(b, 2 * NH, 2 * h + 2))
                        first, query = PTC[j]
                        place = (HC - 1 - h % HC) * HD
                        mm = pe.matmul(psO[:, query:S], vpad[:, j, place:place + P],
                                       pt[:, h % 2, first:first + S - query],
                                       start=(h % HC == 0 and j == 0), stop=(h % HC == HC - 1 and j == 2))
                    mm.then_inc(pv_done, 1)

                for s in range(NSLOT):
                    h, t = s - LEAD, s - LEAD - 1
                    if s == 0:
                        pe.wait_ge(xh_in, b * 16 + 16)
                        pe.wait_ge(xlo_in, b * 16 + 16)
                        project("kv", wkv_hi, wkv_lo)
                        queries(0)
                    if 0 <= h < NH:
                        scores(h, ROWS[0])
                        scores(h, ROWS[1])
                    if 1 <= s <= NH:
                        down(s - 1)
                    if 0 <= h < NH:
                        scores(h, ROWS[2])
                        scores(h, ROWS[3])
                    if 0 <= t < NH:
                        transposes(t, 0)
                        transposes(t, 1)
                    if s < NH:
                        up(s)
                    if 0 <= t < NH:
                        transposes(t, 2)
                        values(t)
                    if s == NH - 1:
                        pe.wait_ge(u_done, at(b, NU, NU))
                        pe.sem_inc(x_used, 1)
                    if s == 1:
                        bank_free("vt")
                        pe.wait_ge(rotated, at(b, KC + 1, 1))
                        for i in range(TB):
                            mm = pe.transpose(psU[:, i * P:(i + 1) * P], kv[:, i * P:(i + 1) * P], ident)
                        mm.then_inc(u_done, 1)
                    if 0 < s < NH and s % HC == 0:
                        queries(s // HC)
                pe.wait_ge(o_out, at(b, KC, KC))
                for k in range(2):
                    pe.wait_ge(y_out, at(b, 4, k + 2))
                    for i in range(2):
                        tile_ = 2 * k + i
                        for c in range(KC):
                            mm = pe.matmul(psY[i][:, :], ot[:, c, tile_ * P:(tile_ + 1) * P],
                                           wproj[:, c, :], start=(c == 0), stop=(c == KC - 1))
                    mm.then_inc(y_done, 1)

NR = 8
NY = 4


def experts(nc, w1, w2, cst, experts_dram, xs, sums):
    with ExitStack() as ctx:
        def sb(name, shape, dt=F32):
            return ctx.enter_context(nc.sbuf_tensor(name, shape, dt))

        def sem(name):
            return ctx.enter_context(nc.semaphore(name))

        def pb(name):
            return ctx.enter_context(nc.psum_tensor(name, [P, S], F32))

        ident = cst[:, COL["ident"]]
        W = LC * INTER
        w1_sb = sb("e_w1", [P, E * W])
        w2_sb = sb("e_w2", [P, E * W])
        table = sb("e_table", [1, 3 * P], I32)
        row = [sb(f"e_row{u}", [P, ROW]) for u in range(NR)]
        xt = [sb(f"e_xt{u}", [P, LAT]) for u in range(2)]
        relu = [sb(f"e_relu{u}", [P, INTER]) for u in range(2)]
        ht = [sb(f"e_ht{u}", [P, INTER]) for u in range(2)]
        y = [sb(f"e_y{u}", [P, LAT]) for u in range(NY)]
        psX, psH, psT, psY = ([pb(f"e_ps{n}{u}") for u in range(2)] for n in "XHTY")
        w_in = [sem("e_w1_in"), sem("e_w2_in")]
        table_in = sem("e_table_in")
        passed = sem("e_passed")
        row_in = [sem(f"e_row_in{u}") for u in range(NR)]
        x_turned, h_done, h_turned, y_done = sem("e_x_turned"), sem("e_h_done"), sem("e_h_turned"), sem("e_y_done")
        xt_made, ht_made, relu_made, y_made = sem("e_xt_made"), sem("e_ht_made"), sem("e_relu_made"), sem("e_y_made")
        added = [sem(f"e_added{u}") for u in range(2)]
        block = ctx.enter_context(nc.Block())

        def program(eng, stages):
            for s in range(NR):
                for lag, step in stages:
                    if s >= lag:
                        step(0, s - lag)
            with eng.Fori(1, SLOT_TILES // NR) as i:
                for s in range(NR):
                    for lag, step in stages:
                        step(i, s - lag)
            for s in range(max(lag for lag, _ in stages)):
                for lag, step in stages:
                    if s < lag:
                        step(SLOT_TILES // NR, s - lag)

        def num(i, u, n=0):
            return i * NR + (BASE + u + n)

        def sums_done(i, u):
            return i * (16 * NR // 2) + 16 * (u // 2 + 1)

        def first(i, u, n):
            return isinstance(i, int) and i * NR + u < n

        @block.sync
        def _(sp):
            sp.dma_start(table[:, :], experts_dram.rearrange("(a n) -> a n", a=1)).then_inc(table_in, 16)

            def load(i, u):
                if not first(i, u, NR):
                    sp.wait_ge(added[u % 2], sums_done(i, u - NR))
                sp.dma_start(row[u][:, :], xs[bass.ds(i * NR * P + u * P, P), :]).then_inc(row_in[u], 16)

            for u in range(NR):
                load(0, u)
            for k in range(4):
                cols = slice(k * E * W // 4, (k + 1) * E * W // 4)
                sp.dma_start(w1_sb[:, cols], w1[:, cols]).then_inc(w_in[0], 16)
            with sp.Fori(1, SLOT_TILES // NR) as i:
                for u in range(NR):
                    load(i, u)

        @block.scalar
        def _(act):
            for s_ in (xt_made, ht_made):
                act.sem_inc(s_, BASE)
            for k in range(4):
                cols = slice(k * E * W // 4, (k + 1) * E * W // 4)
                act.dma_start(w2_sb[:, cols], w2[:, cols]).then_inc(w_in[1], 16)

            def turned_x(i, u):
                act.wait_ge(x_turned, num(i, u, 1))
                act.wait_ge(h_done, num(i, u, -1))
                nc.scalar.activation(xt[u % 2][:, :], psX[u % 2][:, 0:LAT], ACT.Copy).then_inc(xt_made, 1)

            def turned_h(i, u):
                act.wait_ge(h_turned, num(i, u, 1))
                act.wait_ge(y_done, num(i, u, -1))
                nc.scalar.activation(ht[u % 2][:, :], psT[u % 2][:, 0:INTER], ACT.Square).then_inc(ht_made, 1)

            program(act, ((0, turned_x), (2, turned_h)))

        @block.vector
        def _(dve):
            for s_ in (relu_made, y_made):
                dve.sem_inc(s_, BASE)
            dve.wait_ge(table_in, 16)

            def rectify(i, u):
                dve.wait_ge(h_done, num(i, u, 1))
                dve.wait_ge(h_turned, num(i, u, -1))
                nc.vector.tensor_scalar(relu[u % 2][:, :], psH[u % 2][:, 0:INTER], 0.0, None, ALU.max).then_inc(relu_made, 1)

            def weigh(i, u):
                e = dve.value_load(table[0:1, bass.ds(i * NR + u, 1)], min_val=0, max_val=E - 1)
                dve.wait_ge(y_done, num(i, u, 1))
                if not first(i, u, NY):
                    dve.wait_ge(added[u % 2], sums_done(i, u - NY))
                nc.vector.tensor_scalar(y[u % NY][:, :], psY[u % 2][:, 0:LAT], row[u % NR][:, bass.ds(e + LAT, 1)], None,
                                        ALU.mult).then_inc(y_made, 1)

            program(dve, ((1, rectify), (3, weigh)))

        @block.gpsimd
        def _(pool):
            def add(i, u):
                pool.wait_ge(y_made, num(i, u, 1))
                if not first(i, u, 2):
                    pool.wait_ge(added[u % 2], sums_done(i, u - 2))
                pool.sem_inc(passed, 1)
                pool.indirect_dma_start(out=sums[u % 2],
                                        out_offset=bass.IndirectOffsetOnAxis(ap=row[u % NR][:, ROW - 1:ROW].bitcast(U32), axis=0),
                                        in_=y[u % NY][:, :], in_offset=None, compute_op=ALU.add).then_inc(added[u % 2], 16)

            program(pool, ((0, add),))
            for u in range(2):
                pool.wait_ge(added[u], 16 * SLOT_TILES // 2)

        @block.tensor
        def _(pe):
            for s_ in (x_turned, h_done, h_turned, y_done):
                pe.sem_inc(s_, BASE)
            pe.wait_ge(table_in, 16)

            def turn_x(i, u):
                pe.wait_ge(row_in[u % NR], i * 16 + (16 if u >= 0 else 0))
                pe.wait_ge(xt_made, num(i, u, -1))
                for c in range(LC):
                    mm = pe.transpose(psX[u % 2][:, c * P:(c + 1) * P], row[u % NR][:, c * P:(c + 1) * P], ident)
                mm.then_inc(x_turned, 1)

            def product(i, u, w, out, lhs, out_free, lhs_made, done):
                e = pe.value_load(table[0:1, bass.ds(i * NR + u, 1)], min_val=0, max_val=E - 1)
                pe.wait_ge(lhs_made, num(i, u, 1))
                pe.wait_ge(out_free, num(i, u, -1))
                for c in range(LC):
                    mm = pe.matmul(out[u % 2][:, 0:INTER], lhs[u % 2][:, c * P:(c + 1) * P],
                                   w[:, bass.ds(e * W + c * INTER, INTER)], start=(c == 0), stop=(c == LC - 1))
                mm.then_inc(done, 1)

            def hidden(i, u):
                if first(i, u, 1):
                    pe.wait_ge(w_in[0], 64)
                product(i, u, w1_sb, psH, xt, relu_made, xt_made, h_done)

            def turn_h(i, u):
                pe.wait_ge(relu_made, num(i, u, 1))
                pe.wait_ge(ht_made, num(i, u, -1))
                for c in range(IC):
                    mm = pe.transpose(psT[u % 2][:, c * P:(c + 1) * P], relu[u % 2][:, c * P:(c + 1) * P], ident)
                mm.then_inc(h_turned, 1)

            def result(i, u):
                if first(i, u, 1):
                    pe.wait_ge(w_in[1], 64)
                product(i, u, w2_sb, psY, ht, y_made, ht_made, y_done)

            program(pe, ((0, turn_x), (1, hidden), (2, turn_h), (3, result)))


def combine(nc, fc2, cst, sums, partial, out):
    R = 4
    with ExitStack() as ctx:
        def sb(name, shape, dt=F32):
            return ctx.enter_context(nc.sbuf_tensor(name, shape, dt))

        def sem(name):
            return ctx.enter_context(nc.semaphore(name))

        ident = cst[:, COL["ident"]]
        w = sb("c_w", [P, LC, D])
        a, z = ([sb(f"c_{n}{u}", [P, LAT]) for u in range(R)] for n in "az")
        y = [sb(f"c_y{u}", [P, LAT]) for u in range(2)]
        yt = [sb(f"c_yt{u}", [P, LAT]) for u in range(2)]
        part = [sb(f"c_part{u}", [P, D]) for u in range(R)]
        psT, psO = ([ctx.enter_context(nc.psum_tensor(f"c_ps{n}{u}", [P, S], F32)) for u in range(2)] for n in "TO")
        w_in = sem("c_w_in")
        sums_in, part_in, saved = ([sem(f"c_{n}{u}") for u in range(R)] for n in ("sums_in", "part_in", "saved"))
        y_made, turned, yt_made, done, added = (sem(f"c_{n}") for n in ("y_made", "turned", "yt_made", "done", "added"))
        block = ctx.enter_context(nc.Block())

        @block.sync
        def _(sp):
            sp.dma_start(w[:, :, :].rearrange("p c n -> p (c n)"), fc2).then_inc(w_in, 16)
            for s_ in saved:
                sp.sem_inc(s_, 16 * BASE)
            with sp.Fori(0, G // R) as i:
                for u in range(R):
                    rows = bass.ds(i * R * P + u * P, P)
                    sp.wait_ge(y_made, at(i, R, u + 1 - R))
                    sp.dma_start(a[u][:, :], sums[0][rows, :]).then_inc(sums_in[u], 16)
                    sp.dma_start(z[u][:, :], sums[1][rows, :]).then_inc(sums_in[u], 16)
                    sp.wait_ge(saved[u], i * 16 + 16 * BASE)
                    sp.dma_start(part[u][:, :], partial[rows, :]).then_inc(part_in[u], 16)

        @block.scalar
        def _(act):
            act.sem_inc(yt_made, BASE)
            with act.Fori(0, G // R) as i:
                for u in range(R):
                    act.wait_ge(turned, at(i, R, u + 1))
                    act.wait_ge(done, at(i, R, u - 1))
                    nc.scalar.activation(yt[u % 2][:, :], psT[u % 2][:, 0:LAT], ACT.Copy).then_inc(yt_made, 1)
                    act.wait_ge(added, at(i, R, u + 1))
                    act.dma_start(out[bass.ds(i * R * P + u * P, P), :], part[u][:, :]).then_inc(saved[u], 16)
            for u in range(R):
                act.wait_ge(saved[u], 16 * (BASE + G // R))

        @block.vector
        def _(dve):
            dve.sem_inc(y_made, BASE)
            dve.sem_inc(added, BASE)
            with dve.Fori(0, G // R) as i:
                for u in range(R):
                    dve.wait_ge(sums_in[u], i * 32 + 32)
                    dve.wait_ge(turned, at(i, R, u - 1))
                    nc.vector.tensor_tensor(y[u % 2][:, :], a[u][:, :], z[u][:, :], ALU.add).then_inc(y_made, 1)
                    dve.wait_ge(done, at(i, R, u + 1))
                    dve.wait_ge(part_in[u], i * 16 + 16)
                    nc.vector.tensor_tensor(part[u][:, :], psO[u % 2][:, :], part[u][:, :], ALU.add).then_inc(added, 1)

        @block.tensor
        def _(pe):
            pe.sem_inc(turned, BASE)
            pe.sem_inc(done, BASE)
            pe.wait_ge(w_in, 16)
            with pe.Fori(0, G // R) as i:
                for u in range(R):
                    pe.wait_ge(y_made, at(i, R, u + 1))
                    pe.wait_ge(yt_made, at(i, R, u - 1))
                    for c in range(LC):
                        mm = pe.transpose(psT[u % 2][:, c * P:(c + 1) * P], y[u % 2][:, c * P:(c + 1) * P], ident)
                    mm.then_inc(turned, 1)
                    pe.wait_ge(yt_made, at(i, R, u + 1))
                    pe.wait_ge(added, at(i, R, u - 1))
                    for c in range(LC):
                        mm = pe.matmul(psO[u % 2][:, :], yt[u % 2][:, c * P:(c + 1) * P], w[:, c, :],
                                       start=(c == 0), stop=(c == LC - 1))
                    mm.then_inc(done, 1)

def constant_table():
    c = np.zeros((P, NCONST), np.float32)
    p = np.arange(P)
    c[:, COL["ident"]] = np.eye(P)
    c[:, COL["tri"]] = np.triu(np.ones((P, P)), 1)
    col = np.arange(S)[None] - (S - P)
    c[:, COL["mask"]] = np.where(col > p[:, None], np.float32(1e38), 0)
    f = np.float32
    inv_freq = f(1) / f(10000) ** (np.arange(0, HD, 2, dtype=f) / f(HD))
    t = np.arange(S, dtype=f)
    freqs = (t[:, None] * inv_freq[None]).astype(f)
    base = ((np.arange(0, HD, 2, dtype=f) + f(0.4 * HD)) / f(1.4 * HD)).astype(f)
    xs = (base[None] ** ((t - S // 2) / f(128))[:, None]).astype(f)
    d = p % HD
    cos, sin, xs = (np.asarray(a[:, d % (HD // 2)].T, np.float64) for a in (np.cos(freqs.astype(np.float64)), np.sin(freqs.astype(np.float64)), xs))
    sign = np.where(d < HD // 2, -1.0, 1.0)[:, None]
    w = float(f(HD ** -0.5))
    c[:, COL["cosq"]], c[:, COL["sinq"]] = -w * cos * xs, -w * sign * sin * xs
    c[:, COL["cosk"]], c[:, COL["sink"]] = w * cos / xs, w * sign * sin / xs
    c[:, COL["token"]] = np.arange(G)[None] * P + p[:, None]
    c[:, COL["earlier"]] = np.tril(np.ones((NG, NG)), -1).reshape(1, -1)
    c[:, COL["tile"]] = np.arange(3)[None] + 3 * p[:, None]
    c[:, COL["lane"]] = p[:, None]
    c[:, COL["spare"]] = T + p[:, None]
    return c


def build(nc, x, w_fc1_gate, gate_bias, wq, wkv, wproj, bproj, wup, wdown, w1, w2, wfc2, consts, out):
    xnt_hi = nc.dram_tensor("xnt_hi", (B, P, KC, S), F32, kind="Internal").ap()
    xnt_lo = nc.dram_tensor("xnt_lo", (B, P, KC, S), F32, kind="Internal").ap()
    xlat = nc.dram_tensor("xlat", (T, LAT), F32, kind="Internal").ap()
    slot_rows = nc.dram_tensor("slot_rows", (SLOTS, ROW), F32, kind="Internal").ap()
    experts_dram = nc.dram_tensor("tile_experts", (3 * P,), I32, kind="Internal").ap()
    sums = [nc.dram_tensor(f"sums{u}", (T + SPARE, LAT), F32, kind="Internal").ap() for u in range(2)]
    partial = nc.dram_tensor("partial", (T, D), F32, kind="Internal").ap()
    with ExitStack() as ctx:
        cst = ctx.enter_context(nc.sbuf_tensor("cst", [P, NCONST], F32))
        with ExitStack() as inner:
            def sb(name, shape, dt=F32):
                return inner.enter_context(nc.sbuf_tensor(name, shape, dt))

            weights_sb = sb("weights", [P, G, E])
            slots_sb = sb("slots", [P, G, TOPK], U32)
            pads_sb = sb("pads", [P, E], U32)
            with nc.semaphore("cst_in") as cst_in, nc.Block() as block:
                @block.sync
                def _(sp):
                    sp.dma_start(cst[:, :], consts).then_inc(cst_in, 16)
                    sp.wait_ge(cst_in, 16)
            front(nc, x, w_fc1_gate, gate_bias, xnt_hi, xnt_lo, xlat, cst, weights_sb, slots_sb, pads_sb, experts_dram, sums)
            halves = {n: tuple(sb(f"{n}_{h}", [P, w.shape[1]], F32R) for h in ("hi", "lo"))
                      for n, w in (("wq", wq), ("wkv", wkv), ("wup", wup), ("wdown", wdown))}
            halves = {n: tuple(a[:, :] for a in pair) for n, pair in halves.items()}
            proj = sb("proj", [P, KC, D])
            with nc.semaphore("proj_in") as proj_in, nc.Block() as block:
                @block.sync
                def _(sp):
                    sp.dma_start(proj[:, :, :].rearrange("p c n -> p (c n)"), wproj).then_inc(proj_in, 16)
                    sp.wait_ge(proj_in, 16)
            split_weights(nc, [(w, *halves[n]) for n, w in (("wkv", wkv), ("wq", wq), ("wup", wup), ("wdown", wdown))])
            middle(nc, x, bproj, xnt_hi, xnt_lo, xlat, halves["wq"], halves["wkv"], proj, halves["wup"], halves["wdown"],
                   cst, weights_sb, slots_sb, pads_sb, slot_rows, partial)
        experts(nc, w1, w2, cst, experts_dram, slot_rows, sums)
        combine(nc, wfc2, cst, sums, partial, out)


def columns(w, chunks):
    return np.ascontiguousarray(w.reshape(chunks, P, -1).transpose(1, 0, 2).reshape(P, -1))


def per_expert(w):
    w = w.transpose(0, 2, 1).reshape(E, LC, P, -1)
    return np.ascontiguousarray(w.transpose(2, 0, 1, 3).reshape(P, -1))


def kernel(L0_attn_hidden_states, L0_attn_w_q, L0_attn_w_kv, L0_attn_w_proj, L0_attn_b_proj, L0_ffn_gate_w,
           L0_ffn_gate_bias, L0_ffn_fc1_w, L0_ffn_fc2_w, L0_ffn_w1, L0_ffn_w2, L0_ffn_shared_up_w,
           L0_ffn_shared_down_w):
    import concourse.bacc as bacc
    from concourse.bass_utils import run_bass_kernel_spmd

    def a(v):
        return np.asarray(v)

    kv = a(L0_attn_w_kv)
    arrays = {
        "x": np.ascontiguousarray(a(L0_attn_hidden_states).reshape(T, D)),
        "w_fc1_gate": columns(np.concatenate([a(L0_ffn_fc1_w).T, a(L0_ffn_gate_w).T], 1), KC).reshape(P, KC, FG),
        "gate_bias": a(L0_ffn_gate_bias),
        "wq": columns(a(L0_attn_w_q).T, KC),
        "wkv": columns(np.concatenate([kv[:HD], kv[:HD], kv[:HD], kv[HD:]], 0).T, KC),
        "wproj": columns(a(L0_attn_w_proj).T, KC),
        "bproj": a(L0_attn_b_proj),
        "wup": columns(a(L0_ffn_shared_up_w).T, KC),
        "wdown": columns(a(L0_ffn_shared_down_w).T, SC),
        "w1": per_expert(a(L0_ffn_w1)),
        "w2": per_expert(a(L0_ffn_w2)),
        "wfc2": columns(a(L0_ffn_fc2_w).T, LC),
        "consts": constant_table(),
    }
    nc = bacc.Bacc("TRN2", target_bir_lowering=False, num_devices=1)
    aps = [nc.dram_tensor(f"in_{n}", v.shape, F32, kind="ExternalInput").ap() for n, v in arrays.items()]
    out = nc.dram_tensor("out", (T, D), F32, kind="ExternalOutput").ap()
    build(nc, *aps, out)
    r = run_bass_kernel_spmd(nc, [{f"in_{n}": v for n, v in arrays.items()}], core_ids=[0])
    return r.results[0]["out"].reshape(B, S, D)
```

```python
import numpy as np
import concourse.bass as bass
from concourse import mybir
from contextlib import ExitStack

F32 = mybir.dt.float32
F32R = mybir.dt.float32r
U32 = mybir.dt.uint32
I32 = mybir.dt.int32
ALU = mybir.AluOpType
ACT = mybir.ActivationFunctionType
AX = mybir.AxisListType

P = 128
B, S, D = 8, 512, 512
T = B * S
TB = S // P
G = T // P
KC = D // P
NH, HD = 16, 32
LAT, INTER, E = 256, 256, 32
NG, GE = 4, 8
TOPG, TOPK = 2, 8
SH = 1024
LC, IC, SC = LAT // P, INTER // P, SH // P
ROUTED_SCALE = 2.5
EPS = 1e-5
FG = LAT + E
FULL_TILES = T * TOPK // P
SLOT_TILES = FULL_TILES + E
SLOTS = SLOT_TILES * P
ROW = LAT + E + 1
SPARE = P
BIG = 3.0e38
BASE = 16

WIDTHS = dict(ident=P, tri=P, mask=S, cosq=S, sinq=S, cosk=S, sink=S, token=G, earlier=NG * NG, tile=3, lane=1, spare=1)
COL, _at = {}, 0
for _n, _w in WIDTHS.items():
    COL[_n] = slice(_at, _at + _w)
    _at += _w
NCONST = _at


def at(i, per, n):
    return i * per + (BASE + n)


def three(pe, out, lhs, rhs, first, last):
    (lh, ll), (rh, rl) = lhs, rhs
    pe.matmul(out, ll, rh, start=first, stop=False)
    pe.matmul(out, lh, rl, start=False, stop=False)
    return pe.matmul(out, lh, rh, start=False, stop=last)


def front(nc, x, fc1g, bias, xnt_hi, xnt_lo, xlat, cst, weights_sb, slots_sb, pads_sb, experts_dram, sums):
    with ExitStack() as ctx:
        def sb(name, shape, dt=F32):
            return ctx.enter_context(nc.sbuf_tensor(name, shape, dt))

        def sem(name):
            return ctx.enter_context(nc.semaphore(name))

        zero = sb("f_zero", [P, LAT])
        ident = cst[:, COL["ident"]]
        wst = sb("f_wst", [P, KC, FG])
        whi = sb("f_whi", [P, KC, FG], F32R)
        wlo = sb("f_wlo", [P, KC, FG], F32R)
        bia = sb("f_bias", [P, E])
        xt = sb("f_xt", [P, TB, D])
        xn = sb("f_xn", [P, TB, D])
        hi = sb("f_hi", [P, KC, S], F32R)
        lo = sb("f_lo", [P, KC, S], F32R)
        xl = sb("f_xl", [P, TB, FG])
        stats = sb("f_stats", [P, TB, 6])
        mv = sb("f_mv", [P, TB, 2])
        veps = sb("f_veps", [P, TB])
        half = sb("f_half", [P, TB])
        tmp = sb("f_tmp", [P, TB])
        rstd = sb("f_rstd", [P, TB])
        logits = sb("f_logits", [P, G, E])
        score = sb("f_score", [P, G, E])
        biased = sb("f_biased", [P, G, E])
        equal = sb("f_equal", [P, G, E])
        other = sb("f_other", [P, G, E])
        picked = sb("f_picked", [P, G, E])
        first_g = sb("f_first", [P, G, NG])
        second_g = sb("f_second", [P, G, NG])
        twice_g = sb("f_twice", [P, G, NG])
        beats = sb("f_beats", [P, G, NG, NG])
        ties = sb("f_ties", [P, G, NG, NG])
        top8 = sb("f_top8", [P, G, TOPK])
        token_sum = sb("f_token_sum", [P, G])
        ones = sb("f_ones", [P, P])
        before = [sb(f"f_before{i}", [P, G, E]) for i in range(2)]
        count = sb("f_count", [P, E])
        count_i = sb("f_count_i", [P, E], I32)
        tiles = [sb(f"f_tiles{i}", [P, E]) for i in range(2)]
        start = sb("f_start", [P, E])
        end = sb("f_end", [P, E])
        pad = [sb(f"f_pad{i}", [P, E]) for i in range(2)]
        owner = sb("f_owner", [P, 3, E])
        expert_f = sb("f_expert_f", [P, 3])
        expert_i = sb("f_expert_i", [P, 3], I32)
        pt = [ctx.enter_context(nc.psum_tensor(f"f_pt{c}", [P, S], F32)) for c in range(KC)]
        pf = [ctx.enter_context(nc.psum_tensor(f"f_pf{i}", [P, S], F32)) for i in range(TB)]

        passed = sem("f_passed")
        w_in, b_in = sem("f_w_in"), sem("f_b_in")
        x_in = [sem(f"f_x_in{i}") for i in range(TB)]
        chain = sem("f_dve_chain")
        whi_made, wlo_made = sem("f_whi_made"), sem("f_wlo_made")
        veps_made, half_made = sem("f_veps_made"), sem("f_half_made")
        xn_made, xnt_done = sem("f_xn_made"), sem("f_xnt_done")
        hi_made, lo_made = sem("f_hi_made"), sem("f_lo_made")
        fc_done, xl_made, lg_made = sem("f_fc_done"), sem("f_xl_made"), sem("f_lg_made")
        xnt_saved, xl_saved = sem("f_xnt_saved"), sem("f_xl_saved")
        exp_made, picked_made, counted = sem("f_exp_made"), sem("f_picked_made"), sem("f_counted")
        copied = sem("f_copied")
        zero_made, zeroed = sem("f_zero_made"), sem("f_zeroed")
        ones_made, expert_made, expert_saved = sem("f_ones_made"), sem("f_expert_made"), sem("f_expert_saved")
        block = ctx.enter_context(nc.Block())

        @block.sync
        def _(sp):
            sp.dma_start(wst[:, :, :], fc1g).then_inc(w_in, 16)
            sp.dma_start(bia[:, :], bias.partition_broadcast(P)).then_inc(b_in, 16)
            with sp.Fori(0, B) as b:
                for i in range(TB):
                    sp.wait_ge(xn_made, at(b, TB, i + 1 - TB))
                    sp.dma_start(xt[:, i, :], x[bass.ds(b * S + i * P, P), :]).then_inc(x_in[i], 16)
            sp.wait_ge(xnt_saved, 16 * (BASE + 2 * B))
            sp.dma_start(xnt_hi[B], xnt_hi[0]).then_inc(copied, 16)
            sp.dma_start(xnt_lo[B], xnt_lo[0]).then_inc(copied, 16)
            sp.wait_ge(copied, 32)
            sp.wait_ge(expert_made, 1)
            sp.dma_start(experts_dram.rearrange("(p q) -> p q", p=P), expert_i[:, :]).then_inc(expert_saved, 16)
            sp.wait_ge(expert_saved, 16)

        @block.gpsimd
        def _(pool):
            nc.gpsimd.memset(zero[:, :], 0.0).then_inc(zero_made, 1)
            pool.wait_ge(zero_made, 1)
            for a in sums:
                pool.dma_start(a.rearrange("(g p) l -> p g l", p=P),
                               zero[:, :].unsqueeze(1).broadcast_to([P, G + 1, LAT])).then_inc(zeroed, 16)
            pool.wait_ge(zeroed, 16 * len(sums))

        @block.scalar
        def _(act):
            act.sem_inc(hi_made, BASE)
            act.sem_inc(xnt_saved, 16 * BASE)
            act.sem_inc(xl_saved, 16 * BASE)
            act.sem_inc(half_made, BASE)
            act.sem_inc(xl_made, BASE)
            act.wait_ge(w_in, 16)
            nc.scalar.activation(whi[:, :, :], wst[:, :, :], ACT.Copy).then_inc(whi_made, 1)
            with act.Fori(0, B) as b:
                act.wait_ge(veps_made, at(b, 1, 1))
                nc.scalar.activation(half[:, :], veps[:, :], ACT.Sqrt, scale=0.25).then_inc(half_made, 1)
                act.wait_ge(xnt_done, at(b, TB, TB))
                act.wait_ge(xnt_saved, b * 32 + 16 * BASE)
                act.wait_ge(fc_done, at(b, TB, 0))
                for c in range(KC):
                    nc.scalar.activation(hi[:, c, :], pt[c][:, :], ACT.Copy).then_inc(hi_made, 1)
                act.wait_ge(xl_saved, b * 16 + 16 * BASE)
                act.wait_ge(lg_made, at(b, TB, 0))
                for i in range(TB):
                    act.wait_ge(fc_done, at(b, TB, i + 1))
                    nc.scalar.activation(xl[:, i, :], pf[i][:, 0:FG], ACT.Copy).then_inc(xl_made, 1)
                act.wait_ge(lo_made, at(b, KC, KC))
                act.dma_start(xnt_hi[bass.ds(b, 1)].rearrange("a p c s -> (a p) c s"),
                              hi[:, :, :].bitcast(F32)).then_inc(xnt_saved, 16)
                act.dma_start(xnt_lo[bass.ds(b, 1)].rearrange("a p c s -> (a p) c s"),
                              lo[:, :, :].bitcast(F32)).then_inc(xnt_saved, 16)
                act.wait_ge(xl_made, at(b, TB, TB))
                act.dma_start(xlat[bass.ds(b * S, S), :].rearrange("(i p) l -> p i l", p=P),
                              xl[:, :, 0:LAT]).then_inc(xl_saved, 16)
            act.wait_ge(lg_made, at(B, TB, 0))
            nc.scalar.activation(score[:, :, :], logits[:, :, :], ACT.Exp, scale=-1.0).then_inc(exp_made, 1)
            act.wait_ge(xnt_saved, 16 * (BASE + 2 * B))
            act.wait_ge(xl_saved, 16 * (BASE + B))

        @block.tensor
        def _(pe):
            pe.sem_inc(xnt_done, BASE)
            pe.sem_inc(fc_done, BASE)
            pe.wait_ge(wlo_made, 1)
            with pe.Fori(0, B) as b:
                pe.wait_ge(lo_made, at(b, KC, 0))
                for i in range(TB):
                    pe.wait_ge(xn_made, at(b, TB, i + 1))
                    for c in range(KC):
                        mm = pe.transpose(pt[c][:, i * P:(i + 1) * P], xn[:, i, c * P:(c + 1) * P], ident)
                    mm.then_inc(xnt_done, 1)
                pe.wait_ge(lo_made, at(b, KC, KC))
                for i in range(TB):
                    pe.wait_ge(xl_made, at(b, TB, i + 1 - TB))
                    for c in range(KC):
                        tok = slice(i * P, (i + 1) * P)
                        mm = three(pe, pf[i][:, 0:FG], (hi[:, c, tok], lo[:, c, tok]), (whi[:, c, :], wlo[:, c, :]),
                                   c == 0, c == KC - 1)
                    mm.then_inc(fc_done, 1)

            pe.wait_ge(picked_made, 1)
            pe.wait_ge(ones_made, 1)
            pe.wait_ge(lo_made, at(B, KC, 0))
            for h in range(2):
                half_g = slice(h * G // 2, (h + 1) * G // 2)
                pe.matmul(pt[h][:, :], cst[:, COL["tri"]], picked[:, half_g, :], start=True, stop=True)
                pe.matmul(pt[2 + h][:, :], ones[:, :], picked[:, half_g, :], start=True, stop=True).then_inc(counted, 1)

        @block.vector
        def _(dve):
            dve.sem_inc(veps_made, BASE)
            dve.sem_inc(xn_made, BASE)
            dve.sem_inc(lo_made, BASE)
            dve.sem_inc(lg_made, BASE)
            dve.wait_ge(whi_made, 1)
            nc.vector.tensor_tensor(wlo[:, :, :], wst[:, :, :], whi[:, :, :].bitcast(F32), ALU.subtract).then_inc(wlo_made, 1)
            with dve.Fori(0, B) as b:
                for i in range(TB):
                    dve.wait_ge(x_in[i], b * 16 + 16)
                    nc.vector.bn_stats(stats[:, i, :], xt[:, i, :]).then_inc(chain, 1)
                dve.wait_ge(chain, b * 12 + 4)
                dve.sem_inc(passed, 1)
                for i in range(TB):
                    nc.vector.bn_aggr(mv[:, i, :], stats[:, i, :]).then_inc(chain, 1)
                dve.wait_ge(chain, b * 12 + 8)
                nc.vector.tensor_scalar(veps[:, :], mv[:, :, 1], EPS, None, ALU.add).then_inc(veps_made, 1)
                dve.wait_ge(half_made, at(b, 1, 1))
                dve.wait_ge(veps_made, at(b, 1, 1))
                nc.vector.reciprocal(tmp[:, :], half[:, :]).then_inc(chain, 1)
                dve.wait_ge(chain, b * 12 + 9)
                nc.vector.tensor_tensor(tmp[:, :], tmp[:, :], veps[:, :], ALU.mult).then_inc(chain, 1)
                dve.wait_ge(chain, b * 12 + 10)
                nc.vector.scalar_tensor_tensor(out=tmp[:, :], in0=tmp[:, :], scalar=0.25, in1=half[:, :],
                                               op0=ALU.mult, op1=ALU.add).then_inc(chain, 1)
                dve.wait_ge(chain, b * 12 + 11)
                nc.vector.reciprocal(rstd[:, :], tmp[:, :]).then_inc(chain, 1)
                dve.wait_ge(chain, b * 12 + 12)
                for i in range(TB):
                    dve.wait_ge(xnt_done, at(b, TB, i + 1 - TB))
                    nc.vector.tensor_scalar(xn[:, i, :], xt[:, i, :], mv[:, i, 0:1], rstd[:, i:i + 1],
                                            ALU.subtract, ALU.mult).then_inc(xn_made, 1)
                for c in range(KC):
                    dve.wait_ge(hi_made, at(b, KC, c + 1))
                    nc.vector.tensor_tensor(lo[:, c, :], pt[c][:, :], hi[:, c, :].bitcast(F32),
                                            ALU.subtract).then_inc(lo_made, 1)
                for i in range(TB):
                    dve.wait_ge(xl_made, at(b, TB, i + 1))
                    nc.vector.tensor_copy(logits[:, bass.ds(b * TB + i, 1), :],
                                          xl[:, i:i + 1, LAT:FG]).then_inc(lg_made, 1)

            linked = [B * 12]

            def link(ins):
                linked[0] += 1
                ins.then_inc(chain, 1)
                dve.wait_ge(chain, linked[0])

            def grouped(a):
                return a[:, :, :].rearrange("p g (n e) -> p (g n) e", e=GE)

            def per_group(a):
                return a[:, :, :].rearrange("p g n -> p (g n)")

            nc.vector.memset(ones[:, :], 1.0).then_inc(ones_made, 1)
            dve.wait_ge(exp_made, 1)
            dve.wait_ge(b_in, 16)
            link(nc.vector.tensor_scalar(score[:, :, :], score[:, :, :], 1.0, None, ALU.add))
            link(nc.vector.reciprocal(score[:, :, :], score[:, :, :]))
            link(nc.vector.tensor_tensor(biased[:, :, :], score[:, :, :],
                                         bia[:, :].unsqueeze(1).broadcast_to([P, G, E]), ALU.add))
            link(nc.vector.tensor_reduce(per_group(first_g), grouped(biased), AX.X, ALU.max))
            link(nc.vector.tensor_tensor(grouped(equal), grouped(biased),
                                         per_group(first_g).unsqueeze(2).broadcast_to([P, G * NG, GE]), ALU.is_equal))
            link(nc.vector.scalar_tensor_tensor(out=grouped(other), in0=grouped(equal), scalar=-BIG, in1=grouped(biased),
                                                op0=ALU.mult, op1=ALU.add))
            link(nc.vector.tensor_reduce(per_group(second_g), grouped(other), AX.X, ALU.max))
            link(nc.vector.tensor_reduce(per_group(twice_g), grouped(equal), AX.X, ALU.add))
            link(nc.vector.tensor_scalar(per_group(twice_g), per_group(twice_g), 2.0, None, ALU.is_lt))
            link(nc.vector.scalar_tensor_tensor(out=per_group(twice_g), in0=per_group(twice_g), scalar=-BIG,
                                                in1=per_group(first_g), op0=ALU.mult, op1=ALU.add))
            link(nc.vector.tensor_tensor(per_group(second_g), per_group(second_g), per_group(twice_g), ALU.max))
            link(nc.vector.tensor_tensor(per_group(first_g), per_group(first_g), per_group(second_g), ALU.add))
            mine = first_g[:, :, :].unsqueeze(3).broadcast_to([P, G, NG, NG])
            theirs = first_g[:, :, :].unsqueeze(2).broadcast_to([P, G, NG, NG])
            earlier = (cst[:, COL["earlier"]].rearrange("p (a b) -> p a b", a=NG).unsqueeze(1)
                       .broadcast_to([P, G, NG, NG]))
            link(nc.vector.tensor_tensor(ties[:, :, :, :], theirs, mine, ALU.is_equal))
            link(nc.vector.tensor_tensor(ties[:, :, :, :], ties[:, :, :, :], earlier, ALU.mult))
            link(nc.vector.tensor_tensor(beats[:, :, :, :], theirs, mine, ALU.is_gt))
            link(nc.vector.tensor_tensor(beats[:, :, :, :], beats[:, :, :, :], ties[:, :, :, :], ALU.add))
            link(nc.vector.tensor_reduce(per_group(twice_g), beats[:, :, :, :].rearrange("p g a b -> p (g a) b"),
                                         AX.X, ALU.add))
            link(nc.vector.tensor_scalar(per_group(twice_g), per_group(twice_g), float(TOPG), -BIG, ALU.is_ge, ALU.mult))
            link(nc.vector.tensor_tensor(grouped(biased), grouped(biased),
                                         per_group(twice_g).unsqueeze(2).broadcast_to([P, G * NG, GE]), ALU.add))
            for g in range(G):
                last = nc.vector.max(top8[:, g, :], biased[:, g, :])
            link(last)
            for g in range(G):
                last = nc.vector.match_replace(out=other[:, g, :], in_to_replace=top8[:, g, :],
                                               in_values=biased[:, g, :], imm_value=BIG)
            link(last)
            link(nc.vector.tensor_tensor(picked[:, :, :], other[:, :, :], biased[:, :, :], ALU.not_equal))
            dve.sem_inc(picked_made, 1)
            link(nc.vector.tensor_tensor(score[:, :, :], score[:, :, :], picked[:, :, :], ALU.mult))
            link(nc.vector.tensor_reduce(token_sum[:, :], score[:, :, :], AX.X, ALU.add))
            link(nc.vector.reciprocal(token_sum[:, :], token_sum[:, :]))
            link(nc.vector.tensor_tensor(score[:, :, :], score[:, :, :],
                                         token_sum[:, :].unsqueeze(2).broadcast_to([P, G, E]), ALU.mult))
            link(nc.vector.tensor_scalar(weights_sb[:, :, :], score[:, :, :], ROUTED_SCALE, None, ALU.mult))
            dve.wait_ge(counted, 2)
            link(nc.vector.memset(before[0][:, 0, :], 0.0))
            for h in range(2):
                n = G // 2 - h
                link(nc.vector.tensor_copy(before[0][:, h * G // 2 + 1:h * G // 2 + 1 + n, :],
                                           pt[2 + h][:, 0:n * E].rearrange("p (g e) -> p g e", e=E)))
            now = 0
            for k in (1, 2, 4, 8, 16):
                a, z = before[now], before[1 - now]
                link(nc.vector.tensor_copy(z[:, 0:k, :], a[:, 0:k, :]))
                link(nc.vector.tensor_tensor(z[:, k:G, :], a[:, k:G, :], a[:, 0:G - k, :], ALU.add))
                now = 1 - now
            earlier_tiles = before[now]
            link(nc.vector.tensor_tensor(count[:, :], earlier_tiles[:, G - 1, :], pt[3][:, (G // 2 - 1) * E:G // 2 * E], ALU.add))
            link(nc.vector.tensor_scalar(count_i[:, :], count[:, :], float(P - 1), None, ALU.add))
            link(nc.vector.tensor_scalar(count_i[:, :], count_i[:, :], 7, None, ALU.logical_shift_right))
            link(nc.vector.tensor_copy(tiles[0][:, :], count_i[:, :]))
            link(nc.vector.tensor_copy(start[:, :], tiles[0][:, :]))
            now = 0
            for k in (1, 2, 4, 8, 16):
                a, z = tiles[now], tiles[1 - now]
                link(nc.vector.tensor_copy(z[:, 0:k], a[:, 0:k]))
                link(nc.vector.tensor_tensor(z[:, k:E], a[:, k:E], a[:, 0:E - k], ALU.add))
                now = 1 - now
            link(nc.vector.tensor_copy(end[:, :], tiles[now][:, :]))
            link(nc.vector.tensor_tensor(start[:, :], end[:, :], start[:, :], ALU.subtract))
            link(nc.vector.tensor_scalar(start[:, :], start[:, :], float(P), None, ALU.mult))
            link(nc.vector.tensor_tensor(other[:, :, :], earlier_tiles[:, :, :],
                                         start[:, :].unsqueeze(1).broadcast_to([P, G, E]), ALU.add))
            for h in range(2):
                gs = slice(h * G // 2, (h + 1) * G // 2)
                link(nc.vector.tensor_tensor(other[:, gs, :], other[:, gs, :],
                                             pt[h][:, :].rearrange("p (g e) -> p g e", e=E), ALU.add))
            link(nc.vector.scalar_tensor_tensor(out=other[:, :, :], in0=other[:, :, :], scalar=1.0, in1=picked[:, :, :],
                                                op0=ALU.add, op1=ALU.mult))
            for g in range(G):
                last = nc.vector.max(top8[:, g, :], other[:, g, :])
            link(last)
            link(nc.vector.tensor_scalar(slots_sb[:, :, :], top8[:, :, :], -1.0, None, ALU.add))
            link(nc.vector.tensor_tensor(pad[0][:, :], start[:, :], count[:, :], ALU.add))
            link(nc.vector.tensor_scalar(pad[0][:, :], pad[0][:, :], cst[:, COL["lane"]], None, ALU.add))
            link(nc.vector.scalar_tensor_tensor(out=pad[1][:, :], in0=end[:, :], scalar=float(P), in1=pad[0][:, :],
                                                op0=ALU.mult, op1=ALU.is_le))
            link(nc.vector.scalar_tensor_tensor(out=pad[0][:, :], in0=pad[1][:, :], scalar=float(2 * SLOTS),
                                                in1=pad[0][:, :], op0=ALU.mult, op1=ALU.add))
            link(nc.vector.tensor_copy(pads_sb[:, :], pad[0][:, :]))
            link(nc.vector.tensor_tensor(owner[:, :, :], end[:, :].unsqueeze(1).broadcast_to([P, 3, E]),
                                         cst[:, COL["tile"]].unsqueeze(2).broadcast_to([P, 3, E]), ALU.is_le))
            link(nc.vector.tensor_reduce(expert_f[:, :], owner[:, :, :], AX.X, ALU.add))
            link(nc.vector.tensor_scalar(expert_f[:, :], expert_f[:, :], float(E - 1), None, ALU.min))
            nc.vector.tensor_copy(expert_i[:, :], expert_f[:, :]).then_inc(expert_made, 1)

NSLOT = NH + 1
HC = NH // KC
SHALF = S // 2
ROWS = [3, 2, 1, 0]
SPC = [0, 128, 384, 768]
NSP = 10 * P
PTC = {0: (0, 0), 1: (512, 128), 3: (896, 384), 2: (1024, 256)}

def q_slot(n):
    return (n - 1) * HC


Q_AT = {q_slot(n): n for n in range(1, KC)}
U_ORDER = []
for _s in range(NH):
    U_ORDER.append(f"up{_s}")
    if _s in Q_AT:
        U_ORDER.append(f"q{Q_AT[_s]}")
U_ORDER += ["q0", "kv", "vt"]
QK_AT = {"q1": 0, "q2": 1, "q3": 2, "q0": 3, "kv": 4}
NQK = len(QK_AT)
NU = len(U_ORDER)
U_AT = {n: k for k, n in enumerate(U_ORDER)}


def split_weights(nc, parts):
    with ExitStack() as ctx:
        W = 2048
        pieces = []
        for dram, hi, lo in parts:
            n = hi.shape[1]
            for a in range(0, n, W):
                pieces.append((dram[:, a:min(n, a + W)], hi[:, a:min(n, a + W)], lo[:, a:min(n, a + W)], min(W, n - a)))
        R = 4
        stage = ctx.enter_context(nc.sbuf_tensor("w_stage", [P, R, W], F32))
        landed = [ctx.enter_context(nc.semaphore(f"w_landed{r}")) for r in range(R)]
        hi_made = ctx.enter_context(nc.semaphore("w_hi_made"))
        lo_made = ctx.enter_context(nc.semaphore("w_lo_made"))
        block = ctx.enter_context(nc.Block())

        @block.sync
        def _(sp):
            for k, (dram, hi, lo, n) in enumerate(pieces):
                if k >= R:
                    sp.wait_ge(lo_made, k - R + 1)
                sp.dma_start(stage[:, k % R, 0:n], dram).then_inc(landed[k % R], 16)

        @block.scalar
        def _(act):
            for k, (dram, hi, lo, n) in enumerate(pieces):
                act.wait_ge(landed[k % R], 16 * (k // R + 1))
                nc.scalar.activation(hi, stage[:, k % R, 0:n], ACT.Copy).then_inc(hi_made, 1)

        @block.vector
        def _(dve):
            for k, (dram, hi, lo, n) in enumerate(pieces):
                dve.wait_ge(hi_made, k + 1)
                nc.vector.tensor_tensor(lo, stage[:, k % R, 0:n], hi.bitcast(F32), ALU.subtract).then_inc(lo_made, 1)


def middle(nc, x, bproj, xnt_hi, xnt_lo, xlat, wq, wkv, wproj, wup, wdown, cst, weights_sb, slots_sb, pads_sb, xs, partial):
    with ExitStack() as ctx:
        def sb(name, shape, dt=F32):
            return ctx.enter_context(nc.sbuf_tensor(name, shape, dt))

        def sem(name):
            return ctx.enter_context(nc.semaphore(name))

        def pb(name):
            return ctx.enter_context(nc.psum_tensor(name, [P, S], F32))

        ident = cst[:, COL["ident"]]
        mask = cst[:, COL["mask"]]
        tables = {"q": (cst[:, COL["cosq"]], cst[:, COL["sinq"]]), "k": (cst[:, COL["cosk"]], cst[:, COL["sink"]])}
        (wq_hi, wq_lo), (wkv_hi, wkv_lo), (up_hi, up_lo), (down_hi, down_lo) = [
            [w.rearrange("p (c n) -> p c n", c=c) for w in pair]
            for pair, c in ((wq, KC), (wkv, KC), (wup, KC), (wdown, SC))]
        xh = sb("m_xh", [P, KC, S], F32R)
        xlo = sb("m_xlo", [P, KC, S], F32R)
        kv = sb("m_kv", [P, S])
        q = sb("m_q", [P, S])
        rot = sb("m_rot", [P, S])
        qhi = sb("m_qhi", [P, S], F32R)
        qlo = sb("m_qlo", [P, S], F32R)
        qs = sb("m_qs", [96, 2, HC, S], F32R)
        ks = sb("m_ks", [96, S], F32R)
        vpad = sb("m_vpad", [P, TB, 7 * HD])
        sc = sb("m_sc", [P, 2, NSP])
        low = sb("m_low", [P, 2, TB])
        total = sb("m_total", [P, 2, TB])
        inv = sb("m_inv", [P, 2, TB])
        pt = sb("m_pt", [P, 2, NSP])
        ot = sb("m_ot", [P, KC, S])
        relu = sb("m_relu", [P, SHALF])
        sq = sb("m_sq", [P, SHALF])
        sqhi = sb("m_sqhi", [P, 2, SHALF], F32R)
        sqlo = sb("m_sqlo", [P, 2, SHALF], F32R)
        res = sb("m_res", [P, TB, D])
        bp = sb("m_bp", [P, D])
        row = [sb(f"m_row{u}", [P, ROW]) for u in range(2)]
        idx = [sb(f"m_idx{u}", [P, TOPK], U32) for u in range(2)]
        empty = sb("m_empty", [P, ROW])
        psS = [pb(f"m_psS{i}") for i in range(2)]
        psT = [pb(f"m_psT{i}") for i in range(2)]
        psO, psU = pb("m_psO"), pb("m_psU")
        psY = [pb(f"m_psY{i}") for i in range(2)]

        dve_passed, pool_passed, sp_passed = sem("m_dve_passed"), sem("m_pool_passed"), sem("m_sp_passed")
        u_done, s_done, t_done, pv_done = sem("m_u_done"), sem("m_s_done"), sem("m_t_done"), sem("m_pv_done")
        y_step, y_done = sem("m_y_step"), sem("m_y_done")
        qk_copied, hi_made = sem("m_qk_copied"), sem("m_hi_made")
        exp_done, relu_made, sqhi_made = sem("m_exp_done"), sem("m_relu_made"), sem("m_sqhi_made")
        ta_out, o_out = sem("m_ta_out"), sem("m_o_out")
        rot_step, rotated, lo_made, v_made = sem("m_rot_step"), sem("m_rotated"), sem("m_lo_made"), sem("m_v_made")
        s_out, inv_made, scaled, tb_out = sem("m_s_out"), sem("m_inv_made"), sem("m_scaled"), sem("m_tb_out")
        sq_made, sqlo_made, res_made, y_out = sem("m_sq_made"), sem("m_sqlo_made"), sem("m_res_made"), sem("m_y_out")
        vpad_clear = sem("m_vpad_clear")
        xh_in, xlo_in, bp_in, res_in = sem("m_xh_in"), sem("m_xlo_in"), sem("m_bp_in"), sem("m_res_in")
        qs_in = [sem(f"m_qs_in{u}") for u in range(2)]
        saved = sem("m_saved")
        row_in = [sem(f"m_row_in{u}") for u in range(2)]
        idx_made = [sem(f"m_idx_made{u}") for u in range(2)]
        sent = [sem(f"m_sent{u}") for u in range(2)]
        empty_made, tail_sent, pads_sent = sem("m_empty_made"), sem("m_tail_sent"), sem("m_pads_sent")
        block = ctx.enter_context(nc.Block())

        NQ = HC * 3 * 16

        def stacked(b, c):
            return b * (2 * NQ) + (16 * BASE + NQ * (c // 2 + c % 2))

        def before(b, c):
            return (b, c - 1) if c else (b - 1, KC - 1)

        @block.sync
        def _(sp):
            def load_tokens(b, h):
                tok = slice(h * SHALF, (h + 1) * SHALF)
                for to, src, landed in ((xh, xnt_hi, xh_in), (xlo, xnt_lo, xlo_in)):
                    sp.dma_start(to[:, :, tok].bitcast(F32),
                                 src[bass.ds(b, 1)].rearrange("a p c s -> (a p) c s")[:, :, tok]).then_inc(landed, 16)

            def stack(b, c, turn):
                for halves_made, parts in ((hi_made, ((0, qhi), (1, qhi))), (lo_made, ((2, qlo),))):
                    sp.wait_ge(halves_made, at(turn, NQK, QK_AT[f"q{c}"] + 1))
                    sp.sem_inc(sp_passed, 1)
                    sp.wait_ge(s_done, at(b, NH * TB, HC * TB * (c - 1)))
                    for j in range(HC):
                        for k, src in parts:
                            sp.dma_start(qs[k * HD:(k + 1) * HD, c % 2, j, :].bitcast(F32),
                                         src[j * HD:(j + 1) * HD, :].bitcast(F32)).then_inc(qs_in[c % 2], 16)

            sp.sem_inc(qs_in[0], 16 * BASE - NQ)
            sp.sem_inc(qs_in[1], 16 * BASE)
            sp.dma_start(bp[:, :], bproj.partition_broadcast(P)).then_inc(bp_in, 16)
            load_tokens(0, 0)
            load_tokens(0, 1)
            stack(0, 0, -1)
            with sp.Fori(0, B) as b:
                stack(b, 1, b)
                sp.wait_ge(saved, b * 16 + 16 * BASE)
                sp.dma_start(res[:, :, :], x[bass.ds(b * S, S), :].rearrange("(i p) d -> p i d", p=P)
                             ).then_inc(res_in, 16)
                stack(b, 2, b)
                sp.wait_ge(u_done, at(b, NU, U_AT["q3"] + 1))
                load_tokens(b + 1, 0)
                stack(b, 3, b)
                sp.wait_ge(u_done, at(b, NU, U_AT["up15"] + 1))
                load_tokens(b + 1, 1)
                stack(b + 1, 0, b)
            for landed, value in ((qs_in[0], stacked(B, 0)), (xh_in, 32 * (B + 1)), (xlo_in, 32 * (B + 1))):
                sp.wait_ge(landed, value)

        @block.gpsimd
        def _(pool):
            nc.gpsimd.memset(empty[:, :], 0.0).then_inc(empty_made, 1)
            pool.wait_ge(empty_made, 1)
            nc.gpsimd.tensor_copy(empty[:, ROW - 1:ROW].bitcast(U32), cst[:, COL["spare"]]).then_inc(empty_made, 1)
            pool.wait_ge(empty_made, 2)
            pool.dma_start(xs[FULL_TILES * P:SLOTS, :].rearrange("(a p) r -> p a r", p=P),
                           empty[:, :].unsqueeze(1).broadcast_to([P, E, ROW])).then_inc(tail_sent, 16)
            pool.wait_ge(tail_sent, 16)
            for e in range(E):
                pool.indirect_dma_start(out=xs, out_offset=bass.IndirectOffsetOnAxis(ap=pads_sb[:, e:e + 1], axis=0),
                                        in_=empty[:, :], in_offset=None, bounds_check=SLOTS - 1,
                                        oob_is_err=False).then_inc(pads_sent, 16)
            pool.wait_ge(pads_sent, 16 * E)
            with pool.Fori(0, G // 2) as i:
                for u in range(2):
                    pool.dma_start(row[u][:, 0:LAT], xlat[bass.ds(i * 2 * P + u * P, P), :]).then_inc(row_in[u], 16)
                    nc.gpsimd.tensor_copy(row[u][:, LAT:LAT + E].unsqueeze(1),
                                          weights_sb[:, bass.ds(i * 2 + u, 1), :]).then_inc(idx_made[u], 1)
                    nc.gpsimd.tensor_copy(row[u][:, ROW - 1:ROW].bitcast(U32),
                                          cst[:, bass.ds(i * 2 + (COL["token"].start + u), 1)]).then_inc(idx_made[u], 1)
                    nc.gpsimd.tensor_copy(idx[u][:, :].unsqueeze(1),
                                          slots_sb[:, bass.ds(i * 2 + u, 1), :]).then_inc(idx_made[u], 1)
                for u in range(2):
                    pool.wait_ge(row_in[u], i * 16 + 16)
                    pool.wait_ge(idx_made[u], i * 3 + 3)
                    pool.sem_inc(pool_passed, 1)
                    for k in range(TOPK):
                        pool.indirect_dma_start(out=xs, out_offset=bass.IndirectOffsetOnAxis(ap=idx[u][:, k:k + 1], axis=0),
                                                in_=row[u][:, :], in_offset=None).then_inc(sent[u], 16)
                for u in range(2):
                    pool.wait_ge(sent[u], i * (16 * TOPK) + 16 * TOPK)

        @block.scalar
        def _(act):
            for s_ in (exp_done, relu_made, sqhi_made, ta_out, o_out):
                act.sem_inc(s_, BASE)
            act.sem_inc(qk_copied, BASE - 2)
            act.sem_inc(hi_made, BASE - 2)
            act.sem_inc(saved, 16 * BASE)

            def copy_out(b, name):
                act.wait_ge(u_done, at(b, NU, U_AT[name] + 1))
                if name == "kv":
                    act.wait_ge(v_made, at(b, 1, 0))
                    act.wait_ge(lo_made, at(b, NQK, QK_AT["kv"] + 1 - NQK))
                else:
                    act.wait_ge(lo_made, at(b, NQK, QK_AT[name] if name in ("q2", "q3") else 0 if name == "q1" else QK_AT["q3"] + 1))
                nc.scalar.activation((kv if name == "kv" else q)[:, :], psU[:, :], ACT.Copy).then_inc(qk_copied, 1)

            def high(b, name):
                act.wait_ge(rotated, at(b, NQK, QK_AT[name] + 1))
                if name == "kv":
                    act.wait_ge(s_done, at(b, NH * TB, NH * TB))
                    nc.scalar.activation(ks[:, :], kv[0:96, :], ACT.Copy).then_inc(hi_made, 1)
                else:
                    c = int(name[1:])
                    bb, cc = before(b if c else b + 1, c)
                    act.wait_ge(qs_in[cc % 2], stacked(bb, cc))
                    nc.scalar.activation(qhi[:, :], q[:, :], ACT.Copy).then_inc(hi_made, 1)

            for name in ("q0", "kv"):
                copy_out(-1, name)
            for name in ("q0", "kv"):
                high(-1, name)
            with act.Fori(0, B) as b:
                def exps(h, i):
                    k = h * TB + ROWS.index(i)
                    act.wait_ge(s_out, at(b, NH * TB, k + 1))
                    if i == ROWS[0]:
                        act.wait_ge(inv_made, at(b, NH, h - 1))
                    cols = sc[:, h % 2, SPC[i]:SPC[i] + (i + 1) * P]
                    nc.scalar.activation(cols, cols, ACT.Exp, bias=low[:, h % 2, i:i + 1], scale=-1.0,
                                         accum_out=total[:, h % 2, i:i + 1]).then_inc(exp_done, 1)

                def ta(h, c):
                    act.wait_ge(t_done, at(b, 3 * NH, 3 * h + (1 if c == 0 else 3)))
                    if c == 0:
                        act.wait_ge(pv_done, at(b, NH, h - 1))
                        nc.scalar.activation(pt[:, h % 2, 0:512], psT[0][:, :], ACT.Copy).then_inc(ta_out, 1)
                    else:
                        nc.scalar.activation(pt[:, h % 2, 1024:1280], psT[0][:, 0:256], ACT.Copy).then_inc(ta_out, 1)

                def shared(s):
                    act.wait_ge(u_done, at(b, NU, U_AT[f"up{s}"] + 1))
                    act.wait_ge(sq_made, at(b, NH, s))
                    act.wait_ge(sqhi_made, at(b, NH, s))
                    nc.scalar.activation(relu[:, :], psU[:, 0:SHALF], ACT.Relu).then_inc(relu_made, 1)
                    act.wait_ge(relu_made, at(b, NH, s + 1))
                    act.wait_ge(y_step, at(b, NH, s - 1))
                    nc.scalar.activation(sqhi[:, s % 2, :], relu[:, :], ACT.Square).then_inc(sqhi_made, 1)

                for s in range(NSLOT):
                    t = s - 1
                    if s - 1 in Q_AT:
                        copy_out(b, f"q{Q_AT[s - 1]}")
                    if s < NH:
                        for i in ROWS[:3]:
                            exps(s, i)
                    if t >= 0:
                        ta(t, 0)
                    if s < NH:
                        exps(s, ROWS[3])
                        shared(s)
                    if s - 2 in Q_AT:
                        high(b, f"q{Q_AT[s - 2]}")
                    if t >= 0:
                        ta(t, 2)
                    if t >= 0 and t % HC == HC - 1:
                        act.wait_ge(pv_done, at(b, NH, t + 1))
                        act.wait_ge(y_done, at(b, 4, 0))
                        nc.scalar.activation(ot[:, t // HC, :], psO[:, :], ACT.Copy).then_inc(o_out, 1)
                for name in ("q0", "kv"):
                    copy_out(b, name)
                for name in ("q0", "kv"):
                    high(b, name)
                act.wait_ge(y_out, at(b, 4, 4))
                act.dma_start(partial[bass.ds(b * S, S), :].rearrange("(i p) d -> p i d", p=P),
                              res[:, :, :]).then_inc(saved, 16)
            act.wait_ge(saved, 16 * (BASE + B))

        @block.vector
        def _(dve):
            dve.sem_inc(rot_step, BASE - 2 * 3)
            dve.sem_inc(rotated, BASE - 2)
            dve.sem_inc(lo_made, BASE - 2)
            dve.sem_inc(v_made, BASE - 1)
            for s_ in (s_out, inv_made, scaled, tb_out, sq_made, sqlo_made,
                       res_made, y_out):
                dve.sem_inc(s_, BASE)
            nc.vector.memset(vpad[:, :, :], 0.0).then_inc(vpad_clear, 1)
            dve.wait_ge(vpad_clear, 1)

            def rotate(b, name, parts=(0, 1)):
                n = QK_AT[name]
                x_ = kv[0:96, :] if name == "kv" else q[:, :]
                r_ = rot[0:96, :] if name == "kv" else rot[:, :]
                cos, sin = (a[0:96, :] if name == "kv" else a for a in tables["k" if name == "kv" else "q"])
                if 0 in parts:
                    dve.wait_ge(qk_copied, at(b, NQK, n + 1))
                    dve.wait_ge(rotated, at(b, NQK, n))
                    dve.sem_inc(dve_passed, 1)
                    nc.vector.stream_shuffle(r_, x_, [(i + HD // 2) % HD for i in range(HD)]).then_inc(rot_step, 1)
                    dve.wait_ge(rot_step, at(b, 3 * NQK, 3 * n + 1))
                    nc.vector.tensor_tensor(x_, x_, cos, ALU.mult).then_inc(rot_step, 1)
                if 1 in parts:
                    nc.vector.tensor_tensor(r_, r_, sin, ALU.mult).then_inc(rot_step, 1)
                    dve.wait_ge(rot_step, at(b, 3 * NQK, 3 * n + 3))
                    nc.vector.tensor_tensor(x_, x_, r_, ALU.add).then_inc(rotated, 1)

            def low_part(b, name):
                dve.wait_ge(hi_made, at(b, NQK, QK_AT[name] + 1))
                dve.wait_ge(rotated, at(b, NQK, QK_AT[name] + 1))
                if name == "kv":
                    nc.vector.tensor_tensor(ks[HD:2 * HD, :], kv[HD:2 * HD, :], ks[HD:2 * HD, :].bitcast(F32),
                                            ALU.subtract).then_inc(lo_made, 1)
                else:
                    c = int(name[1:])
                    bb, cc = before(b if c else b + 1, c)
                    dve.wait_ge(qs_in[cc % 2], stacked(bb, cc))
                    nc.vector.tensor_tensor(qlo[:, :], q[:, :], qhi[:, :].bitcast(F32), ALU.subtract).then_inc(lo_made, 1)

            def place_values(b):
                dve.wait_ge(u_done, at(b, NU, U_AT["vt"] + 1))
                dve.wait_ge(pv_done, at(b, NH, NH))
                nc.vector.tensor_copy(vpad[:, :, 3 * HD:4 * HD],
                                      psU[:, :].rearrange("p (t n) -> p t n", n=P)[:, :, 3 * HD:4 * HD]
                                      ).then_inc(v_made, 1)

            for name in ("q0", "kv"):
                rotate(-1, name)
            for name in ("q0", "kv"):
                low_part(-1, name)
            place_values(-1)
            with dve.Fori(0, B) as b:
                def mask_and_min(h, i):
                    k = h * TB + ROWS.index(i)
                    dve.wait_ge(s_done, at(b, NH * TB, k + 1))
                    if i == ROWS[0]:
                        dve.wait_ge(t_done, at(b, 3 * NH, 3 * (h - 1)))
                        dve.wait_ge(exp_done, at(b, NH * TB, TB * (h - 1)))
                        dve.wait_ge(scaled, at(b, NH, h - 1))
                    n = (i + 1) * P
                    dve.sem_inc(dve_passed, 1)
                    nc.vector.tensor_tensor_reduce(out=sc[:, h % 2, SPC[i]:SPC[i] + n], in0=psS[k % 2][:, 0:n],
                                                   in1=mask[:, S - n:S], scale=1.0, scalar=3.0e38, op0=ALU.add,
                                                   op1=ALU.min, accum_out=low[:, h % 2, i:i + 1]).then_inc(s_out, 1)

                def scale(h):
                    dve.wait_ge(exp_done, at(b, NH * TB, TB * (h + 1)))
                    nc.vector.reciprocal(inv[:, h % 2, :], total[:, h % 2, :]).then_inc(inv_made, 1)
                    dve.wait_ge(inv_made, at(b, NH, h + 1))
                    for i in range(TB):
                        cols = sc[:, h % 2, SPC[i]:SPC[i] + (i + 1) * P]
                        last = nc.vector.tensor_scalar(cols, cols, inv[:, h % 2, i:i + 1], None, ALU.mult)
                    last.then_inc(scaled, 1)

                def tb(h):
                    dve.wait_ge(t_done, at(b, 3 * NH, 3 * h + 2))
                    dve.wait_ge(pv_done, at(b, NH, h - 1))
                    nc.vector.tensor_copy(pt[:, h % 2, 512:1024], psT[1][:, :]).then_inc(tb_out, 1)

                def shared(s):
                    dve.wait_ge(relu_made, at(b, NH, s + 1))
                    dve.wait_ge(sqlo_made, at(b, NH, s))
                    nc.vector.tensor_tensor(sq[:, :], relu[:, :], relu[:, :], ALU.mult).then_inc(sq_made, 1)
                    dve.wait_ge(sq_made, at(b, NH, s + 1))
                    dve.wait_ge(sqhi_made, at(b, NH, s + 1))
                    dve.wait_ge(y_step, at(b, NH, s - 1))
                    nc.vector.tensor_tensor(sqlo[:, s % 2, :], sq[:, :], sqhi[:, s % 2, :].bitcast(F32),
                                            ALU.subtract).then_inc(sqlo_made, 1)

                def add_result(k):
                    dve.wait_ge(y_done, at(b, 4, k + 1))
                    if k < 2:
                        dve.wait_ge(res_made, at(b, 1, 1))
                    else:
                        dve.wait_ge(y_out, at(b, 4, k - 1))
                    for i in range(2):
                        r_ = res[:, 2 * (k % 2) + i, :]
                        last = nc.vector.tensor_tensor(r_, psY[i][:, :], r_, ALU.add)
                    last.then_inc(y_out, 1)

                for s in range(NSLOT):
                    t = s - 1
                    if s < NH:
                        for i in ROWS:
                            mask_and_min(s, i)
                    if t >= 0:
                        tb(t)
                    if s - 2 in Q_AT:
                        rotate(b, f"q{Q_AT[s - 2]}", (1,))
                    if s < NH:
                        shared(s)
                        scale(s)
                    if s - 2 in Q_AT:
                        low_part(b, f"q{Q_AT[s - 2]}")
                    if s - 1 in Q_AT:
                        rotate(b, f"q{Q_AT[s - 1]}", (0,))
                    if s == 4:
                        dve.wait_ge(res_in, b * 16 + 16)
                        dve.wait_ge(bp_in, 16)
                        nc.vector.tensor_tensor(res[:, :, :], res[:, :, :], bp[:, :].unsqueeze(1).broadcast_to([P, TB, D]),
                                                ALU.add).then_inc(res_made, 1)
                    if s in (8, 16):
                        add_result(s // 8 - 1)
                add_result(2)
                rotate(b, "q0")
                low_part(b, "q0")
                rotate(b, "kv")
                low_part(b, "kv")
                place_values(b)
                add_result(3)

        @block.tensor
        def _(pe):
            for s_ in (s_done, t_done, pv_done, y_step, y_done):
                pe.sem_inc(s_, BASE)
            pe.sem_inc(u_done, BASE - 3)
            pe.wait_ge(vpad_clear, 1)

            def bank_free(b, name):
                k = U_AT[name]
                last, back = (U_ORDER[k - 1], 0) if k else (U_ORDER[-1], 1)
                if last.startswith("up"):
                    pe.wait_ge(relu_made, at(b, NH, int(last[2:]) + 1))
                elif last == "vt":
                    pe.wait_ge(v_made, at(b, 1, 1 - back))
                else:
                    pe.wait_ge(qk_copied, at(b, NQK, QK_AT[last] + 1))

            def project(b, name, whi, wlo):
                bank_free(b, name)
                if name == "q0":
                    pe.wait_ge(xh_in, b * 32 + 64)
                    pe.wait_ge(xlo_in, b * 32 + 64)
                for c in range(KC):
                    mm = three(pe, psU[:, :], (whi[:, c, :], wlo[:, c, :]), (xh[:, c, :], xlo[:, c, :]),
                               c == 0, c == KC - 1)
                mm.then_inc(u_done, 1)

            def queries(b, n):
                cols = slice(n * P, (n + 1) * P)
                project(b, f"q{n}", wq_hi[:, :, cols], wq_lo[:, :, cols])

            def turn_values(b):
                bank_free(b, "vt")
                pe.wait_ge(rotated, at(b, NQK, QK_AT["kv"] + 1))
                for i in range(TB):
                    mm = pe.transpose(psU[:, i * P:(i + 1) * P], kv[:, i * P:(i + 1) * P], ident)
                mm.then_inc(u_done, 1)

            queries(-1, 0)
            project(-1, "kv", wkv_hi, wkv_lo)
            turn_values(-1)
            with pe.Fori(0, B) as b:
                def up(s):
                    tok = slice(s // 8 * SHALF, (s // 8 + 1) * SHALF)
                    cols = slice(s % 8 * P, (s % 8 + 1) * P)
                    bank_free(b, f"up{s}")
                    for c in range(KC):
                        mm = three(pe, psU[:, 0:SHALF], (up_hi[:, c, cols], up_lo[:, c, cols]),
                                   (xh[:, c, tok], xlo[:, c, tok]), c == 0, c == KC - 1)
                    mm.then_inc(u_done, 1)

                def down(s):
                    pe.wait_ge(sqhi_made, at(b, NH, s + 1))
                    pe.wait_ge(sqlo_made, at(b, NH, s + 1))
                    if s % 8 == 0:
                        pe.wait_ge(y_out, at(b, 4, s // 8))
                    for i in range(2):
                        tok = slice(i * P, (i + 1) * P)
                        mm = three(pe, psY[i][:, :], (sqhi[:, s % 2, tok], sqlo[:, s % 2, tok]),
                                   (down_hi[:, s % 8, :], down_lo[:, s % 8, :]), s % 8 == 0, s % 8 == 7)
                    mm.then_inc(y_step, 1)
                    if s % 8 == 7:
                        pe.wait_ge(y_step, at(b, NH, s + 1))
                        pe.sem_inc(y_done, 1)

                def scores(h, i):
                    k = h * TB + ROWS.index(i)
                    c = h // HC
                    if i == ROWS[0]:
                        pe.wait_ge(qs_in[c % 2], stacked(b, c))
                        if h == 0:
                            pe.wait_ge(lo_made, at(b, NQK, 0))
                            pe.wait_ge(hi_made, at(b, NQK, 0))
                    pe.wait_ge(s_out, at(b, NH * TB, k - 1))
                    n = max((i + 1) * P, 2 * P)
                    pe.matmul(psS[k % 2][:, 0:n], qs[:, c % 2, h % HC, i * P:(i + 1) * P], ks[:, 0:n],
                              start=True, stop=True).then_inc(s_done, 1)

                def transposes(h, g):
                    if g == 0:
                        pe.wait_ge(scaled, at(b, NH, h + 1))
                        pe.wait_ge(ta_out, at(b, 2 * NH, 2 * h))
                        todo = [(0, 0, i) for i in range(4)]
                    elif g == 1:
                        pe.wait_ge(tb_out, at(b, NH, h))
                        todo = [(1, 1, i) for i in range(1, 4)] + [(1, 3, 3)]
                    else:
                        pe.wait_ge(ta_out, at(b, 2 * NH, 2 * h + 1))
                        todo = [(0, 2, i) for i in range(2, 4)]
                    for bank, j, i in todo:
                        first, query = PTC[j]
                        to = (first + i * P - query) % 512
                        mm = pe.transpose(psT[bank][:, to:to + P], sc[:, h % 2, SPC[i] + j * P:SPC[i] + (j + 1) * P], ident)
                    mm.then_inc(t_done, 1)

                def values(h):
                    if h % HC == 0:
                        pe.wait_ge(o_out, at(b, KC, h // HC))
                    if h == 0:
                        pe.wait_ge(v_made, at(b, 1, 0))
                    for j in (0, 1, 3, 2):
                        if j == 0:
                            pe.wait_ge(ta_out, at(b, 2 * NH, 2 * h + 1))
                        elif j == 1:
                            pe.wait_ge(tb_out, at(b, NH, h + 1))
                        elif j == 2:
                            pe.wait_ge(ta_out, at(b, 2 * NH, 2 * h + 2))
                        first, query = PTC[j]
                        place = (HC - 1 - h % HC) * HD
                        mm = pe.matmul(psO[:, query:S], vpad[:, j, place:place + P],
                                       pt[:, h % 2, first:first + S - query],
                                       start=(h % HC == 0 and j == 0), stop=(h % HC == HC - 1 and j == 2))
                    mm.then_inc(pv_done, 1)

                def attention_result(k):
                    pe.wait_ge(y_out, at(b, 4, k + 2))
                    for i in range(2):
                        tok = slice((2 * k + i) * P, (2 * k + i + 1) * P)
                        for c in range(KC):
                            mm = pe.matmul(psY[i][:, :], ot[:, c, tok], wproj[:, c, :], start=(c == 0), stop=(c == KC - 1))
                    mm.then_inc(y_done, 1)

                for s in range(NSLOT):
                    t = s - 1
                    if s < NH:
                        scores(s, ROWS[0])
                        scores(s, ROWS[1])
                    if s >= 1:
                        down(s - 1)
                    if s < NH:
                        scores(s, ROWS[2])
                        scores(s, ROWS[3])
                    if t >= 0:
                        transposes(t, 0)
                        transposes(t, 1)
                    if s < NH:
                        up(s)
                    if t >= 0:
                        transposes(t, 2)
                        values(t)
                    if s in Q_AT:
                        queries(b, Q_AT[s])
                pe.wait_ge(o_out, at(b, KC, KC))
                attention_result(0)
                queries(b, 0)
                project(b, "kv", wkv_hi, wkv_lo)
                attention_result(1)
                turn_values(b)

NR = 8
NY = 4


def experts(nc, w1, w2, cst, experts_dram, xs, sums):
    with ExitStack() as ctx:
        def sb(name, shape, dt=F32):
            return ctx.enter_context(nc.sbuf_tensor(name, shape, dt))

        def sem(name):
            return ctx.enter_context(nc.semaphore(name))

        def pb(name):
            return ctx.enter_context(nc.psum_tensor(name, [P, S], F32))

        ident = cst[:, COL["ident"]]
        W = LC * INTER
        w1_sb = sb("e_w1", [P, E * W])
        w2_sb = sb("e_w2", [P, E * W])
        table = sb("e_table", [1, 3 * P], I32)
        row = [sb(f"e_row{u}", [P, ROW]) for u in range(NR)]
        xt = [sb(f"e_xt{u}", [P, LAT]) for u in range(2)]
        relu = [sb(f"e_relu{u}", [P, INTER]) for u in range(2)]
        ht = [sb(f"e_ht{u}", [P, INTER]) for u in range(2)]
        y = [sb(f"e_y{u}", [P, LAT]) for u in range(NY)]
        psX, psH, psT, psY = ([pb(f"e_ps{n}{u}") for u in range(2)] for n in "XHTY")
        w_in = [sem("e_w1_in"), sem("e_w2_in")]
        table_in = sem("e_table_in")
        passed = sem("e_passed")
        row_in = [sem(f"e_row_in{u}") for u in range(NR)]
        x_turned, h_done, h_turned, y_done = sem("e_x_turned"), sem("e_h_done"), sem("e_h_turned"), sem("e_y_done")
        xt_made, ht_made, relu_made, y_made = sem("e_xt_made"), sem("e_ht_made"), sem("e_relu_made"), sem("e_y_made")
        added = [sem(f"e_added{u}") for u in range(2)]
        block = ctx.enter_context(nc.Block())

        def program(eng, stages):
            for s in range(NR):
                for lag, step in stages:
                    if s >= lag:
                        step(0, s - lag)
            with eng.Fori(1, SLOT_TILES // NR) as i:
                for s in range(NR):
                    for lag, step in stages:
                        step(i, s - lag)
            for s in range(max(lag for lag, _ in stages)):
                for lag, step in stages:
                    if s < lag:
                        step(SLOT_TILES // NR, s - lag)

        def num(i, u, n=0):
            return i * NR + (BASE + u + n)

        def sums_done(i, u):
            return i * (16 * NR // 2) + 16 * (u // 2 + 1)

        def first(i, u, n):
            return isinstance(i, int) and i * NR + u < n

        @block.sync
        def _(sp):
            sp.dma_start(table[:, :], experts_dram.rearrange("(a n) -> a n", a=1)).then_inc(table_in, 16)

            def load(i, u):
                if not first(i, u, NR):
                    sp.wait_ge(added[u % 2], sums_done(i, u - NR))
                sp.dma_start(row[u][:, :], xs[bass.ds(i * NR * P + u * P, P), :]).then_inc(row_in[u], 16)

            for u in range(NR):
                load(0, u)
            for k in range(4):
                cols = slice(k * E * W // 4, (k + 1) * E * W // 4)
                sp.dma_start(w1_sb[:, cols], w1[:, cols]).then_inc(w_in[0], 16)
            with sp.Fori(1, SLOT_TILES // NR) as i:
                for u in range(NR):
                    load(i, u)

        @block.scalar
        def _(act):
            for s_ in (xt_made, ht_made):
                act.sem_inc(s_, BASE)
            for k in range(4):
                cols = slice(k * E * W // 4, (k + 1) * E * W // 4)
                act.dma_start(w2_sb[:, cols], w2[:, cols]).then_inc(w_in[1], 16)

            def turned_x(i, u):
                act.wait_ge(x_turned, num(i, u, 1))
                act.wait_ge(h_done, num(i, u, -1))
                nc.scalar.activation(xt[u % 2][:, :], psX[u % 2][:, 0:LAT], ACT.Copy).then_inc(xt_made, 1)

            def turned_h(i, u):
                act.wait_ge(h_turned, num(i, u, 1))
                act.wait_ge(y_done, num(i, u, -1))
                nc.scalar.activation(ht[u % 2][:, :], psT[u % 2][:, 0:INTER], ACT.Square).then_inc(ht_made, 1)

            program(act, ((0, turned_x), (2, turned_h)))

        @block.vector
        def _(dve):
            for s_ in (relu_made, y_made):
                dve.sem_inc(s_, BASE)
            dve.wait_ge(table_in, 16)

            def rectify(i, u):
                dve.wait_ge(h_done, num(i, u, 1))
                dve.wait_ge(h_turned, num(i, u, -1))
                nc.vector.tensor_scalar(relu[u % 2][:, :], psH[u % 2][:, 0:INTER], 0.0, None, ALU.max).then_inc(relu_made, 1)

            def weigh(i, u):
                e = dve.value_load(table[0:1, bass.ds(i * NR + u, 1)], min_val=0, max_val=E - 1)
                dve.wait_ge(y_done, num(i, u, 1))
                if not first(i, u, NY):
                    dve.wait_ge(added[u % 2], sums_done(i, u - NY))
                nc.vector.tensor_scalar(y[u % NY][:, :], psY[u % 2][:, 0:LAT], row[u % NR][:, bass.ds(e + LAT, 1)], None,
                                        ALU.mult).then_inc(y_made, 1)

            program(dve, ((1, rectify), (3, weigh)))

        @block.gpsimd
        def _(pool):
            def add(i, u):
                pool.wait_ge(y_made, num(i, u, 1))
                if not first(i, u, 2):
                    pool.wait_ge(added[u % 2], sums_done(i, u - 2))
                pool.sem_inc(passed, 1)
                pool.indirect_dma_start(out=sums[u % 2],
                                        out_offset=bass.IndirectOffsetOnAxis(ap=row[u % NR][:, ROW - 1:ROW].bitcast(U32), axis=0),
                                        in_=y[u % NY][:, :], in_offset=None, compute_op=ALU.add).then_inc(added[u % 2], 16)

            program(pool, ((0, add),))
            for u in range(2):
                pool.wait_ge(added[u], 16 * SLOT_TILES // 2)

        @block.tensor
        def _(pe):
            for s_ in (x_turned, h_done, h_turned, y_done):
                pe.sem_inc(s_, BASE)
            pe.wait_ge(table_in, 16)

            def turn_x(i, u):
                pe.wait_ge(row_in[u % NR], i * 16 + (16 if u >= 0 else 0))
                pe.wait_ge(xt_made, num(i, u, -1))
                for c in range(LC):
                    mm = pe.transpose(psX[u % 2][:, c * P:(c + 1) * P], row[u % NR][:, c * P:(c + 1) * P], ident)
                mm.then_inc(x_turned, 1)

            expert = {}

            def load_expert(i, u):
                expert[u % NR] = pe.value_load(table[0:1, bass.ds(i * NR + u, 1)], min_val=0, max_val=E - 1)

            def product(i, u, w, out, lhs, out_free, lhs_made, done):
                e = expert[u % NR]
                pe.wait_ge(lhs_made, num(i, u, 1))
                pe.wait_ge(out_free, num(i, u, -1))
                for c in range(LC):
                    mm = pe.matmul(out[u % 2][:, 0:INTER], lhs[u % 2][:, c * P:(c + 1) * P],
                                   w[:, bass.ds(e * W + c * INTER, INTER)], start=(c == 0), stop=(c == LC - 1))
                mm.then_inc(done, 1)

            def hidden(i, u):
                if first(i, u, 1):
                    pe.wait_ge(w_in[0], 64)
                product(i, u, w1_sb, psH, xt, relu_made, xt_made, h_done)

            def turn_h(i, u):
                pe.wait_ge(relu_made, num(i, u, 1))
                pe.wait_ge(ht_made, num(i, u, -1))
                for c in range(IC):
                    mm = pe.transpose(psT[u % 2][:, c * P:(c + 1) * P], relu[u % 2][:, c * P:(c + 1) * P], ident)
                mm.then_inc(h_turned, 1)

            def result(i, u):
                if first(i, u, 1):
                    pe.wait_ge(w_in[1], 64)
                product(i, u, w2_sb, psY, ht, y_made, ht_made, y_done)

            program(pe, ((1, load_expert), (3, load_expert), (0, turn_x), (1, hidden), (2, turn_h), (3, result)))


def combine(nc, fc2, cst, sums, partial, out):
    R = 4
    with ExitStack() as ctx:
        def sb(name, shape, dt=F32):
            return ctx.enter_context(nc.sbuf_tensor(name, shape, dt))

        def sem(name):
            return ctx.enter_context(nc.semaphore(name))

        ident = cst[:, COL["ident"]]
        w = sb("c_w", [P, LC, D])
        a, z = ([sb(f"c_{n}{u}", [P, LAT]) for u in range(R)] for n in "az")
        y = [sb(f"c_y{u}", [P, LAT]) for u in range(2)]
        yt = [sb(f"c_yt{u}", [P, LAT]) for u in range(2)]
        part = [sb(f"c_part{u}", [P, D]) for u in range(R)]
        psT, psO = ([ctx.enter_context(nc.psum_tensor(f"c_ps{n}{u}", [P, S], F32)) for u in range(2)] for n in "TO")
        w_in = sem("c_w_in")
        sums_in, part_in, saved = ([sem(f"c_{n}{u}") for u in range(R)] for n in ("sums_in", "part_in", "saved"))
        y_made, turned, yt_made, done, added = (sem(f"c_{n}") for n in ("y_made", "turned", "yt_made", "done", "added"))
        block = ctx.enter_context(nc.Block())

        @block.sync
        def _(sp):
            sp.dma_start(w[:, :, :].rearrange("p c n -> p (c n)"), fc2).then_inc(w_in, 16)
            for s_ in saved:
                sp.sem_inc(s_, 16 * BASE)
            with sp.Fori(0, G // R) as i:
                for u in range(R):
                    rows = bass.ds(i * R * P + u * P, P)
                    sp.wait_ge(y_made, at(i, R, u + 1 - R))
                    sp.dma_start(a[u][:, :], sums[0][rows, :]).then_inc(sums_in[u], 16)
                    sp.dma_start(z[u][:, :], sums[1][rows, :]).then_inc(sums_in[u], 16)
                    sp.wait_ge(saved[u], i * 16 + 16 * BASE)
                    sp.dma_start(part[u][:, :], partial[rows, :]).then_inc(part_in[u], 16)

        @block.scalar
        def _(act):
            act.sem_inc(yt_made, BASE)
            with act.Fori(0, G // R) as i:
                for u in range(R):
                    act.wait_ge(turned, at(i, R, u + 1))
                    act.wait_ge(done, at(i, R, u - 1))
                    nc.scalar.activation(yt[u % 2][:, :], psT[u % 2][:, 0:LAT], ACT.Copy).then_inc(yt_made, 1)
                    act.wait_ge(added, at(i, R, u + 1))
                    act.dma_start(out[bass.ds(i * R * P + u * P, P), :], part[u][:, :]).then_inc(saved[u], 16)
            for u in range(R):
                act.wait_ge(saved[u], 16 * (BASE + G // R))

        @block.vector
        def _(dve):
            dve.sem_inc(y_made, BASE)
            dve.sem_inc(added, BASE)
            with dve.Fori(0, G // R) as i:
                for u in range(R):
                    dve.wait_ge(sums_in[u], i * 32 + 32)
                    dve.wait_ge(turned, at(i, R, u - 1))
                    nc.vector.tensor_tensor(y[u % 2][:, :], a[u][:, :], z[u][:, :], ALU.add).then_inc(y_made, 1)
                    dve.wait_ge(done, at(i, R, u + 1))
                    dve.wait_ge(part_in[u], i * 16 + 16)
                    nc.vector.tensor_tensor(part[u][:, :], psO[u % 2][:, :], part[u][:, :], ALU.add).then_inc(added, 1)

        @block.tensor
        def _(pe):
            pe.sem_inc(turned, BASE)
            pe.sem_inc(done, BASE)
            pe.wait_ge(w_in, 16)
            with pe.Fori(0, G // R) as i:
                for u in range(R):
                    pe.wait_ge(y_made, at(i, R, u + 1))
                    pe.wait_ge(yt_made, at(i, R, u - 1))
                    for c in range(LC):
                        mm = pe.transpose(psT[u % 2][:, c * P:(c + 1) * P], y[u % 2][:, c * P:(c + 1) * P], ident)
                    mm.then_inc(turned, 1)
                    pe.wait_ge(yt_made, at(i, R, u + 1))
                    pe.wait_ge(added, at(i, R, u - 1))
                    for c in range(LC):
                        mm = pe.matmul(psO[u % 2][:, :], yt[u % 2][:, c * P:(c + 1) * P], w[:, c, :],
                                       start=(c == 0), stop=(c == LC - 1))
                    mm.then_inc(done, 1)

def constant_table():
    c = np.zeros((P, NCONST), np.float32)
    p = np.arange(P)
    c[:, COL["ident"]] = np.eye(P)
    c[:, COL["tri"]] = np.triu(np.ones((P, P)), 1)
    col = np.arange(S)[None] - (S - P)
    c[:, COL["mask"]] = np.where(col > p[:, None], np.float32(1e38), 0)
    f = np.float32
    inv_freq = f(1) / f(10000) ** (np.arange(0, HD, 2, dtype=f) / f(HD))
    t = np.arange(S, dtype=f)
    freqs = (t[:, None] * inv_freq[None]).astype(f)
    base = ((np.arange(0, HD, 2, dtype=f) + f(0.4 * HD)) / f(1.4 * HD)).astype(f)
    xs = (base[None] ** ((t - S // 2) / f(128))[:, None]).astype(f)
    d = p % HD
    cos, sin, xs = (np.asarray(a[:, d % (HD // 2)].T, np.float64) for a in (np.cos(freqs.astype(np.float64)), np.sin(freqs.astype(np.float64)), xs))
    sign = np.where(d < HD // 2, -1.0, 1.0)[:, None]
    w = float(f(HD ** -0.5))
    c[:, COL["cosq"]], c[:, COL["sinq"]] = -w * cos * xs, -w * sign * sin * xs
    c[:, COL["cosk"]], c[:, COL["sink"]] = w * cos / xs, w * sign * sin / xs
    c[:, COL["token"]] = np.arange(G)[None] * P + p[:, None]
    c[:, COL["earlier"]] = np.tril(np.ones((NG, NG)), -1).reshape(1, -1)
    c[:, COL["tile"]] = np.arange(3)[None] + 3 * p[:, None]
    c[:, COL["lane"]] = p[:, None]
    c[:, COL["spare"]] = T + p[:, None]
    return c


def build(nc, x, w_fc1_gate, gate_bias, wq, wkv, wproj, bproj, wup, wdown, w1, w2, wfc2, consts, out):
    xnt_hi = nc.dram_tensor("xnt_hi", (B + 1, P, KC, S), F32, kind="Internal").ap()
    xnt_lo = nc.dram_tensor("xnt_lo", (B + 1, P, KC, S), F32, kind="Internal").ap()
    xlat = nc.dram_tensor("xlat", (T, LAT), F32, kind="Internal").ap()
    slot_rows = nc.dram_tensor("slot_rows", (SLOTS, ROW), F32, kind="Internal").ap()
    experts_dram = nc.dram_tensor("tile_experts", (3 * P,), I32, kind="Internal").ap()
    sums = [nc.dram_tensor(f"sums{u}", (T + SPARE, LAT), F32, kind="Internal").ap() for u in range(2)]
    partial = nc.dram_tensor("partial", (T, D), F32, kind="Internal").ap()
    with ExitStack() as ctx:
        cst = ctx.enter_context(nc.sbuf_tensor("cst", [P, NCONST], F32))
        with ExitStack() as inner:
            def sb(name, shape, dt=F32):
                return inner.enter_context(nc.sbuf_tensor(name, shape, dt))

            weights_sb = sb("weights", [P, G, E])
            slots_sb = sb("slots", [P, G, TOPK], U32)
            pads_sb = sb("pads", [P, E], U32)
            with nc.semaphore("cst_in") as cst_in, nc.Block() as block:
                @block.sync
                def _(sp):
                    sp.dma_start(cst[:, :], consts).then_inc(cst_in, 16)
                    sp.wait_ge(cst_in, 16)
            front(nc, x, w_fc1_gate, gate_bias, xnt_hi, xnt_lo, xlat, cst, weights_sb, slots_sb, pads_sb, experts_dram, sums)
            halves = {n: tuple(sb(f"{n}_{h}", [P, w.shape[1]], F32R) for h in ("hi", "lo"))
                      for n, w in (("wq", wq), ("wkv", wkv), ("wup", wup), ("wdown", wdown))}
            halves = {n: tuple(a[:, :] for a in pair) for n, pair in halves.items()}
            proj = sb("proj", [P, KC, D])
            with nc.semaphore("proj_in") as proj_in, nc.Block() as block:
                @block.sync
                def _(sp):
                    sp.dma_start(proj[:, :, :].rearrange("p c n -> p (c n)"), wproj).then_inc(proj_in, 16)
                    sp.wait_ge(proj_in, 16)
            split_weights(nc, [(w, *halves[n]) for n, w in (("wkv", wkv), ("wq", wq), ("wup", wup), ("wdown", wdown))])
            middle(nc, x, bproj, xnt_hi, xnt_lo, xlat, halves["wq"], halves["wkv"], proj, halves["wup"], halves["wdown"],
                   cst, weights_sb, slots_sb, pads_sb, slot_rows, partial)
        experts(nc, w1, w2, cst, experts_dram, slot_rows, sums)
        combine(nc, wfc2, cst, sums, partial, out)


def columns(w, chunks):
    return np.ascontiguousarray(w.reshape(chunks, P, -1).transpose(1, 0, 2).reshape(P, -1))


def per_expert(w):
    w = w.transpose(0, 2, 1).reshape(E, LC, P, -1)
    return np.ascontiguousarray(w.transpose(2, 0, 1, 3).reshape(P, -1))


def kernel(L0_attn_hidden_states, L0_attn_w_q, L0_attn_w_kv, L0_attn_w_proj, L0_attn_b_proj, L0_ffn_gate_w,
           L0_ffn_gate_bias, L0_ffn_fc1_w, L0_ffn_fc2_w, L0_ffn_w1, L0_ffn_w2, L0_ffn_shared_up_w,
           L0_ffn_shared_down_w):
    import concourse.bacc as bacc
    from concourse.bass_utils import run_bass_kernel_spmd

    def a(v):
        return np.asarray(v)

    kv = a(L0_attn_w_kv)
    arrays = {
        "x": np.ascontiguousarray(a(L0_attn_hidden_states).reshape(T, D)),
        "w_fc1_gate": columns(np.concatenate([a(L0_ffn_fc1_w).T, a(L0_ffn_gate_w).T], 1), KC).reshape(P, KC, FG),
        "gate_bias": a(L0_ffn_gate_bias),
        "wq": columns(a(L0_attn_w_q).T, KC),
        "wkv": columns(np.concatenate([kv[:HD], kv[:HD], kv[:HD], kv[HD:]], 0).T, KC),
        "wproj": columns(a(L0_attn_w_proj).T, KC),
        "bproj": a(L0_attn_b_proj),
        "wup": columns(a(L0_ffn_shared_up_w).T, KC),
        "wdown": columns(a(L0_ffn_shared_down_w).T, SC),
        "w1": per_expert(a(L0_ffn_w1)),
        "w2": per_expert(a(L0_ffn_w2)),
        "wfc2": columns(a(L0_ffn_fc2_w).T, LC),
        "consts": constant_table(),
    }
    nc = bacc.Bacc("TRN2", target_bir_lowering=False, num_devices=1)
    aps = [nc.dram_tensor(f"in_{n}", v.shape, F32, kind="ExternalInput").ap() for n, v in arrays.items()]
    out = nc.dram_tensor("out", (T, D), F32, kind="ExternalOutput").ap()
    build(nc, *aps, out)
    r = run_bass_kernel_spmd(nc, [{f"in_{n}": v for n, v in arrays.items()}], core_ids=[0])
    return r.results[0]["out"].reshape(B, S, D)
```

```python
import numpy as np
import concourse.bass as bass
from concourse import mybir
from contextlib import ExitStack

F32 = mybir.dt.float32
F32R = mybir.dt.float32r
U32 = mybir.dt.uint32
I32 = mybir.dt.int32
ALU = mybir.AluOpType
ACT = mybir.ActivationFunctionType
AX = mybir.AxisListType

P = 128
B, S, D = 8, 512, 512
T = B * S
TB = S // P
G = T // P
KC = D // P
NH, HD = 16, 32
LAT, INTER, E = 256, 256, 32
NG, GE = 4, 8
TOPG, TOPK = 2, 8
SH = 1024
LC, IC, SC = LAT // P, INTER // P, SH // P
ROUTED_SCALE = 2.5
EPS = 1e-5
FG = LAT + E
FULL_TILES = T * TOPK // P
SLOT_TILES = FULL_TILES + E
SLOTS = SLOT_TILES * P
ROW = LAT + E + 1
SPARE = P
BIG = 3.0e38
BASE = 16

WIDTHS = dict(ident=P, tri=P, mask=S, cosq=S, sinq=S, cosk=S, sink=S, token=G, earlier=NG * NG, tile=3, lane=1, spare=1)
COL, _at = {}, 0
for _n, _w in WIDTHS.items():
    COL[_n] = slice(_at, _at + _w)
    _at += _w
NCONST = _at


def at(i, per, n):
    return i * per + (BASE + n)


def three(pe, out, lhs, rhs, first, last):
    (lh, ll), (rh, rl) = lhs, rhs
    pe.matmul(out, ll, rh, start=first, stop=False)
    pe.matmul(out, lh, rl, start=False, stop=False)
    return pe.matmul(out, lh, rh, start=False, stop=last)


def pipeline(eng, stages, turns, per):
    for s in range(per):
        for lag, step in stages:
            if s >= lag:
                step(0, s - lag)
    with eng.Fori(1, turns) as i:
        for s in range(per):
            for lag, step in stages:
                step(i, s - lag)
    for s in range(max(lag for lag, _ in stages)):
        for lag, step in stages:
            if s < lag:
                step(turns, s - lag)


def front(nc, x, consts, fc1g, xnt_hi, xnt_lo, xlat, cst, logits):
    with ExitStack() as ctx:
        def sb(name, shape, dt=F32):
            return ctx.enter_context(nc.sbuf_tensor(name, shape, dt))

        def sem(name):
            return ctx.enter_context(nc.semaphore(name))

        R = 2
        ident = cst[:, COL["ident"]]
        wst = sb("f_wst", [P, KC, FG])
        whi = sb("f_whi", [P, KC, FG], F32R)
        wlo = sb("f_wlo", [P, KC, FG], F32R)
        xt = [sb(f"f_xt{u}", [P, TB, D]) for u in range(R)]
        xn = sb("f_xn", [P, TB, D])
        hi = [sb(f"f_hi{u}", [P, KC, S], F32R) for u in range(R)]
        lo = [sb(f"f_lo{u}", [P, KC, S], F32R) for u in range(R)]
        xl = [sb(f"f_xl{u}", [P, TB, FG]) for u in range(R)]
        stats = sb("f_stats", [P, TB, 6])
        mv = sb("f_mv", [P, TB, 2])
        veps = sb("f_veps", [P, TB])
        half = sb("f_half", [P, TB])
        tmp = sb("f_tmp", [P, TB])
        rstd = sb("f_rstd", [P, TB])
        pt = [ctx.enter_context(nc.psum_tensor(f"f_pt{c}", [P, S], F32)) for c in range(KC)]
        pf = [ctx.enter_context(nc.psum_tensor(f"f_pf{i}", [P, S], F32)) for i in range(TB)]

        passed = sem("f_passed")
        w_in, ident_in, cst_in = sem("f_w_in"), sem("f_ident_in"), sem("f_cst_in")
        x_in = [sem(f"f_x_in{u}") for u in range(R)]
        chain = sem("f_dve_chain")
        whi_made, wlo_made = sem("f_whi_made"), sem("f_wlo_made")
        veps_made, half_made = sem("f_veps_made"), sem("f_half_made")
        xn_made, xnt_done = sem("f_xn_made"), sem("f_xnt_done")
        hi_made, lo_made = sem("f_hi_made"), sem("f_lo_made")
        fc_done, xl_made, lg_made = sem("f_fc_done"), sem("f_xl_made"), sem("f_lg_made")
        xnt_saved = [sem(f"f_xnt_saved{u}") for u in range(R)]
        xl_saved = [sem(f"f_xl_saved{u}") for u in range(R)]
        block = ctx.enter_context(nc.Block())

        def after(i, u, per, n):
            return i * (R * per) + (u * per + BASE + n)

        def stored(i, u):
            return i * 32 + (16 * BASE + 32 * (u // R + 1))

        def xl_stored(i, u):
            return i * 16 + (16 * BASE + 16 * (u // R + 1))

        def first(i):
            return isinstance(i, int) and i == 0

        @block.sync
        def _(sp):
            for s_ in xnt_saved:
                sp.sem_inc(s_, 16 * BASE)

            def load(i, u):
                if not first(i):
                    sp.wait_ge(xn_made, after(i, u - R, TB, TB))
                sp.dma_start(xt[u][:, :, :], x[bass.ds(i * R * S + u * S, S), :].rearrange("(i p) d -> p i d", p=P)
                             ).then_inc(x_in[u], 16)

            def store_halves(i, u):
                sp.wait_ge(lo_made, after(i, u, KC, KC))
                for half_of, to in ((hi, xnt_hi), (lo, xnt_lo)):
                    sp.dma_start(to[bass.ds(i * R + u, 1)].rearrange("a p c s -> (a p) c s"),
                                 half_of[u % R][:, :, :].bitcast(F32)).then_inc(xnt_saved[u % R], 16)

            pipeline(sp, ((0, load), (2, store_halves)), B // R, R)
            for u in range(R):
                sp.wait_ge(xnt_saved[u], stored(B // R - 1, u))
                sp.wait_ge(xl_saved[u], xl_stored(B // R - 1, u))

        @block.scalar
        def _(act):
            for s_ in (hi_made, half_made, xl_made):
                act.sem_inc(s_, BASE)
            for s_ in xl_saved:
                act.sem_inc(s_, 16 * BASE)
            act.dma_start(wst[:, :, :], fc1g).then_inc(w_in, 16)
            act.dma_start(ident, consts[:, COL["ident"]]).then_inc(ident_in, 16)
            act.dma_start(cst[:, P:NCONST], consts[:, P:NCONST]).then_inc(cst_in, 16)
            act.wait_ge(w_in, 16)
            nc.scalar.activation(whi[:, :, :], wst[:, :, :], ACT.Copy).then_inc(whi_made, 1)

            def root(i, u):
                act.wait_ge(veps_made, after(i, u, 1, 1))
                nc.scalar.activation(half[:, :], veps[:, :], ACT.Sqrt, scale=0.25).then_inc(half_made, 1)

            def high(i, u):
                act.wait_ge(xnt_done, after(i, u, TB, TB))
                if not first(i):
                    act.wait_ge(xnt_saved[u % R], stored(i, u - R))
                act.wait_ge(fc_done, after(i, u - R, TB, TB))
                for c in range(KC):
                    nc.scalar.activation(hi[u % R][:, c, :], pt[c][:, :], ACT.Copy).then_inc(hi_made, 1)

            def latent(i, u):
                if not first(i):
                    act.wait_ge(xl_saved[u % R], xl_stored(i, u - R))
                act.wait_ge(lg_made, after(i, u - R, TB, TB))
                for t in range(TB):
                    act.wait_ge(fc_done, after(i, u, TB, t + 1))
                    nc.scalar.activation(xl[u % R][:, t, :], pf[t][:, 0:FG], ACT.Copy).then_inc(xl_made, 1)
                act.wait_ge(xl_made, after(i, u, TB, TB))
                act.dma_start(xlat[bass.ds(i * R * S + u * S, S), :].rearrange("(i p) l -> p i l", p=P),
                              xl[u % R][:, :, 0:LAT]).then_inc(xl_saved[u % R], 16)

            pipeline(act, ((0, root), (1, high), (2, latent)), B // R, R)
            act.wait_ge(cst_in, 16)

        @block.tensor
        def _(pe):
            pe.sem_inc(xnt_done, BASE)
            pe.sem_inc(fc_done, BASE)
            pe.wait_ge(ident_in, 16)

            def turn(i, u):
                pe.wait_ge(lo_made, after(i, u, KC, 0))
                for t in range(TB):
                    pe.wait_ge(xn_made, after(i, u, TB, t + 1))
                    for c in range(KC):
                        mm = pe.transpose(pt[c][:, t * P:(t + 1) * P], xn[:, t, c * P:(c + 1) * P], ident)
                    mm.then_inc(xnt_done, 1)

            def multiply(i, u):
                if first(i) and u == 0:
                    pe.wait_ge(wlo_made, 1)
                pe.wait_ge(lo_made, after(i, u, KC, KC))
                for t in range(TB):
                    pe.wait_ge(xl_made, after(i, u - 1, TB, t + 1))
                    for c in range(KC):
                        tok = slice(t * P, (t + 1) * P)
                        mm = three(pe, pf[t][:, 0:FG], (hi[u % R][:, c, tok], lo[u % R][:, c, tok]),
                                   (whi[:, c, :], wlo[:, c, :]), c == 0, c == KC - 1)
                    mm.then_inc(fc_done, 1)

            pipeline(pe, ((1, turn), (2, multiply)), B // R, R)

        @block.vector
        def _(dve):
            for s_ in (veps_made, xn_made, lo_made, lg_made, chain):
                dve.sem_inc(s_, BASE)
            NC = 3 * TB

            def statistics(i, u):
                dve.wait_ge(x_in[u], i * 16 + 16)
                for t in range(TB):
                    nc.vector.bn_stats(stats[:, t, :], xt[u][:, t, :]).then_inc(chain, 1)
                dve.wait_ge(chain, after(i, u, NC, 4))
                dve.wait_ge(xn_made, after(i, u, TB, 0))
                dve.sem_inc(passed, 1)
                for t in range(TB):
                    nc.vector.bn_aggr(mv[:, t, :], stats[:, t, :]).then_inc(chain, 1)
                dve.wait_ge(chain, after(i, u, NC, 8))
                nc.vector.tensor_scalar(veps[:, :], mv[:, :, 1], EPS, None, ALU.add).then_inc(veps_made, 1)

            def normalise(i, u):
                dve.wait_ge(half_made, after(i, u, 1, 1))
                dve.wait_ge(veps_made, after(i, u, 1, 1))
                nc.vector.reciprocal(tmp[:, :], half[:, :]).then_inc(chain, 1)
                dve.wait_ge(chain, after(i, u, NC, 9))
                nc.vector.tensor_tensor(tmp[:, :], tmp[:, :], veps[:, :], ALU.mult).then_inc(chain, 1)
                dve.wait_ge(chain, after(i, u, NC, 10))
                nc.vector.scalar_tensor_tensor(out=tmp[:, :], in0=tmp[:, :], scalar=0.25, in1=half[:, :],
                                               op0=ALU.mult, op1=ALU.add).then_inc(chain, 1)
                dve.wait_ge(chain, after(i, u, NC, 11))
                nc.vector.reciprocal(rstd[:, :], tmp[:, :]).then_inc(chain, 1)
                dve.wait_ge(chain, after(i, u, NC, 12))
                for t in range(TB):
                    dve.wait_ge(xnt_done, after(i, u, TB, t + 1 - TB))
                    nc.vector.tensor_scalar(xn[:, t, :], xt[u][:, t, :], mv[:, t, 0:1], rstd[:, t:t + 1],
                                            ALU.subtract, ALU.mult).then_inc(xn_made, 1)

            def low(i, u):
                dve.wait_ge(fc_done, after(i, u - R, TB, TB))
                if not first(i):
                    dve.wait_ge(xnt_saved[u % R], stored(i, u - R))
                for c in range(KC):
                    dve.wait_ge(hi_made, after(i, u, KC, c + 1))
                    nc.vector.tensor_tensor(lo[u % R][:, c, :], pt[c][:, :], hi[u % R][:, c, :].bitcast(F32),
                                            ALU.subtract).then_inc(lo_made, 1)

            def copy_logits(i, u):
                for t in range(TB):
                    dve.wait_ge(xl_made, after(i, u, TB, t + 1))
                    nc.vector.tensor_copy(logits[:, bass.ds(i * R * TB + (u * TB + t), 1), :],
                                          xl[u % R][:, t:t + 1, LAT:FG]).then_inc(lg_made, 1)

            dve.wait_ge(whi_made, 1)
            nc.vector.tensor_tensor(wlo[:, :, :], wst[:, :, :], whi[:, :, :].bitcast(F32), ALU.subtract).then_inc(wlo_made, 1)
            pipeline(dve, ((0, statistics), (1, low), (0, normalise), (2, copy_logits)), B // R, R)


def routing(nc, xnt_hi, xnt_lo, xh, xlo, bias, cst, logits, weights_sb, slots_sb, pads_sb,
            empty, xs, experts_dram, halves, proj, wproj):
    with ExitStack() as ctx:
        def sb(name, shape, dt=F32):
            return ctx.enter_context(nc.sbuf_tensor(name, shape, dt))

        def sem(name):
            return ctx.enter_context(nc.semaphore(name))

        R, W = 4, 2048
        pieces = []
        for dram, hi, lo in halves:
            for a in range(0, hi.shape[1], W):
                z = min(hi.shape[1], a + W)
                pieces.append((dram[:, a:z], hi[:, a:z], lo[:, a:z], z - a))
        stage = sb("r_stage", [P, R, W])
        bia = sb("r_bias", [P, E])
        score = sb("r_score", [P, G, E])
        biased = sb("r_biased", [P, G, E])
        equal = sb("r_equal", [P, G, E])
        other = sb("r_other", [P, G, E])
        picked_r = sb("r_picked", [P, G, E], F32R)
        picked = picked_r[:, :, :].bitcast(F32)
        tri_r = sb("r_tri", [P, P], F32R)
        first_g = sb("r_first", [P, G, NG])
        second_g = sb("r_second", [P, G, NG])
        twice_g = sb("r_twice", [P, G, NG])
        beats = sb("r_beats", [P, G, NG, NG])
        ties = sb("r_ties", [P, G, NG, NG])
        top8 = sb("r_top8", [P, G, TOPK])
        token_sum = sb("r_token_sum", [P, G])
        ones = sb("r_ones", [P, P])
        ones_r = sb("r_ones_r", [P, P], F32R)
        before = [sb(f"r_before{i}", [P, G, E]) for i in range(2)]
        count = sb("r_count", [P, E])
        count_i = sb("r_count_i", [P, E], I32)
        tiles = [sb(f"r_tiles{i}", [P, E]) for i in range(2)]
        start = sb("r_start", [P, E])
        end = sb("r_end", [P, E])
        pad = [sb(f"r_pad{i}", [P, E]) for i in range(2)]
        owner = sb("r_owner", [P, 3, E])
        expert_f = sb("r_expert_f", [P, 3])
        expert_i = sb("r_expert_i", [P, 3], I32)
        pt = [ctx.enter_context(nc.psum_tensor(f"r_pt{c}", [P, S], F32)) for c in range(4)]
        landed = [sem(f"r_landed{r}") for r in range(R)]
        hi_made, lo_made, proj_in = sem("r_hi_made"), sem("r_lo_made"), sem("r_proj_in")
        chain, b_in, exp_made, picked_made = sem("r_dve_chain"), sem("r_b_in"), sem("r_exp_made"), sem("r_picked_made")
        counted, ones_made, rounded, x_in = sem("r_counted"), sem("r_ones_made"), sem("r_rounded"), sem("r_x_in")
        empty_made, tail_sent = sem("r_empty_made"), sem("r_tail_sent")
        expert_made, expert_saved, copied = sem("r_expert_made"), sem("r_expert_saved"), sem("r_copied")
        block = ctx.enter_context(nc.Block())

        @block.sync
        def _(sp):
            sp.dma_start(bia[:, :], bias.partition_broadcast(P)).then_inc(b_in, 16)
            for to, src in ((xh, xnt_hi), (xlo, xnt_lo)):
                sp.dma_start(to[:, :, :].bitcast(F32), src[0]).then_inc(x_in, 16)
            for k, (dram, hi, lo, n) in enumerate(pieces):
                if k >= R:
                    sp.wait_ge(lo_made, k - R + 1)
                sp.dma_start(stage[:, k % R, 0:n], dram).then_inc(landed[k % R], 16)
            sp.dma_start(proj, wproj).then_inc(proj_in, 16)
            for halves_of in (xnt_hi, xnt_lo):
                sp.dma_start(halves_of[B], halves_of[0]).then_inc(copied, 16)
            sp.wait_ge(expert_made, 1)
            sp.dma_start(experts_dram.rearrange("(p q) -> p q", p=P), expert_i[:, :]).then_inc(expert_saved, 16)
            sp.wait_ge(expert_saved, 16)
            sp.wait_ge(proj_in, 16)
            sp.wait_ge(copied, 32)
            sp.wait_ge(x_in, 32)

        @block.gpsimd
        def _(pool):
            nc.gpsimd.memset(empty[:, :], 0.0).then_inc(empty_made, 1)
            pool.wait_ge(empty_made, 1)
            nc.gpsimd.tensor_copy(empty[:, ROW - 1:ROW].bitcast(U32), cst[:, COL["spare"]]).then_inc(empty_made, 1)
            pool.wait_ge(empty_made, 2)
            pool.dma_start(xs[FULL_TILES * P:SLOTS, :].rearrange("(a p) r -> p a r", p=P),
                           empty[:, :].unsqueeze(1).broadcast_to([P, E, ROW])).then_inc(tail_sent, 16)
            for k, (dram, hi, lo, n) in enumerate(pieces):
                pool.wait_ge(hi_made, k + 1)
                nc.gpsimd.tensor_tensor(lo, stage[:, k % R, 0:n], hi.bitcast(F32), ALU.subtract).then_inc(lo_made, 1)
            pool.wait_ge(tail_sent, 16)

        @block.scalar
        def _(act):
            nc.scalar.activation(score[:, :, :], logits[:, :, :], ACT.Exp, scale=-1.0).then_inc(exp_made, 1)
            act.wait_ge(ones_made, 1)
            nc.scalar.activation(ones_r[:, :], ones[:, :], ACT.Copy).then_inc(rounded, 1)
            nc.scalar.activation(tri_r[:, :], cst[:, COL["tri"]], ACT.Copy).then_inc(rounded, 1)
            for k, (dram, hi, lo, n) in enumerate(pieces):
                act.wait_ge(landed[k % R], 16 * (k // R + 1))
                nc.scalar.activation(hi, stage[:, k % R, 0:n], ACT.Copy).then_inc(hi_made, 1)

        @block.tensor
        def _(pe):
            pe.wait_ge(picked_made, 1)
            pe.wait_ge(rounded, 2)
            for h in range(2):
                half_g = slice(h * G // 2, (h + 1) * G // 2)
                pe.matmul(pt[h][:, :], tri_r[:, :], picked_r[:, half_g, :], start=True, stop=True)
                pe.matmul(pt[2 + h][:, :], ones_r[:, :], picked_r[:, half_g, :], start=True, stop=True).then_inc(counted, 1)

        @block.vector
        def _(dve):
            linked = [0]

            def link(ins):
                linked[0] += 1
                ins.then_inc(chain, 1)
                dve.wait_ge(chain, linked[0])

            def grouped(a):
                return a[:, :, :].rearrange("p g (n e) -> p (g n) e", e=GE)

            def per_group(a):
                return a[:, :, :].rearrange("p g n -> p (g n)")

            nc.vector.memset(ones[:, :], 1.0).then_inc(ones_made, 1)
            dve.wait_ge(exp_made, 1)
            dve.wait_ge(b_in, 16)
            link(nc.vector.tensor_scalar(score[:, :, :], score[:, :, :], 1.0, None, ALU.add))
            link(nc.vector.reciprocal(score[:, :, :], score[:, :, :]))
            link(nc.vector.tensor_tensor(biased[:, :, :], score[:, :, :],
                                         bia[:, :].unsqueeze(1).broadcast_to([P, G, E]), ALU.add))
            link(nc.vector.tensor_reduce(per_group(first_g), grouped(biased), AX.X, ALU.max))
            link(nc.vector.tensor_tensor(grouped(equal), grouped(biased),
                                         per_group(first_g).unsqueeze(2).broadcast_to([P, G * NG, GE]), ALU.is_equal))
            link(nc.vector.scalar_tensor_tensor(out=grouped(other), in0=grouped(equal), scalar=-BIG, in1=grouped(biased),
                                                op0=ALU.mult, op1=ALU.add))
            link(nc.vector.tensor_reduce(per_group(second_g), grouped(other), AX.X, ALU.max))
            link(nc.vector.tensor_reduce(per_group(twice_g), grouped(equal), AX.X, ALU.add))
            link(nc.vector.tensor_scalar(per_group(twice_g), per_group(twice_g), 2.0, None, ALU.is_lt))
            link(nc.vector.scalar_tensor_tensor(out=per_group(twice_g), in0=per_group(twice_g), scalar=-BIG,
                                                in1=per_group(first_g), op0=ALU.mult, op1=ALU.add))
            link(nc.vector.tensor_tensor(per_group(second_g), per_group(second_g), per_group(twice_g), ALU.max))
            link(nc.vector.tensor_tensor(per_group(first_g), per_group(first_g), per_group(second_g), ALU.add))
            mine = first_g[:, :, :].unsqueeze(3).broadcast_to([P, G, NG, NG])
            theirs = first_g[:, :, :].unsqueeze(2).broadcast_to([P, G, NG, NG])
            earlier = (cst[:, COL["earlier"]].rearrange("p (a b) -> p a b", a=NG).unsqueeze(1)
                       .broadcast_to([P, G, NG, NG]))
            link(nc.vector.tensor_tensor(ties[:, :, :, :], theirs, mine, ALU.is_equal))
            link(nc.vector.tensor_tensor(ties[:, :, :, :], ties[:, :, :, :], earlier, ALU.mult))
            link(nc.vector.tensor_tensor(beats[:, :, :, :], theirs, mine, ALU.is_gt))
            link(nc.vector.tensor_tensor(beats[:, :, :, :], beats[:, :, :, :], ties[:, :, :, :], ALU.add))
            link(nc.vector.tensor_reduce(per_group(twice_g), beats[:, :, :, :].rearrange("p g a b -> p (g a) b"),
                                         AX.X, ALU.add))
            link(nc.vector.tensor_scalar(per_group(twice_g), per_group(twice_g), float(TOPG), -BIG, ALU.is_ge, ALU.mult))
            link(nc.vector.tensor_tensor(grouped(biased), grouped(biased),
                                         per_group(twice_g).unsqueeze(2).broadcast_to([P, G * NG, GE]), ALU.add))
            for g in range(G):
                last = nc.vector.max(top8[:, g, :], biased[:, g, :])
            link(last)
            for g in range(G):
                last = nc.vector.match_replace(out=other[:, g, :], in_to_replace=top8[:, g, :],
                                               in_values=biased[:, g, :], imm_value=BIG)
            link(last)
            link(nc.vector.tensor_tensor(picked_r[:, :, :], other[:, :, :], biased[:, :, :], ALU.not_equal))
            dve.sem_inc(picked_made, 1)
            link(nc.vector.tensor_tensor(score[:, :, :], score[:, :, :], picked[:, :, :], ALU.mult))
            link(nc.vector.tensor_reduce(token_sum[:, :], score[:, :, :], AX.X, ALU.add))
            link(nc.vector.reciprocal(token_sum[:, :], token_sum[:, :]))
            link(nc.vector.scalar_tensor_tensor(out=weights_sb[:, :, :], in0=score[:, :, :], scalar=ROUTED_SCALE,
                                                in1=token_sum[:, :].unsqueeze(2).broadcast_to([P, G, E]),
                                                op0=ALU.mult, op1=ALU.mult))
            dve.wait_ge(counted, 2)
            link(nc.vector.memset(before[0][:, 0, :], 0.0))
            for h in range(2):
                n = G // 2 - h
                link(nc.vector.tensor_copy(before[0][:, h * G // 2 + 1:h * G // 2 + 1 + n, :],
                                           pt[2 + h][:, 0:n * E].rearrange("p (g e) -> p g e", e=E)))
            now = 0
            for k in (1, 2, 4, 8, 16):
                a, z = before[now], before[1 - now]
                link(nc.vector.tensor_copy(z[:, 0:k, :], a[:, 0:k, :]))
                link(nc.vector.tensor_tensor(z[:, k:G, :], a[:, k:G, :], a[:, 0:G - k, :], ALU.add))
                now = 1 - now
            earlier_tiles = before[now]
            link(nc.vector.tensor_tensor(count[:, :], earlier_tiles[:, G - 1, :], pt[3][:, (G // 2 - 1) * E:G // 2 * E], ALU.add))
            link(nc.vector.tensor_scalar(count_i[:, :], count[:, :], float(P - 1), None, ALU.add))
            link(nc.vector.tensor_scalar(count_i[:, :], count_i[:, :], 7, None, ALU.logical_shift_right))
            link(nc.vector.tensor_copy(tiles[0][:, :], count_i[:, :]))
            link(nc.vector.tensor_copy(start[:, :], tiles[0][:, :]))
            now = 0
            for k in (1, 2, 4, 8, 16):
                a, z = tiles[now], tiles[1 - now]
                link(nc.vector.tensor_copy(z[:, 0:k], a[:, 0:k]))
                link(nc.vector.tensor_tensor(z[:, k:E], a[:, k:E], a[:, 0:E - k], ALU.add))
                now = 1 - now
            link(nc.vector.tensor_copy(end[:, :], tiles[now][:, :]))
            link(nc.vector.tensor_tensor(start[:, :], end[:, :], start[:, :], ALU.subtract))
            link(nc.vector.tensor_scalar(start[:, :], start[:, :], float(P), None, ALU.mult))
            link(nc.vector.tensor_tensor(other[:, :, :], earlier_tiles[:, :, :],
                                         start[:, :].unsqueeze(1).broadcast_to([P, G, E]), ALU.add))
            for h in range(2):
                gs = slice(h * G // 2, (h + 1) * G // 2)
                link(nc.vector.tensor_tensor(other[:, gs, :], other[:, gs, :],
                                             pt[h][:, :].rearrange("p (g e) -> p g e", e=E), ALU.add))
            link(nc.vector.scalar_tensor_tensor(out=other[:, :, :], in0=other[:, :, :], scalar=1.0, in1=picked[:, :, :],
                                                op0=ALU.add, op1=ALU.mult))
            for g in range(G):
                last = nc.vector.max(top8[:, g, :], other[:, g, :])
            link(last)
            link(nc.vector.tensor_scalar(slots_sb[:, :, :], top8[:, :, :], -1.0, None, ALU.add))
            link(nc.vector.tensor_tensor(pad[0][:, :], start[:, :], count[:, :], ALU.add))
            link(nc.vector.tensor_scalar(pad[0][:, :], pad[0][:, :], cst[:, COL["lane"]], None, ALU.add))
            link(nc.vector.scalar_tensor_tensor(out=pad[1][:, :], in0=end[:, :], scalar=float(P), in1=pad[0][:, :],
                                                op0=ALU.mult, op1=ALU.is_le))
            link(nc.vector.scalar_tensor_tensor(out=pad[0][:, :], in0=pad[1][:, :], scalar=float(2 * SLOTS),
                                                in1=pad[0][:, :], op0=ALU.mult, op1=ALU.add))
            link(nc.vector.tensor_copy(pads_sb[:, :], pad[0][:, :]))
            link(nc.vector.tensor_tensor(owner[:, :, :], end[:, :].unsqueeze(1).broadcast_to([P, 3, E]),
                                         cst[:, COL["tile"]].unsqueeze(2).broadcast_to([P, 3, E]), ALU.is_le))
            link(nc.vector.tensor_reduce(expert_f[:, :], owner[:, :, :], AX.X, ALU.add))
            link(nc.vector.tensor_scalar(expert_f[:, :], expert_f[:, :], float(E - 1), None, ALU.min))
            nc.vector.tensor_copy(expert_i[:, :], expert_f[:, :]).then_inc(expert_made, 1)

NSLOT = NH + 1
HC = NH // KC
SHALF = S // 2
ROWS = [3, 2, 1, 0]
SPC = [0, 128, 384, 768]
NSP = 10 * P
PTC = {0: (0, 0), 1: (512, 128), 3: (896, 384), 2: (1024, 256)}

def q_slot(n):
    return (n - 1) * HC


Q_AT = {q_slot(n): n for n in range(1, KC)}
U_ORDER = []
for _s in range(NH):
    U_ORDER.append(f"up{_s}")
    if _s in Q_AT:
        U_ORDER.append(f"q{Q_AT[_s]}")
U_ORDER += ["q0", "kv", "vt"]
QK_AT = {"q1": 0, "q2": 1, "q3": 2, "q0": 3, "kv": 4}
NQK = len(QK_AT)
NU = len(U_ORDER)
U_AT = {n: k for k, n in enumerate(U_ORDER)}


def middle(nc, x, bproj, xnt_hi, xnt_lo, xh, xlo, xlat, wq, wkv, wproj, wup, wdown, cst,
           weights_sb, slots_sb, pads_sb, empty, xs, sums, partial):
    with ExitStack() as ctx:
        def sb(name, shape, dt=F32):
            return ctx.enter_context(nc.sbuf_tensor(name, shape, dt))

        def sem(name):
            return ctx.enter_context(nc.semaphore(name))

        def pb(name):
            return ctx.enter_context(nc.psum_tensor(name, [P, S], F32))

        ident = cst[:, COL["ident"]]
        mask = cst[:, COL["mask"]]
        tables = {"q": (cst[:, COL["cosq"]], cst[:, COL["sinq"]]), "k": (cst[:, COL["cosk"]], cst[:, COL["sink"]])}
        (wq_hi, wq_lo), (wkv_hi, wkv_lo), (up_hi, up_lo), (down_hi, down_lo) = [
            [w.rearrange("p (c n) -> p c n", c=c) for w in pair]
            for pair, c in ((wq, KC), (wkv, KC), (wup, KC), (wdown, SC))]
        kv = sb("m_kv", [P, S])
        q = sb("m_q", [P, S])
        rot = sb("m_rot", [P, S])
        qhi = sb("m_qhi", [P, S], F32R)
        qlo = sb("m_qlo", [P, S], F32R)
        qs = sb("m_qs", [96, 2, HC, S], F32R)
        ks = sb("m_ks", [96, S], F32R)
        vpad = sb("m_vpad", [P, TB, 7 * HD])
        sc = sb("m_sc", [P, 2, NSP])
        low = sb("m_low", [P, 2, TB])
        total = sb("m_total", [P, 2, TB])
        inv = sb("m_inv", [P, 2, TB])
        pt = sb("m_pt", [P, 2, NSP])
        ot = sb("m_ot", [P, KC, S])
        relu = sb("m_relu", [P, SHALF])
        sq = sb("m_sq", [P, SHALF])
        sqhi = sb("m_sqhi", [P, 2, SHALF], F32R)
        sqlo = sb("m_sqlo", [P, 2, SHALF], F32R)
        res = sb("m_res", [P, TB, D])
        bp = sb("m_bp", [P, D])
        row = [sb(f"m_row{u}", [P, ROW]) for u in range(2)]
        idx = [sb(f"m_idx{u}", [P, TOPK], U32) for u in range(2)]
        psS = [pb(f"m_psS{i}") for i in range(2)]
        psT = [pb(f"m_psT{i}") for i in range(2)]
        psO, psU = pb("m_psO"), pb("m_psU")
        psY = [pb(f"m_psY{i}") for i in range(2)]

        dve_passed, pool_passed, sp_passed = sem("m_dve_passed"), sem("m_pool_passed"), sem("m_sp_passed")
        u_done, s_done, t_done, pv_done = sem("m_u_done"), sem("m_s_done"), sem("m_t_done"), sem("m_pv_done")
        y_step, y_done = sem("m_y_step"), sem("m_y_done")
        qk_copied, hi_made = sem("m_qk_copied"), sem("m_hi_made")
        exp_done, relu_made, sqhi_made = sem("m_exp_done"), sem("m_relu_made"), sem("m_sqhi_made")
        ta_out, tb_out, o_out = sem("m_ta_out"), sem("m_tb_out"), sem("m_o_out")
        rot_step, rotated, lo_made, v_made = sem("m_rot_step"), sem("m_rotated"), sem("m_lo_made"), sem("m_v_made")
        s_out, inv_made, scaled = sem("m_s_out"), sem("m_inv_made"), sem("m_scaled")
        sq_made, sqlo_made, res_made, y_out = sem("m_sq_made"), sem("m_sqlo_made"), sem("m_res_made"), sem("m_y_out")
        vpad_clear = sem("m_vpad_clear")
        xh_in, xlo_in, bp_in, res_in = sem("m_xh_in"), sem("m_xlo_in"), sem("m_bp_in"), sem("m_res_in")
        qs_in = [[sem(f"m_qs_in{u}_{j}") for j in range(HC)] for u in range(2)]
        saved = sem("m_saved")
        row_in = [sem(f"m_row_in{u}") for u in range(2)]
        idx_made = [sem(f"m_idx_made{u}") for u in range(2)]
        sent = [sem(f"m_sent{u}") for u in range(2)]
        zeroed = sem("m_zeroed")
        pads_sent = sem("m_pads_sent")
        block = ctx.enter_context(nc.Block())

        NQ = 3 * 16

        def stacked(b, c):
            return b * (2 * NQ) + (16 * BASE + NQ * (c // 2 + c % 2))

        def before(b, c):
            return (b, c - 1) if c else (b - 1, KC - 1)

        @block.sync
        def _(sp):
            def load_tokens(b, h):
                tok = slice(h * SHALF, (h + 1) * SHALF)
                for to, src, landed in ((xh, xnt_hi, xh_in), (xlo, xnt_lo, xlo_in)):
                    sp.dma_start(to[:, :, tok].bitcast(F32),
                                 src[bass.ds(b, 1)].rearrange("a p c s -> (a p) c s")[:, :, tok]).then_inc(landed, 16)

            def stack(b, c, turn):
                sp.wait_ge(hi_made, at(turn, NQK, QK_AT[f"q{c}"] + 1))
                sp.sem_inc(sp_passed, 1)
                sp.wait_ge(s_done, at(b, NH * TB, HC * TB * (c - 1)))

                def move(j, k, src):
                    sp.dma_start(qs[k * HD:(k + 1) * HD, c % 2, j, :].bitcast(F32),
                                 src[j * HD:(j + 1) * HD, :].bitcast(F32)).then_inc(qs_in[c % 2][j], 16)

                for j in range(HC):
                    move(j, 0, qhi)
                    move(j, 1, qhi)
                    if j == 0:
                        sp.wait_ge(lo_made, at(turn, NQK, QK_AT[f"q{c}"] + 1))
                    move(j, 2, qlo)

            for j in range(HC):
                sp.sem_inc(qs_in[0][j], 16 * BASE - NQ)
                sp.sem_inc(qs_in[1][j], 16 * BASE)
            sp.dma_start(bp[:, :], bproj.partition_broadcast(P)).then_inc(bp_in, 16)
            stack(0, 0, -1)
            with sp.Fori(0, B) as b:
                stack(b, 1, b)
                sp.wait_ge(saved, b * 16 + 16 * BASE)
                sp.dma_start(res[:, :, :], x[bass.ds(b * S, S), :].rearrange("(i p) d -> p i d", p=P)
                             ).then_inc(res_in, 16)
                stack(b, 2, b)
                sp.wait_ge(u_done, at(b, NU, U_AT["q3"] + 1))
                load_tokens(b + 1, 0)
                stack(b, 3, b)
                sp.wait_ge(u_done, at(b, NU, U_AT["up15"] + 1))
                load_tokens(b + 1, 1)
                stack(b + 1, 0, b)
            for landed, value in (*((a, stacked(B, 0)) for a in qs_in[0]), (xh_in, 32 * B), (xlo_in, 32 * B)):
                sp.wait_ge(landed, value)

        @block.gpsimd
        def _(pool):
            for e in range(E):
                pool.indirect_dma_start(out=xs, out_offset=bass.IndirectOffsetOnAxis(ap=pads_sb[:, e:e + 1], axis=0),
                                        in_=empty[:, :], in_offset=None, bounds_check=SLOTS - 1,
                                        oob_is_err=False).then_inc(pads_sent, 16)
            pool.wait_ge(pads_sent, 16 * E)
            for a in sums:
                pool.dma_start(a[T:T + SPARE, :], empty[:, 0:LAT]).then_inc(zeroed, 16)
            with pool.Fori(0, G // 2) as i:
                for a in sums:
                    pool.dma_start(a[bass.ds(i * 2 * P, 2 * P), :].rearrange("(g p) l -> p g l", p=P),
                                   empty[:, 0:LAT].unsqueeze(1).broadcast_to([P, 2, LAT])).then_inc(zeroed, 16)
                for u in range(2):
                    pool.dma_start(row[u][:, 0:LAT], xlat[bass.ds(i * 2 * P + u * P, P), :]).then_inc(row_in[u], 16)
                    nc.gpsimd.tensor_copy(row[u][:, LAT:LAT + E].unsqueeze(1),
                                          weights_sb[:, bass.ds(i * 2 + u, 1), :]).then_inc(idx_made[u], 1)
                    nc.gpsimd.tensor_copy(row[u][:, ROW - 1:ROW].bitcast(U32),
                                          cst[:, bass.ds(i * 2 + (COL["token"].start + u), 1)]).then_inc(idx_made[u], 1)
                    nc.gpsimd.tensor_copy(idx[u][:, :].unsqueeze(1),
                                          slots_sb[:, bass.ds(i * 2 + u, 1), :]).then_inc(idx_made[u], 1)
                for u in range(2):
                    pool.wait_ge(row_in[u], i * 16 + 16)
                    pool.wait_ge(idx_made[u], i * 3 + 3)
                    pool.sem_inc(pool_passed, 1)
                    for k in range(TOPK):
                        pool.indirect_dma_start(out=xs, out_offset=bass.IndirectOffsetOnAxis(ap=idx[u][:, k:k + 1], axis=0),
                                                in_=row[u][:, :], in_offset=None).then_inc(sent[u], 16)
                for u in range(2):
                    pool.wait_ge(sent[u], i * (16 * TOPK) + 16 * TOPK)
            pool.wait_ge(zeroed, 16 * len(sums) * (1 + G // 2))

        @block.scalar
        def _(act):
            for s_ in (exp_done, relu_made, sqhi_made, ta_out, tb_out, o_out):
                act.sem_inc(s_, BASE)
            act.sem_inc(qk_copied, BASE - 2)
            act.sem_inc(hi_made, BASE - 2)
            act.sem_inc(saved, 16 * BASE)

            def copy_out(b, name):
                act.wait_ge(u_done, at(b, NU, U_AT[name] + 1))
                if name == "kv":
                    act.wait_ge(v_made, at(b, 1, 0))
                    act.wait_ge(lo_made, at(b, NQK, QK_AT["kv"] + 1 - NQK))
                else:
                    act.wait_ge(lo_made, at(b, NQK, QK_AT[name]))
                nc.scalar.activation((kv if name == "kv" else q)[:, :], psU[:, :], ACT.Copy).then_inc(qk_copied, 1)

            def high(b, name):
                act.wait_ge(rotated, at(b, NQK, QK_AT[name] + 1))
                if name == "kv":
                    act.wait_ge(s_done, at(b, NH * TB, NH * TB))
                    nc.scalar.activation(ks[:, :], kv[0:96, :], ACT.Copy).then_inc(hi_made, 1)
                else:
                    c = int(name[1:])
                    bb, cc = before(b if c else b + 1, c)
                    for j in range(HC):
                        act.wait_ge(qs_in[cc % 2][j], stacked(bb, cc))
                    nc.scalar.activation(qhi[:, :], q[:, :], ACT.Copy).then_inc(hi_made, 1)

            for name in ("q0", "kv"):
                copy_out(-1, name)
            for name in ("q0", "kv"):
                high(-1, name)
            with act.Fori(0, B) as b:
                def exps(h, i):
                    k = h * TB + ROWS.index(i)
                    act.wait_ge(s_out, at(b, NH * TB, k + 1))
                    if i == ROWS[0]:
                        act.wait_ge(inv_made, at(b, NH, h - 1))
                    cols = sc[:, h % 2, SPC[i]:SPC[i] + (i + 1) * P]
                    nc.scalar.activation(cols, cols, ACT.Exp, bias=low[:, h % 2, i:i + 1], scale=-1.0,
                                         accum_out=total[:, h % 2, i:i + 1]).then_inc(exp_done, 1)

                def turned_out_b(h):
                    act.wait_ge(t_done, at(b, 3 * NH, 3 * h + 2))
                    nc.scalar.activation(pt[:, h % 2, 512:1024], psT[1][:, :], ACT.Copy).then_inc(tb_out, 1)

                def turned_out_a(h, c):
                    act.wait_ge(t_done, at(b, 3 * NH, 3 * h + (1 if c == 0 else 3)))
                    if c == 0:
                        act.wait_ge(pv_done, at(b, NH, h - 1))
                        nc.scalar.activation(pt[:, h % 2, 0:512], psT[0][:, :], ACT.Copy).then_inc(ta_out, 1)
                    else:
                        nc.scalar.activation(pt[:, h % 2, 1024:1280], psT[0][:, 0:256], ACT.Copy).then_inc(ta_out, 1)

                def shared(s):
                    act.wait_ge(u_done, at(b, NU, U_AT[f"up{s}"] + 1))
                    act.wait_ge(sq_made, at(b, NH, s))
                    act.wait_ge(sqhi_made, at(b, NH, s))
                    nc.scalar.activation(relu[:, :], psU[:, 0:SHALF], ACT.Relu).then_inc(relu_made, 1)
                    act.wait_ge(relu_made, at(b, NH, s + 1))
                    act.wait_ge(y_step, at(b, NH, s - 1))
                    nc.scalar.activation(sqhi[:, s % 2, :], relu[:, :], ACT.Square).then_inc(sqhi_made, 1)

                for s in range(NSLOT):
                    t = s - 1
                    if s < NH:
                        for i in ROWS[:3]:
                            exps(s, i)
                    if t >= 0:
                        turned_out_a(t, 0)
                        turned_out_b(t)
                    if s < NH:
                        exps(s, ROWS[3])
                    if s < NH:
                        shared(s)
                    if s - 2 in Q_AT:
                        high(b, f"q{Q_AT[s - 2]}")
                    if t >= 0:
                        turned_out_a(t, 2)
                    if s in Q_AT:
                        copy_out(b, f"q{Q_AT[s]}")
                    if s == NH:
                        copy_out(b, "q0")
                    if t >= 0 and t % HC == HC - 1:
                        act.wait_ge(pv_done, at(b, NH, t + 1))
                        act.wait_ge(y_done, at(b, 8, 0))
                        nc.scalar.activation(ot[:, t // HC, :], psO[:, :], ACT.Copy).then_inc(o_out, 1)
                high(b, "q0")
                copy_out(b, "kv")
                high(b, "kv")
                act.wait_ge(y_out, at(b, 8, 8))
                act.dma_start(partial[bass.ds(b * S, S), :].rearrange("(i p) d -> p i d", p=P),
                              res[:, :, :]).then_inc(saved, 16)
            act.wait_ge(saved, 16 * (BASE + B))

        @block.vector
        def _(dve):
            dve.sem_inc(rot_step, BASE - 2 * 3)
            dve.sem_inc(rotated, BASE - 2)
            dve.sem_inc(lo_made, BASE - 2)
            dve.sem_inc(v_made, BASE - 1)
            for s_ in (s_out, inv_made, scaled, sq_made, sqlo_made, res_made, y_out):
                dve.sem_inc(s_, BASE)
            nc.vector.memset(vpad[:, :, :], 0.0).then_inc(vpad_clear, 1)
            dve.wait_ge(vpad_clear, 1)

            def rotate(b, name, parts=(0, 1)):
                n = QK_AT[name]
                x_ = kv[0:96, :] if name == "kv" else q[:, :]
                r_ = rot[0:96, :] if name == "kv" else rot[:, :]
                cos, sin = (a[0:96, :] if name == "kv" else a for a in tables["k" if name == "kv" else "q"])
                if 0 in parts:
                    dve.wait_ge(qk_copied, at(b, NQK, n + 1))
                    dve.wait_ge(rotated, at(b, NQK, n))
                    dve.sem_inc(dve_passed, 1)
                    nc.vector.stream_shuffle(r_, x_, [(i + HD // 2) % HD for i in range(HD)]).then_inc(rot_step, 1)
                    dve.wait_ge(rot_step, at(b, 3 * NQK, 3 * n + 1))
                    nc.vector.tensor_tensor(x_, x_, cos, ALU.mult).then_inc(rot_step, 1)
                if 1 in parts:
                    nc.vector.tensor_tensor(r_, r_, sin, ALU.mult).then_inc(rot_step, 1)
                    dve.wait_ge(rot_step, at(b, 3 * NQK, 3 * n + 3))
                    nc.vector.tensor_tensor(x_, x_, r_, ALU.add).then_inc(rotated, 1)

            def low_part(b, name):
                dve.wait_ge(hi_made, at(b, NQK, QK_AT[name] + 1))
                dve.wait_ge(rotated, at(b, NQK, QK_AT[name] + 1))
                if name == "kv":
                    nc.vector.tensor_tensor(ks[HD:2 * HD, :], kv[HD:2 * HD, :], ks[HD:2 * HD, :].bitcast(F32),
                                            ALU.subtract).then_inc(lo_made, 1)
                else:
                    c = int(name[1:])
                    bb, cc = before(b if c else b + 1, c)
                    for j in range(HC):
                        dve.wait_ge(qs_in[cc % 2][j], stacked(bb, cc))
                    nc.vector.tensor_tensor(qlo[:, :], q[:, :], qhi[:, :].bitcast(F32), ALU.subtract).then_inc(lo_made, 1)

            def place_values(b):
                dve.wait_ge(u_done, at(b, NU, U_AT["vt"] + 1))
                dve.wait_ge(pv_done, at(b, NH, NH))
                nc.vector.tensor_copy(vpad[:, :, 3 * HD:4 * HD],
                                      psU[:, :].rearrange("p (t n) -> p t n", n=P)[:, :, 3 * HD:4 * HD]
                                      ).then_inc(v_made, 1)

            for name in ("q0", "kv"):
                rotate(-1, name)
            for name in ("q0", "kv"):
                low_part(-1, name)
            place_values(-1)
            with dve.Fori(0, B) as b:
                def mask_and_min(h, i):
                    k = h * TB + ROWS.index(i)
                    dve.wait_ge(s_done, at(b, NH * TB, k + 1))
                    if i == ROWS[0]:
                        dve.wait_ge(t_done, at(b, 3 * NH, 3 * (h - 1)))
                        dve.wait_ge(exp_done, at(b, NH * TB, TB * (h - 1)))
                        dve.wait_ge(scaled, at(b, NH, h - 1))
                    n = (i + 1) * P
                    dve.sem_inc(dve_passed, 1)
                    nc.vector.tensor_tensor_reduce(out=sc[:, h % 2, SPC[i]:SPC[i] + n], in0=psS[k % 2][:, 0:n],
                                                   in1=mask[:, S - n:S], scale=1.0, scalar=3.0e38, op0=ALU.add,
                                                   op1=ALU.min, accum_out=low[:, h % 2, i:i + 1]).then_inc(s_out, 1)

                def scale(h):
                    dve.wait_ge(exp_done, at(b, NH * TB, TB * (h + 1)))
                    nc.vector.reciprocal(inv[:, h % 2, :], total[:, h % 2, :]).then_inc(inv_made, 1)
                    dve.wait_ge(inv_made, at(b, NH, h + 1))
                    for i in range(TB):
                        cols = sc[:, h % 2, SPC[i]:SPC[i] + (i + 1) * P]
                        last = nc.vector.tensor_scalar(cols, cols, inv[:, h % 2, i:i + 1], None, ALU.mult)
                    last.then_inc(scaled, 1)

                def shared(s):
                    dve.wait_ge(relu_made, at(b, NH, s + 1))
                    dve.wait_ge(sqlo_made, at(b, NH, s))
                    nc.vector.tensor_tensor(sq[:, :], relu[:, :], relu[:, :], ALU.mult).then_inc(sq_made, 1)
                    dve.wait_ge(sq_made, at(b, NH, s + 1))
                    dve.wait_ge(sqhi_made, at(b, NH, s + 1))
                    dve.wait_ge(y_step, at(b, NH, s - 1))
                    nc.vector.tensor_tensor(sqlo[:, s % 2, :], sq[:, :], sqhi[:, s % 2, :].bitcast(F32),
                                            ALU.subtract).then_inc(sqlo_made, 1)

                def add_result(k, i):
                    dve.wait_ge(y_done, at(b, 8, 2 * k + i + 1))
                    if k < 2:
                        dve.wait_ge(res_made, at(b, 1, 1))
                    else:
                        dve.wait_ge(y_out, at(b, 8, 2 * (k - 2) + i + 1))
                    r_ = res[:, 2 * (k % 2) + i, :]
                    nc.vector.tensor_tensor(r_, psY[i][:, :], r_, ALU.add).then_inc(y_out, 1)

                for s in range(NSLOT):
                    t = s - 1
                    if s < NH:
                        for i in ROWS:
                            mask_and_min(s, i)
                    if s - 1 in Q_AT:
                        rotate(b, f"q{Q_AT[s - 1]}", (0,))
                    if s - 2 in Q_AT:
                        rotate(b, f"q{Q_AT[s - 2]}", (1,))
                    if s < NH:
                        shared(s)
                    if s < NH:
                        scale(s)
                    if s - 2 in Q_AT:
                        low_part(b, f"q{Q_AT[s - 2]}")
                    if s == 4:
                        dve.wait_ge(res_in, b * 16 + 16)
                        dve.wait_ge(bp_in, 16)
                        nc.vector.tensor_tensor(res[:, :, :], res[:, :, :], bp[:, :].unsqueeze(1).broadcast_to([P, TB, D]),
                                                ALU.add).then_inc(res_made, 1)
                    if s in (8, 16):
                        add_result(s // 8 - 1, 0)
                        add_result(s // 8 - 1, 1)
                rotate(b, "q0")
                low_part(b, "q0")
                rotate(b, "kv")
                low_part(b, "kv")
                add_result(2, 0)
                add_result(2, 1)
                place_values(b)
                add_result(3, 0)
                add_result(3, 1)

        @block.tensor
        def _(pe):
            for s_ in (s_done, t_done, pv_done, y_step, y_done):
                pe.sem_inc(s_, BASE)
            pe.sem_inc(u_done, BASE - 3)
            pe.wait_ge(vpad_clear, 1)

            def bank_free(b, name):
                k = U_AT[name]
                last, back = (U_ORDER[k - 1], 0) if k else (U_ORDER[-1], 1)
                if last.startswith("up"):
                    pe.wait_ge(relu_made, at(b, NH, int(last[2:]) + 1))
                elif last == "vt":
                    pe.wait_ge(v_made, at(b, 1, 1 - back))
                else:
                    pe.wait_ge(qk_copied, at(b, NQK, QK_AT[last] + 1))

            def project(b, name, whi, wlo):
                bank_free(b, name)
                if name == "q0" and not isinstance(b, int):
                    pe.wait_ge(xh_in, b * 32 + 32)
                    pe.wait_ge(xlo_in, b * 32 + 32)
                for c in range(KC):
                    mm = three(pe, psU[:, :], (whi[:, c, :], wlo[:, c, :]), (xh[:, c, :], xlo[:, c, :]),
                               c == 0, c == KC - 1)
                mm.then_inc(u_done, 1)

            def queries(b, n):
                cols = slice(n * P, (n + 1) * P)
                project(b, f"q{n}", wq_hi[:, :, cols], wq_lo[:, :, cols])

            def turn_values(b):
                bank_free(b, "vt")
                pe.wait_ge(rotated, at(b, NQK, QK_AT["kv"] + 1))
                for i in range(TB):
                    mm = pe.transpose(psU[:, i * P:(i + 1) * P], kv[:, i * P:(i + 1) * P], ident)
                mm.then_inc(u_done, 1)

            queries(-1, 0)
            project(-1, "kv", wkv_hi, wkv_lo)
            turn_values(-1)
            with pe.Fori(0, B) as b:
                def up(s):
                    tok = slice(s // 8 * SHALF, (s // 8 + 1) * SHALF)
                    cols = slice(s % 8 * P, (s % 8 + 1) * P)
                    bank_free(b, f"up{s}")
                    for c in range(KC):
                        mm = three(pe, psU[:, 0:SHALF], (up_hi[:, c, cols], up_lo[:, c, cols]),
                                   (xh[:, c, tok], xlo[:, c, tok]), c == 0, c == KC - 1)
                    mm.then_inc(u_done, 1)

                def down(s):
                    pe.wait_ge(sqhi_made, at(b, NH, s + 1))
                    pe.wait_ge(sqlo_made, at(b, NH, s + 1))
                    if s % 8 == 0:
                        pe.wait_ge(y_out, at(b, 8, s // 8 * 2))
                    for i in range(2):
                        tok = slice(i * P, (i + 1) * P)
                        mm = three(pe, psY[i][:, :], (sqhi[:, s % 2, tok], sqlo[:, s % 2, tok]),
                                   (down_hi[:, s % 8, :], down_lo[:, s % 8, :]), s % 8 == 0, s % 8 == 7)
                    mm.then_inc(y_step, 1)
                    if s % 8 == 7:
                        pe.wait_ge(y_step, at(b, NH, s + 1))
                        pe.sem_inc(y_done, 2)

                def scores(h, i):
                    k = h * TB + ROWS.index(i)
                    c = h // HC
                    if i == ROWS[0]:
                        pe.wait_ge(qs_in[c % 2][h % HC], stacked(b, c))
                        if h == 0:
                            pe.wait_ge(lo_made, at(b, NQK, 0))
                            pe.wait_ge(hi_made, at(b, NQK, 0))
                    pe.wait_ge(s_out, at(b, NH * TB, k - 1))
                    n = max((i + 1) * P, 2 * P)
                    pe.matmul(psS[k % 2][:, 0:n], qs[:, c % 2, h % HC, i * P:(i + 1) * P], ks[:, 0:n],
                              start=True, stop=True).then_inc(s_done, 1)

                def transposes(h, g):
                    if g == 0:
                        pe.wait_ge(scaled, at(b, NH, h + 1))
                        pe.wait_ge(ta_out, at(b, 2 * NH, 2 * h))
                        todo = [(0, 0, i) for i in range(4)]
                    elif g == 1:
                        pe.wait_ge(tb_out, at(b, NH, h))
                        todo = [(1, 1, i) for i in range(1, 4)] + [(1, 3, 3)]
                    else:
                        pe.wait_ge(ta_out, at(b, 2 * NH, 2 * h + 1))
                        todo = [(0, 2, i) for i in range(2, 4)]
                    for bank, j, i in todo:
                        first, query = PTC[j]
                        to = (first + i * P - query) % 512
                        mm = pe.transpose(psT[bank][:, to:to + P], sc[:, h % 2, SPC[i] + j * P:SPC[i] + (j + 1) * P], ident)
                    mm.then_inc(t_done, 1)

                def values(h, key_tiles):
                    if h % HC == 0:
                        pe.wait_ge(o_out, at(b, KC, h // HC))
                    if h == 0:
                        pe.wait_ge(v_made, at(b, 1, 0))
                    for j in key_tiles:
                        if j == 0:
                            pe.wait_ge(ta_out, at(b, 2 * NH, 2 * h + 1))
                        elif j == 1:
                            pe.wait_ge(tb_out, at(b, NH, h + 1))
                        elif j == 2:
                            pe.wait_ge(ta_out, at(b, 2 * NH, 2 * h + 2))
                        first, query = PTC[j]
                        place = (HC - 1 - h % HC) * HD
                        mm = pe.matmul(psO[:, query:S], vpad[:, j, place:place + P],
                                       pt[:, h % 2, first:first + S - query],
                                       start=(h % HC == 0 and j == 0), stop=(h % HC == HC - 1 and j == 2))
                    if j == 2:
                        mm.then_inc(pv_done, 1)

                def attention_result(k, i):
                    pe.wait_ge(y_out, at(b, 8, 2 * (k + 1) + i + 1))
                    tok = slice((2 * k + i) * P, (2 * k + i + 1) * P)
                    for c in range(KC):
                        mm = pe.matmul(psY[i][:, :], ot[:, c, tok], wproj[:, c, :], start=(c == 0), stop=(c == KC - 1))
                    mm.then_inc(y_done, 1)

                for s in range(NSLOT):
                    t = s - 1
                    if s < NH:
                        scores(s, ROWS[0])
                        scores(s, ROWS[1])
                    if s >= 1:
                        down(s - 1)
                    if s < NH:
                        scores(s, ROWS[2])
                    if t >= 0:
                        transposes(t, 0)
                    if s < NH:
                        scores(s, ROWS[3])
                    if t >= 0:
                        transposes(t, 1)
                    if s < NH:
                        up(s)
                    if t >= 0:
                        transposes(t, 2)
                    if t >= 0:
                        values(t, (0,))
                    if s in Q_AT:
                        queries(b, Q_AT[s])
                    if s == NH:
                        queries(b, 0)
                    if t >= 0:
                        values(t, (1, 3, 2))
                project(b, "kv", wkv_hi, wkv_lo)
                pe.wait_ge(o_out, at(b, KC, KC))
                attention_result(0, 0)
                attention_result(0, 1)
                turn_values(b)
                attention_result(1, 0)
                attention_result(1, 1)

NR = 16
NY = 4
WR = 2


def experts(nc, w1, w2, cst, experts_dram, xs, sums):
    with ExitStack() as ctx:
        def sb(name, shape, dt=F32):
            return ctx.enter_context(nc.sbuf_tensor(name, shape, dt))

        def sem(name):
            return ctx.enter_context(nc.semaphore(name))

        def pb(name):
            return ctx.enter_context(nc.psum_tensor(name, [P, S], F32))

        ident = cst[:, COL["ident"]]
        W = LC * INTER
        w1_sb = sb("e_w1", [P, E * W])
        w2_sb = sb("e_w2", [P, E * W])
        table = sb("e_table", [1, 3 * P], I32)
        row = [sb(f"e_row{u}", [P, ROW]) for u in range(NR)]
        xt = [sb(f"e_xt{u}", [P, LAT]) for u in range(2)]
        relu = [sb(f"e_relu{u}", [P, INTER]) for u in range(2)]
        ht = [sb(f"e_ht{u}", [P, INTER]) for u in range(2)]
        y = [sb(f"e_y{u}", [P, LAT]) for u in range(NY)]
        psX, psH, psT, psY = ([pb(f"e_ps{n}{u}") for u in range(2)] for n in "XHTY")
        w_in = [sem(f"e_w_in{k}") for k in range(WR)]
        w_ready = sem("e_w_ready")
        table_in = sem("e_table_in")
        passed = sem("e_passed")
        row_in = [sem(f"e_row_in{u}") for u in range(NR)]
        x_turned, h_done, h_turned, y_done = sem("e_x_turned"), sem("e_h_done"), sem("e_h_turned"), sem("e_y_done")
        xt_made, ht_made, relu_made, y_made = sem("e_xt_made"), sem("e_ht_made"), sem("e_relu_made"), sem("e_y_made")
        added = [sem(f"e_added{u}") for u in range(2)]
        block = ctx.enter_context(nc.Block())

        def num(i, u, n=0):
            return i * NR + (BASE + u + n)

        def sums_done(i, u):
            return i * (16 * NR // 2) + 16 * (u // 2 + 1)

        def first(i, u, n):
            return isinstance(i, int) and i * NR + u < n

        @block.sync
        def _(sp):
            sp.dma_start(table[:, :], experts_dram.rearrange("(a n) -> a n", a=1)).then_inc(table_in, 16)

            def arrived(k):
                sp.wait_ge(w_in[k % WR], 32 * (k // WR + 1))
                sp.sem_inc(w_ready, 1)

            for k in range(E):
                cols = slice(k * W, (k + 1) * W)
                if k >= WR:
                    arrived(k - WR)
                sp.dma_start(w1_sb[:, cols], w1[:, cols]).then_inc(w_in[k % WR], 16)
                sp.dma_start(w2_sb[:, cols], w2[:, cols]).then_inc(w_in[k % WR], 16)
            for k in range(E - WR, E):
                arrived(k)

        @block.scalar
        def _(act):
            for s_ in (xt_made, ht_made):
                act.sem_inc(s_, BASE)

            def load(i, u):
                if not first(i, u, NR):
                    act.wait_ge(added[u % 2], sums_done(i, u - NR))
                act.dma_start(row[u][:, :], xs[bass.ds(i * NR * P + u * P, P), :]).then_inc(row_in[u], 16)

            def turned_x(i, u):
                act.wait_ge(x_turned, num(i, u, 1))
                act.wait_ge(h_done, num(i, u, -1))
                nc.scalar.activation(xt[u % 2][:, :], psX[u % 2][:, 0:LAT], ACT.Copy).then_inc(xt_made, 1)

            def turned_h(i, u):
                act.wait_ge(h_turned, num(i, u, 1))
                act.wait_ge(y_done, num(i, u, -1))
                nc.scalar.activation(ht[u % 2][:, :], psT[u % 2][:, 0:INTER], ACT.Square).then_inc(ht_made, 1)

            pipeline(act, ((2, turned_x), (4, turned_h), (0, load)), SLOT_TILES // NR, NR)

        @block.vector
        def _(dve):
            for s_ in (relu_made, y_made):
                dve.sem_inc(s_, BASE)
            dve.wait_ge(table_in, 16)

            def rectify(i, u):
                dve.wait_ge(h_done, num(i, u, 1))
                dve.wait_ge(h_turned, num(i, u, -1))
                nc.vector.tensor_scalar(relu[u % 2][:, :], psH[u % 2][:, 0:INTER], 0.0, None, ALU.max).then_inc(relu_made, 1)

            def weigh(i, u):
                e = dve.value_load(table[0:1, bass.ds(i * NR + u, 1)], min_val=0, max_val=E - 1)
                dve.wait_ge(y_done, num(i, u, 1))
                if not first(i, u, NY):
                    dve.wait_ge(added[u % 2], sums_done(i, u - NY))
                nc.vector.tensor_scalar(y[u % NY][:, :], psY[u % 2][:, 0:LAT], row[u % NR][:, bass.ds(e + LAT, 1)], None,
                                        ALU.mult).then_inc(y_made, 1)

            pipeline(dve, ((1, rectify), (3, weigh)), SLOT_TILES // NR, NR)

        @block.gpsimd
        def _(pool):
            def add(i, u):
                pool.wait_ge(y_made, num(i, u, 1))
                if not first(i, u, 2):
                    pool.wait_ge(added[u % 2], sums_done(i, u - 2))
                pool.sem_inc(passed, 1)
                pool.indirect_dma_start(out=sums[u % 2],
                                        out_offset=bass.IndirectOffsetOnAxis(ap=row[u % NR][:, ROW - 1:ROW].bitcast(U32), axis=0),
                                        in_=y[u % NY][:, :], in_offset=None, compute_op=ALU.add).then_inc(added[u % 2], 16)

            pipeline(pool, ((0, add),), SLOT_TILES // NR, NR)
            for u in range(2):
                pool.wait_ge(added[u], 16 * SLOT_TILES // 2)

        @block.tensor
        def _(pe):
            for s_ in (x_turned, h_done, h_turned, y_done):
                pe.sem_inc(s_, BASE)
            pe.wait_ge(table_in, 16)

            def turn_x(i, u):
                pe.wait_ge(row_in[u], i * 16 + 16)
                for c in range(LC):
                    mm = pe.transpose(psX[u % 2][:, c * P:(c + 1) * P], row[u % NR][:, c * P:(c + 1) * P], ident)
                mm.then_inc(x_turned, 1)

            expert = {}

            def load_expert(i, u):
                expert[u % NR] = pe.value_load(table[0:1, bass.ds(i * NR + u, 1)], min_val=0, max_val=E - 1)

            def product(i, u, w, out, lhs, done):
                e = expert[u % NR]
                for c in range(LC):
                    mm = pe.matmul(out[u % 2][:, 0:INTER], lhs[u % 2][:, c * P:(c + 1) * P],
                                   w[:, bass.ds(e * W + c * INTER, INTER)], start=(c == 0), stop=(c == LC - 1))
                mm.then_inc(done, 1)

            def hidden(i, u):
                pe.wait_ge(xt_made, num(i, u, 1))
                pe.wait_ge(w_ready, expert[u % NR] + 1)
                product(i, u, w1_sb, psH, xt, h_done)

            def turn_h(i, u):
                pe.wait_ge(relu_made, num(i, u, 1))
                for c in range(IC):
                    mm = pe.transpose(psT[u % 2][:, c * P:(c + 1) * P], relu[u % 2][:, c * P:(c + 1) * P], ident)
                mm.then_inc(h_turned, 1)

            def result(i, u):
                pe.wait_ge(ht_made, num(i, u, 1))
                pe.wait_ge(y_made, num(i, u, -1))
                product(i, u, w2_sb, psY, ht, y_done)

            pipeline(pe, ((1, load_expert), (0, turn_x), (1, hidden), (3, load_expert), (2, turn_h), (3, result)),
                     SLOT_TILES // NR, NR)


def combine(nc, fc2, cst, sums, partial, out):
    R = 8
    with ExitStack() as ctx:
        def sb(name, shape, dt=F32):
            return ctx.enter_context(nc.sbuf_tensor(name, shape, dt))

        def sem(name):
            return ctx.enter_context(nc.semaphore(name))

        ident = cst[:, COL["ident"]]
        w = sb("c_w", [P, LC, D])
        a, z = ([sb(f"c_{n}{u}", [P, LAT]) for u in range(R)] for n in "az")
        y = [sb(f"c_y{u}", [P, LAT]) for u in range(2)]
        yt = [sb(f"c_yt{u}", [P, LAT]) for u in range(2)]
        part = [sb(f"c_part{u}", [P, D]) for u in range(R)]
        psT, psO = ([ctx.enter_context(nc.psum_tensor(f"c_ps{n}{u}", [P, S], F32)) for u in range(2)] for n in "TO")
        w_in = sem("c_w_in")
        sums_in, part_in, saved = ([sem(f"c_{n}{u}") for u in range(R)] for n in ("sums_in", "part_in", "saved"))
        y_made, turned, yt_made, done, added = (sem(f"c_{n}") for n in ("y_made", "turned", "yt_made", "done", "added"))
        block = ctx.enter_context(nc.Block())

        @block.sync
        def _(sp):
            for s_ in saved:
                sp.sem_inc(s_, 16 * BASE)
            with sp.Fori(0, G // R) as i:
                for u in range(R):
                    rows = bass.ds(i * R * P + u * P, P)
                    sp.wait_ge(y_made, at(i, R, u + 1 - R))
                    sp.dma_start(a[u][:, :], sums[0][rows, :]).then_inc(sums_in[u], 16)
                    sp.dma_start(z[u][:, :], sums[1][rows, :]).then_inc(sums_in[u], 16)
                    sp.wait_ge(saved[u], i * 16 + 16 * BASE)
                    sp.dma_start(part[u][:, :], partial[rows, :]).then_inc(part_in[u], 16)

        @block.scalar
        def _(act):
            act.sem_inc(yt_made, BASE)
            act.dma_start(w[:, :, :].rearrange("p c n -> p (c n)"), fc2).then_inc(w_in, 16)

            def copy_turned(i, u):
                act.wait_ge(turned, at(i, R, u + 1))
                act.wait_ge(done, at(i, R, u - 1))
                nc.scalar.activation(yt[u % 2][:, :], psT[u % 2][:, 0:LAT], ACT.Copy).then_inc(yt_made, 1)

            def store(i, u):
                act.wait_ge(added, at(i, R, u + 1))
                act.dma_start(out[bass.ds(i * R * P + u * P, P), :], part[u % R][:, :]).then_inc(saved[u % R], 16)

            pipeline(act, ((0, copy_turned), (2, store)), G // R, R)
            for u in range(R):
                act.wait_ge(saved[u], 16 * (BASE + G // R))

        @block.vector
        def _(dve):
            dve.sem_inc(y_made, BASE)
            dve.sem_inc(added, BASE)

            def add_sums(i, u):
                dve.wait_ge(sums_in[u], i * 32 + 32)
                dve.wait_ge(turned, at(i, R, u - 1))
                nc.vector.tensor_tensor(y[u % 2][:, :], a[u][:, :], z[u][:, :], ALU.add).then_inc(y_made, 1)

            def add_partial(i, u):
                dve.wait_ge(done, at(i, R, u + 1))
                dve.wait_ge(part_in[u % R], i * 16 + 16 * (u // R + 1))
                nc.vector.tensor_tensor(part[u % R][:, :], psO[u % 2][:, :], part[u % R][:, :], ALU.add).then_inc(added, 1)

            pipeline(dve, ((0, add_sums), (2, add_partial)), G // R, R)

        @block.tensor
        def _(pe):
            pe.sem_inc(turned, BASE)
            pe.sem_inc(done, BASE)

            def turn(i, u):
                pe.wait_ge(y_made, at(i, R, u + 1))
                pe.wait_ge(yt_made, at(i, R, u - 1))
                for c in range(LC):
                    mm = pe.transpose(psT[u % 2][:, c * P:(c + 1) * P], y[u % 2][:, c * P:(c + 1) * P], ident)
                mm.then_inc(turned, 1)

            def multiply(i, u):
                if isinstance(i, int) and u == 0:
                    pe.wait_ge(w_in, 16)
                pe.wait_ge(yt_made, at(i, R, u + 1))
                pe.wait_ge(added, at(i, R, u - 1))
                for c in range(LC):
                    mm = pe.matmul(psO[u % 2][:, :], yt[u % 2][:, c * P:(c + 1) * P], w[:, c, :],
                                   start=(c == 0), stop=(c == LC - 1))
                mm.then_inc(done, 1)

            pipeline(pe, ((0, turn), (1, multiply)), G // R, R)

def constant_table():
    c = np.zeros((P, NCONST), np.float32)
    p = np.arange(P)
    c[:, COL["ident"]] = np.eye(P)
    c[:, COL["tri"]] = np.triu(np.ones((P, P)), 1)
    col = np.arange(S)[None] - (S - P)
    c[:, COL["mask"]] = np.where(col > p[:, None], np.float32(1e38), 0)
    f = np.float32
    inv_freq = f(1) / f(10000) ** (np.arange(0, HD, 2, dtype=f) / f(HD))
    t = np.arange(S, dtype=f)
    freqs = (t[:, None] * inv_freq[None]).astype(f)
    base = ((np.arange(0, HD, 2, dtype=f) + f(0.4 * HD)) / f(1.4 * HD)).astype(f)
    xs = (base[None] ** ((t - S // 2) / f(128))[:, None]).astype(f)
    d = p % HD
    angles = freqs.astype(np.float64)
    cos, sin, xs = (np.asarray(a[:, d % (HD // 2)].T, np.float64) for a in (np.cos(angles), np.sin(angles), xs))
    sign = np.where(d < HD // 2, -1.0, 1.0)[:, None]
    w = float(f(HD ** -0.5))
    c[:, COL["cosq"]], c[:, COL["sinq"]] = -w * cos * xs, -w * sign * sin * xs
    c[:, COL["cosk"]], c[:, COL["sink"]] = w * cos / xs, w * sign * sin / xs
    c[:, COL["token"]] = np.arange(G)[None] * P + p[:, None]
    c[:, COL["earlier"]] = np.tril(np.ones((NG, NG)), -1).reshape(1, -1)
    c[:, COL["tile"]] = np.arange(3)[None] + 3 * p[:, None]
    c[:, COL["lane"]] = p[:, None]
    c[:, COL["spare"]] = T + p[:, None]
    return c


def build(nc, x, w_fc1_gate, gate_bias, wq, wkv, wproj, bproj, wup, wdown, w1, w2, wfc2, consts, out):
    xnt_hi = nc.dram_tensor("xnt_hi", (B + 1, P, KC, S), F32, kind="Internal").ap()
    xnt_lo = nc.dram_tensor("xnt_lo", (B + 1, P, KC, S), F32, kind="Internal").ap()
    xlat = nc.dram_tensor("xlat", (T, LAT), F32, kind="Internal").ap()
    slot_rows = nc.dram_tensor("slot_rows", (SLOTS, ROW), F32, kind="Internal").ap()
    experts_dram = nc.dram_tensor("tile_experts", (3 * P,), I32, kind="Internal").ap()
    sums = [nc.dram_tensor(f"sums{u}", (T + SPARE, LAT), F32, kind="Internal").ap() for u in range(2)]
    partial = nc.dram_tensor("partial", (T, D), F32, kind="Internal").ap()
    with ExitStack() as ctx:
        cst = ctx.enter_context(nc.sbuf_tensor("cst", [P, NCONST], F32))
        with ExitStack() as inner:
            def sb(name, shape, dt=F32):
                return inner.enter_context(nc.sbuf_tensor(name, shape, dt))

            weights_sb = sb("weights", [P, G, E])
            slots_sb = sb("slots", [P, G, TOPK], U32)
            pads_sb = sb("pads", [P, E], U32)
            empty = sb("empty", [P, ROW])
            logits = sb("logits", [P, G, E])
            front(nc, x, consts, w_fc1_gate, xnt_hi, xnt_lo, xlat, cst, logits)
            halves = {n: tuple(sb(f"{n}_{h}", [P, w.shape[1]], F32R) for h in ("hi", "lo"))
                      for n, w in (("wq", wq), ("wkv", wkv), ("wup", wup), ("wdown", wdown))}
            halves = {n: tuple(a[:, :] for a in pair) for n, pair in halves.items()}
            proj = sb("proj", [P, KC, D])
            xh, xlo = (sb(n, [P, KC, S], F32R) for n in ("xh", "xlo"))
            routing(nc, xnt_hi, xnt_lo, xh, xlo, gate_bias, cst, logits, weights_sb, slots_sb,
                    pads_sb, empty, slot_rows, experts_dram,
                    [(w, *halves[n]) for n, w in (("wkv", wkv), ("wq", wq), ("wup", wup), ("wdown", wdown))],
                    proj[:, :, :].rearrange("p c n -> p (c n)"), wproj)
            middle(nc, x, bproj, xnt_hi, xnt_lo, xh, xlo, xlat, halves["wq"], halves["wkv"], proj, halves["wup"], halves["wdown"],
                   cst, weights_sb, slots_sb, pads_sb, empty, slot_rows, sums, partial)
        experts(nc, w1, w2, cst, experts_dram, slot_rows, sums)
        combine(nc, wfc2, cst, sums, partial, out)


def columns(w, chunks):
    return np.ascontiguousarray(w.reshape(chunks, P, -1).transpose(1, 0, 2).reshape(P, -1))


def per_expert(w):
    w = w.transpose(0, 2, 1).reshape(E, LC, P, -1)
    return np.ascontiguousarray(w.transpose(2, 0, 1, 3).reshape(P, -1))


def kernel(L0_attn_hidden_states, L0_attn_w_q, L0_attn_w_kv, L0_attn_w_proj, L0_attn_b_proj, L0_ffn_gate_w,
           L0_ffn_gate_bias, L0_ffn_fc1_w, L0_ffn_fc2_w, L0_ffn_w1, L0_ffn_w2, L0_ffn_shared_up_w,
           L0_ffn_shared_down_w):
    import concourse.bacc as bacc
    from concourse.bass_utils import run_bass_kernel_spmd

    def a(v):
        return np.asarray(v)

    kv = a(L0_attn_w_kv)
    arrays = {
        "x": np.ascontiguousarray(a(L0_attn_hidden_states).reshape(T, D)),
        "w_fc1_gate": columns(np.concatenate([a(L0_ffn_fc1_w).T, a(L0_ffn_gate_w).T], 1), KC).reshape(P, KC, FG),
        "gate_bias": a(L0_ffn_gate_bias),
        "wq": columns(a(L0_attn_w_q).T, KC),
        "wkv": columns(np.concatenate([kv[:HD], kv[:HD], kv[:HD], kv[HD:]], 0).T, KC),
        "wproj": columns(a(L0_attn_w_proj).T, KC),
        "bproj": a(L0_attn_b_proj),
        "wup": columns(a(L0_ffn_shared_up_w).T, KC),
        "wdown": columns(a(L0_ffn_shared_down_w).T, SC),
        "w1": per_expert(a(L0_ffn_w1)),
        "w2": per_expert(a(L0_ffn_w2)),
        "wfc2": columns(a(L0_ffn_fc2_w).T, LC),
        "consts": constant_table(),
    }
    nc = bacc.Bacc("TRN2", target_bir_lowering=False, num_devices=1)
    aps = [nc.dram_tensor(f"in_{n}", v.shape, F32, kind="ExternalInput").ap() for n, v in arrays.items()]
    out = nc.dram_tensor("out", (T, D), F32, kind="ExternalOutput").ap()
    build(nc, *aps, out)
    r = run_bass_kernel_spmd(nc, [{f"in_{n}": v for n, v in arrays.items()}], core_ids=[0])
    return r.results[0]["out"].reshape(B, S, D)
```
